# Optimizing a Trainium2 kernel written in Bass

```python
import numpy as np
import jax
import jax.numpy as jnp

def _softmax(x, axis=-1):
    return jax.nn.softmax(x, axis=axis)
def _gelu(x):
    return jax.nn.gelu(x, approximate=True)
def _silu(x):
    return jax.nn.silu(x)
def _sigmoid(x):
    return jax.nn.sigmoid(x)
def _layernorm(x, axis=-1, eps=1e-5):
    m = jnp.mean(x, axis=axis, keepdims=True)
    v = jnp.var(x, axis=axis, keepdims=True)
    return (x - m) / jnp.sqrt(v + eps)
def _scatter_add(tgt, idx, src, axis=0):
    return tgt.at[idx].add(src)
def _segment_sum(src, seg, n):
    return jax.ops.segment_sum(src, seg, n)

kernel_name = 'mk_adj_resnorm_d4_adj_128_5b1380'

def setup_inputs(seed: int = 0):
    np.random.seed(seed)
    _w = jnp.asarray
    def _rec_inputs():
        import jax
        import jax.numpy as jnp
        _gk = jax.random.key(seed)
        x = -0.0005207 + 1.001 * jax.random.normal(jax.random.fold_in(_gk, 1), (2708, 128), jnp.float32)
        _w = (1.0 + jnp.arange(2708, dtype=jnp.float32)) ** -0.5
        _w = _w / _w.mean()
        _pij = jnp.clip(0.00295421 * _w[:, None] * _w[None, :], 0.0, 1.0)
        _a = jax.random.uniform(jax.random.fold_in(_gk, 2), (2708, 2708)) < _pij
        _a = jnp.logical_or(_a, jnp.eye(2708, dtype=bool))
        _af = _a.astype(jnp.float32)
        _af = _af * jax.random.uniform(jax.random.fold_in(_gk, 3), (2708, 2708), jnp.float32, 0.05, 1)
        adj = _af
        return x, adj
    x, adj = _rec_inputs()
    def _L0_gnn_setup():
        import jax, jax.numpy as jnp
        import numpy as np
        N = 16384
        IN_DIM = 128
        OUT_DIM = 128

        def _message(X, A, W):
            deg = jnp.sum(A, axis=1, keepdims=True)
            A_norm = A / jnp.where(deg > 0, deg, 1.0)
            return A_norm @ X @ W
        key = jax.random.key(seed)
        k1, k2, k3, k4 = jax.random.split(key, 4)
        X = jax.random.normal(k1, (N, IN_DIM), dtype=jnp.float32)
        A = jax.random.uniform(k2, (N, N), dtype=jnp.float32)
        W_in = jax.random.normal(k3, (IN_DIM, OUT_DIM), dtype=jnp.float32) / np.sqrt(IN_DIM)
        W_out = jax.random.normal(k4, (IN_DIM, OUT_DIM), dtype=jnp.float32) / np.sqrt(IN_DIM)
        return {'X': X, 'A': A, 'W_in': W_in, 'W_out': W_out}
    _L0_gnn_all = _L0_gnn_setup()
    _L0_gnn_in = {k: v for k, v in _L0_gnn_all.items() if k in ('W_in', 'W_out', )}
    del _L0_gnn_all

    def _L1_gnn_setup():
        import jax, jax.numpy as jnp
        import numpy as np
        N, DIM = (16384, 128)

        def _gru_cell(x, h, W_ih, W_hh, b_ih, b_hh):
            gi = x @ W_ih.T + b_ih
            gh = h @ W_hh.T + b_hh
            i_r, i_z, i_n = jnp.split(gi, 3, axis=-1)
            h_r, h_z, h_n = jnp.split(gh, 3, axis=-1)
            r = jax.nn.sigmoid(i_r + h_r)
            z = jax.nn.sigmoid(i_z + h_z)
            n = jnp.tanh(i_n + r * h_n)
            return (1.0 - z) * n + z * h
        key = jax.random.key(seed)
        ks = jax.random.split(key, 8)
        states = jax.random.normal(ks[0], (N, DIM), dtype=jnp.float32)
        adj = jax.random.uniform(ks[1], (N, N), dtype=jnp.float32)
        s = 1.0 / np.sqrt(DIM)
        W_msg = jax.random.uniform(ks[2], (DIM, DIM), minval=-s, maxval=s, dtype=jnp.float32)
        b_msg = jax.random.uniform(ks[3], (DIM,), minval=-s, maxval=s, dtype=jnp.float32)
        W_ih = jax.random.uniform(ks[4], (3 * DIM, DIM), minval=-s, maxval=s, dtype=jnp.float32)
        W_hh = jax.random.uniform(ks[5], (3 * DIM, DIM), minval=-s, maxval=s, dtype=jnp.float32)
        b_ih = jax.random.uniform(ks[6], (3 * DIM,), minval=-s, maxval=s, dtype=jnp.float32)
        b_hh = jax.random.uniform(ks[7], (3 * DIM,), minval=-s, maxval=s, dtype=jnp.float32)
        return {'states': states, 'adj': adj, 'W_msg': W_msg, 'b_msg': b_msg, 'W_ih': W_ih, 'W_hh': W_hh, 'b_ih': b_ih, 'b_hh': b_hh}
    _L1_gnn_all = _L1_gnn_setup()
    _L1_gnn_in = {k: v for k, v in _L1_gnn_all.items() if k in ('W_msg', 'b_msg', 'W_ih', 'W_hh', 'b_ih', 'b_hh', )}
    del _L1_gnn_all

    def _L2_gnn_setup():
        import jax, jax.numpy as jnp
        import numpy as np
        LN_EPS = 1e-05
        key = jax.random.key(seed)
        ks = jax.random.split(key, 6)
        N, D = (1024, 128)
        return {'node_feats': jax.random.normal(ks[0], (N, D), dtype=jnp.float32), 'adj': jax.random.uniform(ks[1], (N, N), dtype=jnp.float32), 'msg_w': jax.random.normal(ks[2], (D, 2 * D), dtype=jnp.float32) * 0.05, 'msg_b': jax.random.normal(ks[3], (D,), dtype=jnp.float32) * 0.05, 'upd_w': jax.random.normal(ks[4], (D, 2 * D), dtype=jnp.float32) * 0.05, 'upd_b': jax.random.normal(ks[5], (D,), dtype=jnp.float32) * 0.05, 'ln_w': jnp.ones((D,), dtype=jnp.float32), 'ln_b': jnp.zeros((D,), dtype=jnp.float32)}
    _L2_gnn_all = _L2_gnn_setup()
    _L2_gnn_in = {k: v for k, v in _L2_gnn_all.items() if k in ('msg_w', 'msg_b', 'upd_w', 'upd_b', 'ln_w', 'ln_b', )}
    del _L2_gnn_all

    def _L3_gnn_setup():
        import jax, jax.numpy as jnp
        import numpy as np
        N = 8192
        IN_DIM = 128
        OUT_DIM = 128
        DENSITY = 0.01
        key = jax.random.key(seed)
        kx, ka, kw, ks, kd = jax.random.split(key, 5)
        x = jax.random.normal(kx, (N, IN_DIM), dtype=jnp.float32) * 0.1
        adj_matrix = (jax.random.uniform(ka, (N, N)) < DENSITY).astype(jnp.float32)
        adj_matrix = jnp.maximum(adj_matrix, jnp.eye(N, dtype=jnp.float32))
        weight = jax.random.normal(kw, (OUT_DIM, IN_DIM), dtype=jnp.float32) * 0.05
        att_src = jax.random.normal(ks, (1, OUT_DIM), dtype=jnp.float32) * 0.1
        att_dst = jax.random.normal(kd, (1, OUT_DIM), dtype=jnp.float32) * 0.1
        return {'x': x, 'adj_matrix': adj_matrix, 'weight': weight, 'att_src': att_src, 'att_dst': att_dst}
    _L3_gnn_all = _L3_gnn_setup()
    _L3_gnn_in = {k: v for k, v in _L3_gnn_all.items() if k in ('weight', 'att_src', 'att_dst', )}
    del _L3_gnn_all

    return {
        "x": x,
        "adj": adj,
        "L0_gnn_W_in": _L0_gnn_in["W_in"],
        "L0_gnn_W_out": _L0_gnn_in["W_out"],
        "L1_gnn_W_msg": _L1_gnn_in["W_msg"],
        "L1_gnn_b_msg": _L1_gnn_in["b_msg"],
        "L1_gnn_W_ih": _L1_gnn_in["W_ih"],
        "L1_gnn_W_hh": _L1_gnn_in["W_hh"],
        "L1_gnn_b_ih": _L1_gnn_in["b_ih"],
        "L1_gnn_b_hh": _L1_gnn_in["b_hh"],
        "L2_gnn_msg_w": _L2_gnn_in["msg_w"],
        "L2_gnn_msg_b": _L2_gnn_in["msg_b"],
        "L2_gnn_upd_w": _L2_gnn_in["upd_w"],
        "L2_gnn_upd_b": _L2_gnn_in["upd_b"],
        "L2_gnn_ln_w": _L2_gnn_in["ln_w"],
        "L2_gnn_ln_b": _L2_gnn_in["ln_b"],
        "L3_gnn_weight": _L3_gnn_in["weight"],
        "L3_gnn_att_src": _L3_gnn_in["att_src"],
        "L3_gnn_att_dst": _L3_gnn_in["att_dst"],
    }

def reference(x, adj, L0_gnn_W_in, L0_gnn_W_out, L1_gnn_W_msg, L1_gnn_b_msg, L1_gnn_W_ih, L1_gnn_W_hh, L1_gnn_b_ih, L1_gnn_b_hh, L2_gnn_msg_w, L2_gnn_msg_b, L2_gnn_upd_w, L2_gnn_upd_b, L2_gnn_ln_w, L2_gnn_ln_b, L3_gnn_weight, L3_gnn_att_src, L3_gnn_att_dst):
    import jax
    import jax.numpy as jnp
    def _L0_gnn_ref(X, A, W_in, W_out):
        import jax, jax.numpy as jnp
        import numpy as np
        N = 16384
        IN_DIM = 128
        OUT_DIM = 128

        def _message(X, A, W):
            deg = jnp.sum(A, axis=1, keepdims=True)
            A_norm = A / jnp.where(deg > 0, deg, 1.0)
            return A_norm @ X @ W
        X_in = _message(X, A, W_in)
        X_out = _message(X, A.T, W_out)
        return X_in + X_out

    def _L1_gnn_ref(states, adj, W_msg, b_msg, W_ih, W_hh, b_ih, b_hh):
        import jax, jax.numpy as jnp
        import numpy as np
        N, DIM = (16384, 128)

        def _gru_cell(x, h, W_ih, W_hh, b_ih, b_hh):
            gi = x @ W_ih.T + b_ih
            gh = h @ W_hh.T + b_hh
            i_r, i_z, i_n = jnp.split(gi, 3, axis=-1)
            h_r, h_z, h_n = jnp.split(gh, 3, axis=-1)
            r = jax.nn.sigmoid(i_r + h_r)
            z = jax.nn.sigmoid(i_z + h_z)
            n = jnp.tanh(i_n + r * h_n)
            return (1.0 - z) * n + z * h
        agg = adj @ states
        msg = jax.nn.relu(agg @ W_msg.T + b_msg)
        return _gru_cell(msg, states, W_ih, W_hh, b_ih, b_hh)

    def _L2_gnn_ref(node_feats, adj, msg_w, msg_b, upd_w, upd_b, ln_w, ln_b):
        import jax, jax.numpy as jnp
        import numpy as np
        LN_EPS = 1e-05
        D = node_feats.shape[-1]
        s = node_feats @ msg_w[:, :D].T
        d = node_feats @ msg_w[:, D:].T
        messages = jax.nn.gelu(s[:, None, :] + d[None, :, :] + msg_b, approximate=False)
        aggregated = jnp.einsum('ijd,ij->id', messages, adj)
        combined = jnp.concatenate([node_feats, aggregated], axis=-1)
        new_feats = combined @ upd_w.T + upd_b
        h = jax.nn.gelu(new_feats, approximate=False) + node_feats
        mu = jnp.mean(h, axis=-1, keepdims=True)
        var = jnp.var(h, axis=-1, keepdims=True)
        return (h - mu) / jnp.sqrt(var + LN_EPS) * ln_w + ln_b

    def _L3_gnn_ref(x, adj_matrix, weight, att_src, att_dst):
        import jax, jax.numpy as jnp
        import numpy as np
        N = 8192
        IN_DIM = 128
        OUT_DIM = 128
        DENSITY = 0.01
        H = x @ weight.T
        alpha_src = jnp.sum(H * att_src[0], axis=-1)
        alpha_dst = jnp.sum(H * att_dst[0], axis=-1)
        C = alpha_src[None, :] + alpha_dst[:, None]
        Tau = adj_matrix.T * jnp.exp(jnp.maximum(0.2 * C, C))
        att_weights = Tau / jnp.sum(Tau, axis=1, keepdims=True)
        Z = adj_matrix.T * att_weights @ H
        return Z

    x = _layernorm(x + _L0_gnn_ref(x, adj, L0_gnn_W_in, L0_gnn_W_out), axis=-1)
    x = _layernorm(x + _L1_gnn_ref(x, adj, L1_gnn_W_msg, L1_gnn_b_msg, L1_gnn_W_ih, L1_gnn_W_hh, L1_gnn_b_ih, L1_gnn_b_hh), axis=-1)
    x = _layernorm(x + _L2_gnn_ref(x, adj, L2_gnn_msg_w, L2_gnn_msg_b, L2_gnn_upd_w, L2_gnn_upd_b, L2_gnn_ln_w, L2_gnn_ln_b), axis=-1)
    x = _layernorm(x + _L3_gnn_ref(x, adj, L3_gnn_weight, L3_gnn_att_src, L3_gnn_att_dst), axis=-1)
    return x


_drawn_inputs = setup_inputs


def setup_inputs(seed=0):
    import zlib

    import numpy as np

    out = dict(_drawn_inputs(seed))
    spreads = {'L2_gnn_ln_w': (1.0, 0.2), 'L2_gnn_ln_b': (0.0, 0.1)}
    factors = {'L1_gnn_b_msg': 8.0, 'L1_gnn_b_ih': 3.262, 'L1_gnn_b_hh': 5.166, 'L2_gnn_upd_b': 2.99}
    for name, (base, spread) in spreads.items():
        noise = np.random.default_rng([zlib.crc32(name.encode()), seed]).standard_normal(out[name].shape)
        drawn = base * np.exp(spread * noise) if base else spread * noise
        out[name] = jnp.asarray(drawn.astype(out[name].dtype))
    for name, factor in factors.items():
        out[name] = (out[name] * factor).astype(out[name].dtype)
    return out
```

```python
import math
from contextlib import ExitStack

import numpy as np

import concourse.bass as bass
from concourse import mybir
from concourse.alu_op_type import AluOpType as ALU

P = 128
N = 2708
T = -(-N // P)
NP = T * P
D = 128
HT = T // 2
HOFF = (0, HT * P)
HWID = (HT * P, N - HT * P)
BANK = 512
RING = 6
EPS = 1e-5

HEAD = ((0, 16, 8), (16, 16, 8), (32, 32, 4), (64, 64, 2))
HEAD_SLOTS = (38, 12, 18, 22)
HEAD_W = tuple(-(-N // parts) for _, _, parts in HEAD)
HEAD_AT = tuple(sum(HEAD_W[:u]) for u in range(len(HEAD) + 1))
TILE_SLOTS = (32, 22, 20, 23, 17, 17, 16, 16, 15, 13, 13, 13, 14, 11, 14, 10, 12, 11, 11, 10, 11)
SLOTS = HEAD_SLOTS + TILE_SLOTS
UNITS = len(SLOTS)
NHEAD = len(HEAD)
ROUNDS = tuple(-(-k // 8) for k in SLOTS)
SLOT_AT = tuple(8 * sum(ROUNDS[:u]) for u in range(UNITS + 1))
SLOT_N = SLOT_AT[UNITS]
SEG_KINDS = ((11, 5), (9, 3), (6, 2))


def seg_kind(t):
    return 0 if t <= 2 else 1 if t <= 6 else 2


def seg_bounds(kind):
    n0, n1 = SEG_KINDS[kind]
    h = HOFF[1]
    first = [0]
    for k in range(1, n0):
        first.append(max(first[-1] + 8, round(h * (k / n0) ** 2)))
    a = math.sqrt(h / N)
    second = [round(N * (a + (1 - a) * k / n1) ** 2) for k in range(n1)]
    return [*first, h], [*second, N]


def cand_width(t):
    return 8 * sum(SEG_KINDS[seg_kind(t)])


CAND_AT = {t: sum(cand_width(s) for s in range(1, t)) for t in range(1, T + 1)}
BASE_AT = (0, 8 * sum(SEG_KINDS[0]), 8 * (sum(SEG_KINDS[0]) + sum(SEG_KINDS[1])))
BASE_N = BASE_AT[2] + 8 * sum(SEG_KINDS[2])
WIDEST = 8 * sum(SEG_KINDS[0])

CONST = {
    "ident": P,
    "spread": NHEAD * P,
    "spread_t": NHEAD * P,
    "seg_base": BASE_N,
    "iota": WIDEST,
    "row": T,
    "head_row": NHEAD,
    "head_part": NHEAD,
    "ones": P,
}
CONST_AT = {}
for _name in CONST:
    CONST_AT[_name] = sum(CONST[k] for k in list(CONST)[: list(CONST).index(_name)])
CONST_N = sum(CONST.values())

WEIGHT = {
    "w_in": D, "w_out": D,
    "w_msg_t": D, "w_ih_t": 3 * D, "w_hh_t": 3 * D,
    "w_sd": 2 * D, "upd_x": D, "upd_a": D,
    "w3_t": D, "w3": D,
    "b_msg": 1, "b_ih": 3, "b_hh": 3, "msg_b": 1, "att_src": 1, "att_dst": 1,
    "diag": T,
}
WEIGHT_AT = {}
for _name in WEIGHT:
    WEIGHT_AT[_name] = sum(WEIGHT[k] for k in list(WEIGHT)[: list(WEIGHT).index(_name)])
WEIGHT_N = sum(WEIGHT.values())
ROWS4 = 4


def constants():
    c = {k: np.zeros((P, w), np.float32) for k, w in CONST.items()}
    c["ident"][:] = np.eye(P)
    c["ones"][:] = 1
    c["iota"][:] = np.arange(WIDEST)
    c["row"][:] = np.arange(P)[:, None] + P * np.arange(T)
    for u, (row, _, parts) in enumerate(HEAD):
        p = np.arange(P)
        r = row + p // parts
        c["spread"][p, u * P + r] = 1
        c["spread_t"][r, u * P + p] = 1
        c["head_row"][:, u] = r
        c["head_part"][:, u] = p % parts
    for kind in range(3):
        first, second = seg_bounds(kind)
        starts = first[:-1] + second[:-1]
        c["seg_base"][:, BASE_AT[kind]:BASE_AT[kind] + 8 * len(starts)] = np.repeat(starts, 8)
    return np.concatenate([c[k] for k in CONST], axis=1)


BATCH = 4


def batches():
    out = []
    for t in range(T):
        out.append((t, None, 0, 1))
        for u in (range(NHEAD) if t == 0 else [NHEAD + t - 1]):
            for k in range(0, SLOTS[u], BATCH):
                out.append((t, u, k, min(BATCH, SLOTS[u] - k)))
    return out


def chunks(h):
    return [(c, min(BANK, HWID[h] - c)) for c in range(0, HWID[h], BANK)]


CH = [(h, HOFF[h] + c, w) for h in range(2) for c, w in chunks(h)]
NB = len(chunks(0))
assert len(chunks(1)) == NB


def build(nc, x, adj_rows, adj_cols, head, weights, rows4, consts, out):
    f32, u32, i32 = mybir.dt.float32, mybir.dt.uint32, mybir.dt.int32
    ACT = mybir.ActivationFunctionType
    AX = mybir.AxisListType.X
    d_table = nc.dram_tensor("d_table", (NP, D), f32).ap()

    ctx = ExitStack()
    with ctx:
        def sb(name, shape, dt=f32):
            return ctx.enter_context(nc.sbuf_tensor(name, shape, dt))

        def sem(name):
            return ctx.enter_context(nc.semaphore(name))

        xa = sb("xa", [P, T, D])
        xb = sb("xb", [P, T, D])
        xt = sb("xt", [P, NP])
        pt1 = sb("pt1", [P, NP])
        pt2 = sb("pt2", [P, NP])
        hn = sb("hn", [P, T, D])
        sd = sb("sd", [P, T, 2 * D])
        rows = sb("rows", [P, RING, HWID[0]])
        cols = sb("cols", [P, RING, HWID[0]])
        cand = sb("cand", [P, CAND_AT[T]])
        cand_i = sb("cand_i", [P, CAND_AT[T]], u32)
        cand_c = sb("cand_c", [P, 2, WIDEST])
        cand_v = sb("cand_v", [P, 2, WIDEST])
        look = sb("look", [P, 2, WIDEST])
        pos = sb("pos", [P, SLOT_N], u32)
        pos_f = sb("pos_f", [P, SLOT_N])
        vals = sb("vals", [P, SLOT_N])
        col_f = sb("col_f", [P, SLOT_N])
        col = sb("col", [P, SLOT_N], u32)
        cst = sb("cst", [P, CONST_N])
        wts = sb("wts", [P, WEIGHT_N])
        rowv = sb("rowv", [P, ROWS4, D])
        sums = sb("sums", [P, 3, 2, T])
        head_sg = sb("head_sg", [P, NHEAD])
        recip = sb("recip", [P, 2, T])
        degs = sb("degs", [P, 3, 2, T])
        found = sb("found", [P, UNITS])
        left = sb("left", [P, 3, UNITS])
        bad = sb("bad", [P, 5, UNITS])
        badc = sb("badc", [P, 1])
        flag = sb("flag", [1, 1], i32)
        stats = sb("stats", [P, T, 6])
        mv = sb("mv", [P, T, 2])
        rstd = sb("rstd", [P, 2, T])
        b_rz = sb("b_rz", [P, 2])
        eps = sb("eps", [P, 1])
        att = sb("att", [P, 2 + P])
        src = sb("src", [P, T])
        src2 = sb("src2", [P, T])

        head_a = hn[:, :, :].rearrange("p t d -> p (t d)")[:, 0:HEAD_AT[NHEAD]]
        gates = sd[:, :, :].rearrange("p t d -> p (t d)")
        gate = lambda n, b: gates[:, (2 * n + b) * BANK:(2 * n + b + 1) * BANK]
        ring2 = cols[:, :, :].rearrange("p r w -> p (r w)")
        QW = BATCH * D
        NG, NZ = 6, 3
        got = lambda b: ring2[:, (b % NG) * QW:(b % NG + 1) * QW]
        zed = lambda b: ring2[:, (NG + b % NZ) * QW:(NG + b % NZ + 1) * QW]
        gel = lambda b: ring2[:, (NG + NZ + b % NZ) * QW:(NG + NZ + b % NZ + 1) * QW]
        dia = lambda b: ring2[:, (NG + 2 * NZ + b % NZ) * QW:(NG + 2 * NZ + b % NZ + 1) * QW]
        assert (NG + 3 * NZ) * QW <= RING * HWID[0]

        ps = [ctx.enter_context(nc.psum_tensor(f"ps{b}", [P, BANK], f32)) for b in range(8)]

        def C(name, a=0, w=None):
            at = CONST_AT[name] + a
            return cst[:, at:at + (CONST[name] if w is None else w)]

        def W(name, a=0, w=None):
            at = WEIGHT_AT[name] + a
            return wts[:, at:at + (WEIGHT[name] if w is None else w)]

        ident = C("ident")

        s_const = sem("s_const")
        s_rows = [sem(f"s_rows{r}") for r in range(RING)]
        s_cols = [sem(f"s_cols{r}") for r in range(RING)]
        s_pe0 = sem("s_pe0")
        s_act0 = sem("s_act0")
        s_max = sem("s_max")
        s_cand = sem("s_cand")
        s_headx = sem("s_headx")
        s_hsg = sem("s_hsg")
        s_ev0 = sem("s_ev0")
        s_zero = sem("s_zero")
        s_deg = sem("s_deg")
        s_p0 = sem("s_p0")
        s_h0 = sem("s_h0")
        s_mv = [sem(f"s_mv{l}") for l in range(5)]
        s_std = [sem(f"s_std{l}") for l in range(5)]
        s_rstd = [sem(f"s_rstd{l}") for l in range(5)]
        s_x = [sem(f"s_x{l}") for l in range(5)]
        s_tp = [sem(f"s_tp{l}") for l in range(5)]
        s_xt = [sem(f"s_xt{l}") for l in range(5)]
        s_pe1 = sem("s_pe1")
        s_ev1 = sem("s_ev1")
        s_msgp = sem("s_msgp")
        s_msg = sem("s_msg")
        s_gp = sem("s_gp")
        s_rz = sem("s_rz")
        s_nin = sem("s_nin")
        s_n = sem("s_n")
        s_hc = sem("s_hc")
        s_hp = sem("s_hp")
        s_hs = sem("s_hs")
        s_ex = sem("s_ex")
        s_badp = sem("s_badp")
        s_flag = sem("s_flag")
        s_sdp = sem("s_sdp")
        s_sd = sem("s_sd")
        s_tab = sem("s_tab")
        s_got = [sem(f"s_got{r}") for r in range(NG)]
        s_zed = sem("s_zed")
        s_dia = sem("s_dia")
        s_gel = sem("s_gel")
        s_su = sem("s_su")
        s_suc = sem("s_suc")
        s_bat = sem("s_bat")
        s_agg = sem("s_agg")
        s_dtp = sem("s_dtp")
        s_dt = sem("s_dt")
        s_row = [sem(f"s_row{r}") for r in range(2)]
        s_gd = sem("s_gd")
        s_dense = sem("s_dense")
        s_up = sem("s_up")
        s_ug = sem("s_ug")
        s_h2 = sem("s_h2")
        s_att = sem("s_att")
        s_attc = sem("s_attc")
        s_rel = sem("s_rel")
        s_g = sem("s_g")
        s_t1 = sem("s_t1")
        s_t2 = sem("s_t2")
        s_tsum = sem("s_tsum")
        s_pe3 = sem("s_pe3")
        s_z = sem("s_z")
        s_zp = sem("s_zp")
        s_zs = sem("s_zs")
        s_out = sem("s_out")

        block = ctx.enter_context(nc.Block())
        STEPS = 2 * T
        BAT = batches()
        LASTB = {t: max(i for i, b in enumerate(BAT) if b[0] == t) for t in range(T)}
        gather_no = {}
        for i, (t, u, k, n) in enumerate(BAT):
            if u is not None:
                gather_no[i] = len(gather_no)
        gathers_of = [sum(BAT[i][3] for i in gather_no if gather_no[i] % NG == r and gather_no[i] <= j)
                      for j in range(len(gather_no)) for r in [j % NG]]

        EX_BAD = 5 + sum(SLOTS[u] % 8 > 0 for u in range(UNITS)) + sum(
            4 + 3 * ROUNDS[u] + 3 + SLOTS[u] for u in range(NHEAD, UNITS))

        def half(n):
            return n // T % 2, n % T

        @block.sync
        def _(sp):
            sp.dma_start(wts[:], weights).then_inc(s_const, 16)
            sp.dma_start(head_a, head).then_inc(s_const, 16)
            sp.dma_start(xa[:, :, :], x).then_inc(s_const, 16)
            sp.dma_start(cst[:], consts).then_inc(s_const, 16)
            sp.dma_start(rowv[:, :, :], rows4.broadcast_to([P, ROWS4, D])).then_inc(s_const, 16)

            def load(ring, sems, dram, n):
                h, t = half(n)
                sp.dma_start(ring[:, n % RING, 0:HWID[h]],
                             dram[t * P:(t + 1) * P, HOFF[h]:HOFF[h] + HWID[h]]).then_inc(sems[n % RING], 16)

            for n in range(STEPS):
                if n >= RING:
                    m = n - RING
                    sp.wait_ge(s_pe0, m + 1)
                    sp.wait_ge(s_act0, 3 * (m + 1))
                    taken = (m // T) * (T - 1) + m % T
                    if taken:
                        sp.wait_ge(s_cand, taken)
                load(rows, s_rows, adj_rows, n)
                load(cols, s_cols, adj_cols, n)
            for n in range(STEPS, 2 * STEPS):
                m = n - RING
                if m < STEPS:
                    sp.wait_ge(s_pe0, m + 1)
                    sp.wait_ge(s_act0, 3 * (m + 1))
                else:
                    sp.wait_ge(s_pe1, m + 1 - STEPS)
                load(cols, s_cols, adj_cols, n)
            for n in range(STEPS, STEPS + RING):
                m = n - RING
                sp.wait_ge(s_cand, (m // T) * (T - 1) + m % T)
                sp.wait_ge(s_pe0, m + 1)
                sp.wait_ge(s_act0, 3 * (m + 1))
                load(rows, s_rows, adj_rows, n)
            sp.wait_ge(s_sd, T)
            sp.dma_start(d_table.rearrange("(t p) d -> p t d", p=P), sd[:, :, D:2 * D]).then_inc(s_tab, 16)
            sp.wait_ge(s_flag, 1)
            over = sp.value_load(flag[0:1, 0:1], min_val=0, max_val=1)
            with sp.If(over > 0):
                with sp.Fori(0, N // 2) as g:
                    for r in range(2):
                        sp.wait_ge(s_dense, 2 * g + r + 1)
                        sp.dma_start(ring2[:, r * NP:r * NP + N],
                                     adj_rows[bass.ds(2 * g + r, 1), :].broadcast_to([P, N])).then_inc(s_row[r], 16)
            with sp.Else():
                sp.nop()
            for n in range(STEPS + RING, 2 * STEPS):
                sp.wait_ge(s_t2, n - RING + 1 - STEPS)
                load(rows, s_rows, adj_rows, n)
            for h in range(2):
                sp.wait_ge(s_x[4], (h + 1) * HT)
                if h == 0:
                    sp.dma_start(out[0:HT * P, :].rearrange("(t p) d -> p t d", p=P),
                                 xa[:, 0:HT, :]).then_inc(s_out, 16)
                else:
                    full = N // P
                    sp.dma_start(out[HT * P:full * P, :].rearrange("(t p) d -> p t d", p=P),
                                 xa[:, HT:full, :]).then_inc(s_out, 16)
                    sp.dma_start(out[full * P:N, :], xa[0:N - full * P, full, :]).then_inc(s_out, 16)
            sp.wait_ge(s_out, 48)

        @block.gpsimd
        def _(pool):
            pool.wait_ge(s_flag, 1)
            over = pool.value_load(flag[0:1, 0:1], min_val=0, max_val=1)
            with pool.If(over > 0):
                pool.nop()
            with pool.Else():
                pool.wait_ge(s_tab, 16)
                for i, (t, u, k, n) in enumerate(BAT):
                    if u is None:
                        continue
                    g = gather_no[i]
                    if g >= NG:
                        prev = [j for j in gather_no if gather_no[j] == g - NG][0]
                        pool.wait_ge(s_zed, prev + 1)
                    for j in range(n):
                        at = SLOT_AT[u] + k + j
                        nc.gpsimd.indirect_dma_start(
                            got(g)[:, j * D:(j + 1) * D], None, d_table,
                            bass.IndirectOffsetOnAxis(ap=col[:, at:at + 1], axis=0),
                        ).then_inc(s_got[g % NG], 16)

        @block.scalar
        def _(act):
            act.wait_ge(s_const, 80)
            act.wait_ge(s_zero, 1)
            for u in range(NHEAD):
                w = HEAD_W[u]
                nc.scalar.activation(sd[:, :, :].rearrange("p t d -> p (t d)")[:, HEAD_AT[u]:HEAD_AT[u] + w],
                                     head_a[:, HEAD_AT[u]:HEAD_AT[u] + w], ACT.Sign,
                                     accum_out=head_sg[:, u:u + 1]).then_inc(s_hsg, 1)
            big = sd[:, :, :].rearrange("p t d -> p (t d)")
            for n in range(STEPS):
                h, t = half(n)
                if n < 2:
                    act.wait_ge(s_hsg, NHEAD)
                for q, (ring, sems, func) in enumerate(((rows, s_rows, ACT.Copy), (rows, s_rows, ACT.Sign),
                                                        (cols, s_cols, ACT.Copy))):
                    if q != 1:
                        act.wait_ge(sems[n % RING], 16 * (n // RING + 1))
                    m = 3 * n + q
                    if m >= 4:
                        act.wait_ge(s_act0, m - 3)
                    nc.scalar.activation(big[:, (m % 4) * HWID[0]:(m % 4) * HWID[0] + HWID[h]],
                                         ring[:, n % RING, 0:HWID[h]], func,
                                         accum_out=sums[:, q, h, t:t + 1]).then_inc(s_act0, 1)
                if t == T - 1:
                    act.wait_ge(s_pe0, n + 1)
                    for b, (c, w) in enumerate(chunks(h)):
                        nc.scalar.copy(pt1[:, HOFF[h] + c:HOFF[h] + c + w], ps[b][:, 0:w]).then_inc(s_ev0, 1)
                        nc.scalar.copy(pt2[:, HOFF[h] + c:HOFF[h] + c + w], ps[NB + b][:, 0:w]).then_inc(s_ev0, 1)

            def std(l):
                for h in range(2):
                    act.wait_ge(s_mv[l], 2 * HT * (h + 1))
                    nc.scalar.activation(rstd[:, 0, h * HT:(h + 1) * HT], mv[:, h * HT:(h + 1) * HT, 1], ACT.Sqrt,
                                         bias=eps[:, 0:1]).then_inc(s_std[l], 1)

            def transposed(l):
                for t in range(T):
                    act.wait_ge(s_tp[l], t + 1)
                    nc.scalar.copy(xt[:, t * P:(t + 1) * P], ps[6 + t % 2][:, 0:P]).then_inc(s_xt[l], 1)

            std(0)
            transposed(0)
            for h in range(2):
                act.wait_ge(s_pe1, (h + 1) * T)
                for b, (c, w) in enumerate(chunks(h)):
                    nc.scalar.copy(pt1[:, HOFF[h] + c:HOFF[h] + c + w], ps[b][:, 0:w]).then_inc(s_ev1, 1)
            act.wait_ge(s_deg, 9)
            for i, (h, c, w) in enumerate(CH):
                b = i % 2
                p = ps[4 * b:4 * b + 4]
                act.wait_ge(s_msgp, i + 1)
                nc.scalar.activation(pt2[:, c:c + w], p[0][:, 0:w], ACT.Relu, bias=W("b_msg")).then_inc(s_msg, 1)
                act.wait_ge(s_gp, i + 1)
                for g in range(2):
                    if i >= 2:
                        act.wait_ge(s_hc, 4 * (i - 1))
                    nc.scalar.activation(gate(g, b)[:, 0:w], p[1 + g][:, 0:w], ACT.Sigmoid,
                                         bias=b_rz[:, g:g + 1]).then_inc(s_rz, 1)
                act.wait_ge(s_nin, 2 * (i + 1))
                nc.scalar.activation(gate(3, b)[:, 0:w], gate(2, b)[:, 0:w], ACT.Tanh,
                                     bias=W("b_ih", 2, 1)).then_inc(s_n, 1)
            for t in range(T):
                act.wait_ge(s_hp, t + 1)
                nc.scalar.copy(hn[:, t, :], ps[t % 8][:, 0:P]).then_inc(s_hs, 1)
            std(1)
            transposed(1)
            for t in range(T):
                act.wait_ge(s_sdp, t + 1)
                nc.scalar.copy(sd[:, t, :], ps[t % 6][:, 0:2 * D]).then_inc(s_sd, 1)
            act.wait_ge(s_flag, 1)
            over = act.value_load(flag[0:1, 0:1], min_val=0, max_val=1)
            with act.If(over > 0):
                for i, (h, c, w) in enumerate(CH):
                    act.wait_ge(s_dtp, i + 1)
                    nc.scalar.activation(pt1[:, c:c + w], ps[i % 2][:, 0:w], ACT.Identity).then_inc(s_dt, 1)
                    nc.scalar.activation(pt2[:, c:c + w], ps[2 + i % 2][:, 0:w], ACT.Identity,
                                         bias=W("msg_b")).then_inc(s_dt, 1)
                act.wait_ge(s_dt, 2 * len(CH))
                with act.Fori(0, N // 2) as g:
                    for r in range(2):
                        act.wait_ge(s_dense, 2 * g + r + 1)
                        nc.scalar.activation(ring2[:, 2 * NP:2 * NP + N], pt1[:, 0:N], ACT.Gelu,
                                             bias=pt2[:, bass.ds(2 * g + r, 1)]).then_inc(s_gd, 1)
            with act.Else():
                for u in range(NHEAD):
                    act.wait_ge(s_su, u + 1)
                    nc.scalar.copy(pt2[:, u * D:(u + 1) * D], ps[u][:, 0:D]).then_inc(s_suc, 1)
                done = 0
                for i, (t, u, k, n) in enumerate(BAT):
                    act.wait_ge(s_zed, i + 1)
                    if i >= NZ:
                        act.wait_ge(s_bat, i - NZ + 1)
                    nc.scalar.activation(gel(i)[:, 0:n * D], zed(i)[:, 0:n * D], ACT.Gelu).then_inc(s_gel, 1)
                    while done < T and LASTB[done] <= i - 2:
                        act.wait_ge(s_bat, LASTB[done] + 1)
                        nc.scalar.copy(pt1[:, done * P:(done + 1) * P], ps[4 + done % 2][:, 0:P]).then_inc(s_agg, 1)
                        done += 1
                while done < T:
                    act.wait_ge(s_bat, LASTB[done] + 1)
                    nc.scalar.copy(pt1[:, done * P:(done + 1) * P], ps[4 + done % 2][:, 0:P]).then_inc(s_agg, 1)
                    done += 1
            act.wait_ge(s_agg, T)
            for t in range(T):
                act.wait_ge(s_up, t + 1)
                nc.scalar.activation(hn[:, t, :], ps[t % 8][:, 0:D], ACT.Gelu).then_inc(s_ug, 1)
            std(2)
            std(3)
            transposed(3)
            act.wait_ge(s_att, 1)
            nc.scalar.copy(att[:, 0:2], ps[0][:, 0:2]).then_inc(s_attc, 1)
            act.wait_ge(s_attc, 1)
            nc.scalar.activation(att[:, 2:2 + P], C("ones"), ACT.Copy, scale=att[:, 1:2]).then_inc(s_attc, 1)
            for t in range(T):
                act.wait_ge(s_att, 2 + t)
                nc.scalar.copy(hn[:, t, :], ps[t % 6][:, 0:D]).then_inc(s_attc, 1)
                nc.scalar.copy(src[:, t:t + 1], ps[t % 6][:, D:D + 1]).then_inc(s_attc, 1)
            for i, (h, c, w) in enumerate(CH):
                act.wait_ge(s_att, 2 + T + i)
                nc.scalar.copy(pt1[:, c:c + w], ps[i % 6][:, 0:w]).then_inc(s_attc, 1)
            act.wait_ge(s_attc, 2 + 2 * T + len(CH))
            nc.scalar.mul(src2[:, :], src[:, :], 0.2).then_inc(s_attc, 1)
            act.wait_ge(s_attc, 3 + 2 * T + len(CH))
            for n in range(STEPS):
                h, t = half(n)
                g = cols[:, n % 2, 0:HWID[h]]
                if n >= 2:
                    act.wait_ge(s_t1, n - 1)
                nc.scalar.activation(g, pt1[:, HOFF[h]:HOFF[h] + HWID[h]], ACT.Relu,
                                     bias=src[:, t:t + 1]).then_inc(s_rel, 1)
                act.wait_ge(s_rel, n + 1)
                nc.scalar.activation(g, g, ACT.Exp, bias=src2[:, t:t + 1], scale=0.8).then_inc(s_g, 1)
            for t in range(T):
                act.wait_ge(s_zp, t + 1)
                nc.scalar.copy(hn[:, t, :], ps[6 + t % 2][:, 0:P]).then_inc(s_zs, 1)
            std(4)

        @block.vector
        def _(dve):
            V = nc.vector
            V.memset(pt1[:, N:NP], 0.0).then_inc(s_deg, 1)
            V.memset(pt2[:, N:NP], 0.0).then_inc(s_deg, 1)
            V.memset(left[:, :, :], 0.0).then_inc(s_deg, 1)
            V.memset(eps[:, :], EPS).then_inc(s_deg, 1)
            dve.wait_ge(s_deg, 4)
            V.memset(flag[0:1, 0:1], 0).then_inc(s_zero, 1)
            dve.wait_ge(s_const, 80)
            dve.wait_ge(s_hsg, NHEAD)
            cnt = [0]

            def hx(ins):
                cnt[0] += 1
                ins.then_inc(s_headx, 1)
                dve.wait_ge(s_headx, cnt[0])

            for u in range(NHEAD):
                a = head_a[:, HEAD_AT[u]:HEAD_AT[u + 1]]
                for r in range(ROUNDS[u]):
                    at = SLOT_AT[u] + 8 * r
                    hx(V.max(vals[:, at:at + 8], a))
                    hx(V.max_index(pos[:, at:at + 8], vals[:, at:at + 8], a))
                    hx(V.match_replace(a, vals[:, at:at + 8], a, 0.0))
                s = slice(SLOT_AT[u], SLOT_AT[u + 1])
                hx(V.reduce_max(left[:, 0, u:u + 1], a, AX))
                hx(V.tensor_scalar(col_f[:, s], pos[:, s], float(HEAD[u][2]), C("head_part", u, 1), ALU.mult, ALU.add))
                hx(V.tensor_scalar(pos_f[:, s], vals[:, s], 0.0, 0.0, ALU.is_gt, ALU.add, accum_out=found[:, u:u + 1]))
                hx(V.scalar_tensor_tensor(vals[:, s], col_f[:, s], C("head_row", u, 1), vals[:, s], ALU.not_equal, ALU.mult))
                hx(V.tensor_scalar(col[:, s], col_f[:, s], float(N - 1), None, ALU.min))

            nm = 0
            for n in range(STEPS):
                h, t = half(n)
                if t == 0:
                    continue
                dve.wait_ge(s_rows[n % RING], 16 * (n // RING + 1))
                kind = seg_kind(t)
                bounds = seg_bounds(kind)[h]
                at = CAND_AT[t] + 8 * (SEG_KINDS[kind][0] if h else 0)
                for k in range(len(bounds) - 1):
                    a = rows[:, n % RING, bounds[k] - HOFF[h]:bounds[k + 1] - HOFF[h]]
                    V.max(cand[:, at + 8 * k:at + 8 * k + 8], a).then_inc(s_max, 1)
                    nm += 1
                dve.wait_ge(s_max, nm)
                for k in range(len(bounds) - 1):
                    a = rows[:, n % RING, bounds[k] - HOFF[h]:bounds[k + 1] - HOFF[h]]
                    ins = V.max_index(cand_i[:, at + 8 * k:at + 8 * k + 8], cand[:, at + 8 * k:at + 8 * k + 8], a)
                ins.then_inc(s_cand, 1)

            dg = [4]

            def dx(ins):
                dg[0] += 1
                ins.then_inc(s_deg, 1)
                dve.wait_ge(s_deg, dg[0])

            dve.wait_ge(s_act0, 3 * STEPS)
            dx(V.tensor_tensor(degs[:, 0, :, :], sums[:, 0::2, 0, :], sums[:, 0::2, 1, :], ALU.add))
            dx(V.tensor_scalar(degs[:, 1, :, :], degs[:, 0, :, :], 0.0, None, ALU.is_gt))
            dx(V.tensor_tensor(degs[:, 0, :, :], degs[:, 0, :, :], degs[:, 1, :, :], ALU.mult))
            dx(V.tensor_scalar(degs[:, 2, :, :], degs[:, 1, :, :], -1.0, 1.0, ALU.mult, ALU.add))
            dx(V.tensor_tensor(b_rz[:, :], W("b_ih", 0, 2), W("b_hh", 0, 2), ALU.add))
            dx(V.tensor_tensor(degs[:, 0, :, :], degs[:, 0, :, :], degs[:, 2, :, :], ALU.add))
            dx(V.reciprocal(recip[:, :, :], degs[:, 0, :, :]))

            def moments(l, h_tile, ready=None):
                for t in range(T):
                    if ready:
                        ready(t)
                    V.bn_stats(stats[:, t, :], h_tile(t)).then_inc(s_mv[l], 1)
                    dve.wait_ge(s_mv[l], 2 * t + 1)
                    V.bn_aggr(mv[:, t, :], stats[:, t, :]).then_inc(s_mv[l], 1)

            def normalise(l, h_tile, to):
                for h in range(2):
                    s = slice(h * HT, (h + 1) * HT)
                    dve.wait_ge(s_std[l], h + 1)
                    V.reciprocal(rstd[:, 1, s], rstd[:, 0, s]).then_inc(s_rstd[l], 1)
                    dve.wait_ge(s_rstd[l], h + 1)
                    for t in range(h * HT, (h + 1) * HT):
                        V.tensor_scalar(to(t), h_tile(t), mv[:, t, 0:1], rstd[:, 1, t:t + 1],
                                        ALU.subtract, ALU.mult).then_inc(s_x[l], 1)

            tile = lambda a: (lambda t: a[:, t, :])

            def layer0(t):
                dve.wait_ge(s_p0, t + 1)
                V.scalar_tensor_tensor(hn[:, t, :], ps[t % 8][:, 0:D], recip[:, 0, t:t + 1], xa[:, t, :],
                                       ALU.mult, ALU.add).then_inc(s_h0, 1)
                dve.wait_ge(s_h0, 2 * t + 1)
                V.scalar_tensor_tensor(hn[:, t, :], ps[t % 8][:, D:2 * D], recip[:, 1, t:t + 1], hn[:, t, :],
                                       ALU.mult, ALU.add).then_inc(s_h0, 1)
                dve.wait_ge(s_h0, 2 * t + 2)

            moments(0, tile(hn), layer0)
            normalise(0, tile(hn), tile(xb))

            ex = [0]

            def sx(ins, wait=True):
                ex[0] += 1
                ins.then_inc(s_ex, 1)
                if wait:
                    dve.wait_ge(s_ex, ex[0])

            dve.wait_ge(s_cand, 2 * (T - 1))
            for t in range(1, T):
                u, kind, w, b = NHEAD + t - 1, seg_kind(t), cand_width(t), t % 2
                v = cand[:, CAND_AT[t]:CAND_AT[t] + w]
                cc, cv = cand_c[:, b, 0:w], cand_v[:, b, 0:w]
                sx(V.tensor_tensor(cc, cand_i[:, CAND_AT[t]:CAND_AT[t] + w], C("seg_base", BASE_AT[kind], w), ALU.add), False)
                sx(V.tensor_scalar(cv, v, 0.0, 0.0, ALU.is_gt, ALU.add, accum_out=found[:, u:u + 1]), False)
                sx(V.reduce_max(left[:, 1, u:u + 1], v.rearrange("p (s e) -> p s e", e=8)[:, :, 7], AX))
                sx(V.scalar_tensor_tensor(cv, cc, C("row", t, 1), v, ALU.not_equal, ALU.mult))
                s0 = SLOT_AT[u]
                for r in range(ROUNDS[u]):
                    at = s0 + 8 * r
                    sx(V.max(vals[:, at:at + 8], cv))
                    sx(V.max_index(pos[:, at:at + 8], vals[:, at:at + 8], cv), False)
                    sx(V.match_replace(cv, vals[:, at:at + 8], cv, 0.0))
                sx(V.reduce_max(left[:, 0, u:u + 1], cv, AX), False)
                if SLOTS[u] % 8:
                    sx(V.reduce_max(left[:, 2, u:u + 1], vals[:, s0 + SLOTS[u]:SLOT_AT[u + 1]], AX), False)
                sx(V.tensor_copy(pos_f[:, s0:SLOT_AT[u + 1]], pos[:, s0:SLOT_AT[u + 1]]))
                for k in range(SLOTS[u]):
                    if k >= 2:
                        dve.wait_ge(s_ex, ex[0] - 1)
                    sx(V.scalar_tensor_tensor(look[:, k % 2, 0:w], C("iota", 0, w), pos_f[:, s0 + k:s0 + k + 1], cc,
                                              ALU.is_equal, ALU.mult, accum_out=col_f[:, s0 + k:s0 + k + 1]), False)
                dve.wait_ge(s_ex, ex[0])
                sx(V.tensor_copy(col[:, s0:s0 + SLOTS[u]], col_f[:, s0:s0 + SLOTS[u]]), False)
            for u in range(NHEAD):
                if SLOTS[u] % 8:
                    sx(V.reduce_max(left[:, 2, u:u + 1], vals[:, SLOT_AT[u] + SLOTS[u]:SLOT_AT[u + 1]], AX), False)
            sx(V.tensor_tensor(degs[:, 0, 0, :], sums[:, 1, 0, :], sums[:, 1, 1, :], ALU.add))
            sx(V.tensor_tensor(bad[:, 0, 0:NHEAD], found[:, 0:NHEAD], head_sg[:, :], ALU.not_equal), False)
            sx(V.tensor_tensor(bad[:, 0, NHEAD:UNITS], found[:, NHEAD:UNITS], degs[:, 0, 0, 1:T], ALU.not_equal), False)
            sx(V.tensor_scalar(bad[:, 1:4, :], left[:, :, :], 0.0, None, ALU.not_equal))
            sx(V.tensor_reduce(badc[:, :], bad[:, 0:4, :], mybir.AxisListType.XY, ALU.add))
            assert ex[0] == EX_BAD
            dve.wait_ge(s_badp, 1)
            V.tensor_scalar(flag[0:1, 0:1], ps[7][0:1, 0:1], 0.0, None, ALU.not_equal).then_inc(s_flag, 1)

            for i, (h, c, w) in enumerate(CH):
                b = i % 2
                p = ps[4 * b:4 * b + 4]
                r, z, a, m, o = (gate(k, b)[:, 0:w] for k in range(5))
                dve.wait_ge(s_rz, 2 * i + 2)
                V.scalar_tensor_tensor(a, p[3][:, 0:w], W("b_hh", 2, 1), r, ALU.add, ALU.mult).then_inc(s_nin, 1)
                dve.wait_ge(s_nin, 2 * i + 1)
                V.tensor_tensor(a, a, p[0][:, 0:w], ALU.add).then_inc(s_nin, 1)
                dve.wait_ge(s_n, i + 1)
                V.tensor_tensor(o, xt[:, c:c + w], m, ALU.subtract).then_inc(s_hc, 1)
                dve.wait_ge(s_hc, 4 * i + 1)
                V.tensor_tensor(o, z, o, ALU.mult).then_inc(s_hc, 1)
                dve.wait_ge(s_hc, 4 * i + 2)
                V.tensor_tensor(o, m, o, ALU.add).then_inc(s_hc, 1)
                dve.wait_ge(s_hc, 4 * i + 3)
                V.tensor_tensor(pt1[:, c:c + w], xt[:, c:c + w], o, ALU.add).then_inc(s_hc, 1)
            moments(1, tile(hn), lambda t: dve.wait_ge(s_hs, t + 1))
            normalise(1, tile(hn), tile(xa))

            over = None
            dve.wait_ge(s_flag, 1)
            over = dve.value_load(flag[0:1, 0:1], min_val=0, max_val=1)
            dve.wait_ge(s_sd, T)
            with dve.If(over > 0):
                V.memset(badc[:, :], 0.0).then_inc(s_dense, 1)
                with dve.Fori(0, N // 2) as g:
                    for r in range(2):
                        dve.wait_ge(s_row[r], 16 * g + 16)
                        dve.wait_ge(s_gd, 2 * g + r + 1)
                        V.scalar_tensor_tensor(ring2[:, 2 * NP:2 * NP + N],
                                               ring2[:, 2 * NP:2 * NP + N], 1.0, ring2[:, r * NP:r * NP + N],
                                               ALU.mult, ALU.mult,
                                               accum_out=xb[:, :, :].rearrange("p t d -> p (t d)")[:, bass.ds(2 * g + r, 1)]).then_inc(s_dense, 1)
                dve.wait_ge(s_dense, N + 1)
                V.tensor_copy(pt1[:, 0:N], xb[:, :, :].rearrange("p t d -> p (t d)")[:, 0:N]).then_inc(s_agg, T)
            with dve.Else():
                nd = 0
                for i, (t, u, k, n) in enumerate(BAT):
                    if u is None:
                        if i >= NZ:
                            dve.wait_ge(s_gel, i - NZ + 1)
                        V.tensor_tensor(zed(i)[:, 0:D], sd[:, t, 0:D], sd[:, t, D:2 * D], ALU.add).then_inc(s_zed, 1)
                    else:
                        g = gather_no[i]
                        dve.wait_ge(s_got[g % NG], 16 * gathers_of[g])
                        if i >= NZ:
                            dve.wait_ge(s_gel, i - NZ + 1)
                        if u < NHEAD:
                            dve.wait_ge(s_suc, u + 1)
                            s_of = pt2[:, u * D:(u + 1) * D]
                        else:
                            s_of = sd[:, t, 0:D]
                        V.tensor_tensor(zed(i)[:, 0:n * D].rearrange("p (j d) -> p j d", d=D),
                                        got(g)[:, 0:n * D].rearrange("p (j d) -> p j d", d=D),
                                        s_of.unsqueeze(1).broadcast_to([P, n, D]), ALU.add).then_inc(s_zed, 1)
                    if i >= NZ:
                        dve.wait_ge(s_bat, i - NZ + 1)
                    for j in range(n):
                        if u is None:
                            val, to = W("diag", t, 1), ident
                        else:
                            at = SLOT_AT[u] + k + j
                            val, to = vals[:, at:at + 1], (C("spread", u * P, P) if u < NHEAD else ident)
                        ins = V.tensor_scalar(dia(i)[:, j * P:(j + 1) * P], to, val, None, ALU.mult)
                    ins.then_inc(s_dia, 1)
            dve.wait_ge(s_agg, T)
            h2 = [0]

            def hx2(ins, wait=True):
                h2[0] += 1
                ins.then_inc(s_h2, 1)
                if wait:
                    dve.wait_ge(s_h2, h2[0])

            def add_x2(t):
                dve.wait_ge(s_ug, t + 1)
                hx2(V.tensor_tensor(hn[:, t, :], hn[:, t, :], xa[:, t, :], ALU.add))

            moments(2, tile(hn), add_x2)
            normalise(2, tile(hn), tile(hn))

            def affine(t):
                dve.wait_ge(s_x[2], t + 1)
                hx2(V.tensor_tensor(hn[:, t, :], hn[:, t, :], rowv[:, 2, :], ALU.mult))
                hx2(V.tensor_tensor(hn[:, t, :], hn[:, t, :], rowv[:, 3, :], ALU.add))
                hx2(V.tensor_tensor(hn[:, t, :], hn[:, t, :], xa[:, t, :], ALU.add))

            moments(3, tile(hn), affine)
            normalise(3, tile(hn), tile(xb))

            dve.wait_ge(s_attc, 3 + 2 * T + len(CH))
            for n in range(STEPS):
                h, t = half(n)
                w = HWID[h]
                g, t1, t2 = cols[:, n % 2, 0:w], cols[:, 2 + n % 2, 0:w], cols[:, 4 + n % 2, 0:w]
                pair = pt2[:, n // 2 % 2 * HWID[0]:n // 2 % 2 * HWID[0] + w]
                a = rows[:, (n + STEPS) % RING, 0:w]
                dve.wait_ge(s_rows[(n + STEPS) % RING], 16 * ((n + STEPS) // RING + 1))
                dve.wait_ge(s_g, n + 1)
                if n >= 2:
                    dve.wait_ge(s_pe3, n - 1)
                    dve.wait_ge(s_tsum, n // 2)
                V.tensor_tensor(t1, a, g, ALU.mult).then_inc(s_t1, 1)
                dve.wait_ge(s_t1, n + 1)
                V.tensor_tensor(t2, a, t1, ALU.mult).then_inc(s_t2, 1)
                if t % 2:
                    if n >= 4:
                        dve.wait_ge(s_pe3, n - 3)
                    V.tensor_tensor(pair, cols[:, 2, 0:w], t1, ALU.add).then_inc(s_tsum, 1)
                if t == T - 1:
                    for i, (hh, c, w) in enumerate(CH):
                        if hh != h:
                            continue
                        b = i % NB
                        dve.wait_ge(s_pe3, T * (h + 1))
                        V.reciprocal(pt1[:, c:c + w], ps[NB + b][:, 0:w]).then_inc(s_z, 1)
                        dve.wait_ge(s_z, 3 * i + 1)
                        V.tensor_tensor(pt1[:, c:c + w], ps[b][:, 0:w], pt1[:, c:c + w], ALU.mult).then_inc(s_z, 1)
                        dve.wait_ge(s_z, 3 * i + 2)
                        V.tensor_tensor(pt1[:, c:c + w], pt1[:, c:c + w], xt[:, c:c + w], ALU.add).then_inc(s_z, 1)
            moments(4, tile(hn), lambda t: dve.wait_ge(s_zs, t + 1))
            normalise(4, tile(hn), tile(xa))

        @block.tensor
        def _(pe):
            mm = nc.tensor.matmul

            def transposes(l, of):
                for t in range(T):
                    pe.wait_ge(s_x[l], t + 1)
                    if t >= 2:
                        pe.wait_ge(s_xt[l], t - 1)
                    nc.tensor.transpose(ps[6 + t % 2][:, 0:P], of[:, t, :], ident).then_inc(s_tp[l], 1)

            pe.wait_ge(s_const, 80)
            for n in range(STEPS):
                h, t = half(n)
                pe.wait_ge(s_cols[n % RING], 16 * (n // RING + 1))
                pe.wait_ge(s_rows[n % RING], 16 * (n // RING + 1))
                if n == T:
                    pe.wait_ge(s_ev0, 2 * NB)
                for ring, b0 in ((cols, 0), (rows, NB)):
                    for b, (c, w) in enumerate(chunks(h)):
                        last = mm(ps[b0 + b][:, 0:w], xa[:, t, :], ring[:, n % RING, c:c + w],
                                  start=(t == 0), stop=(t == T - 1))
                last.then_inc(s_pe0, 1)
            pe.wait_ge(s_ev0, 4 * NB)
            pe.wait_ge(s_deg, 2)
            for t in range(T):
                if t >= 8:
                    pe.wait_ge(s_h0, 2 * (t - 7))
                s = slice(t * P, (t + 1) * P)
                mm(ps[t % 8][:, 0:D], pt1[:, s], W("w_in"), start=True, stop=True)
                mm(ps[t % 8][:, D:2 * D], pt2[:, s], W("w_out"), start=True, stop=True).then_inc(s_p0, 1)
            transposes(0, xb)

            for n in range(STEPS):
                h, t = half(n)
                m = n + STEPS
                pe.wait_ge(s_cols[m % RING], 16 * (m // RING + 1))
                if n == T:
                    pe.wait_ge(s_ev1, NB)
                for b, (c, w) in enumerate(chunks(h)):
                    last = mm(ps[b][:, 0:w], xb[:, t, :], cols[:, m % RING, c:c + w],
                              start=(t == 0), stop=(t == T - 1))
                last.then_inc(s_pe1, 1)
            pe.wait_ge(s_ex, EX_BAD)
            mm(ps[7][0:1, 0:1], badc[:, 0:1], C("ones", 0, 1), start=True, stop=True).then_inc(s_badp, 1)
            pe.wait_ge(s_ev1, 2 * NB)
            pe.wait_ge(s_xt[0], T)
            pe.wait_ge(s_flag, 1)

            def message(i):
                h, c, w = CH[i]
                if i >= 2:
                    pe.wait_ge(s_hc, 4 * (i - 1))
                mm(ps[4 * (i % 2)][:, 0:w], W("w_msg_t"), pt1[:, c:c + w], start=True, stop=True).then_inc(s_msgp, 1)

            message(0)
            for i, (h, c, w) in enumerate(CH):
                if i + 1 < len(CH):
                    message(i + 1)
                p = ps[4 * (i % 2):4 * (i % 2) + 4]
                pe.wait_ge(s_msg, i + 1)
                for g in range(2):
                    mm(p[1 + g][:, 0:w], W("w_ih_t", g * D, D), pt2[:, c:c + w], start=True, stop=False)
                    mm(p[1 + g][:, 0:w], W("w_hh_t", g * D, D), xt[:, c:c + w], start=False, stop=True)
                mm(p[0][:, 0:w], W("w_ih_t", 2 * D, D), pt2[:, c:c + w], start=True, stop=True)
                mm(p[3][:, 0:w], W("w_hh_t", 2 * D, D), xt[:, c:c + w], start=True, stop=True).then_inc(s_gp, 1)
            pe.wait_ge(s_hc, 4 * len(CH))
            for t in range(T):
                if t >= 8:
                    pe.wait_ge(s_hs, t - 7)
                nc.tensor.transpose(ps[t % 8][:, 0:P], pt1[:, t * P:(t + 1) * P], ident).then_inc(s_hp, 1)
            transposes(1, xa)

            for t in range(T):
                pe.wait_ge(s_xt[1], t + 1)
                if t >= 6:
                    pe.wait_ge(s_sd, t - 5)
                mm(ps[t % 6][:, 0:2 * D], xt[:, t * P:(t + 1) * P], W("w_sd"), start=True, stop=False)
                mm(ps[t % 6][:, 0:D], C("ones")[0:1, :], rowv[0:1, 0, :], start=False, stop=True).then_inc(s_sdp, 1)
            pe.wait_ge(s_flag, 1)
            over = pe.value_load(flag[0:1, 0:1], min_val=0, max_val=1)
            pe.wait_ge(s_sd, T)
            with pe.If(over > 0):
                for i, (h, c, w) in enumerate(CH):
                    if i >= 2:
                        pe.wait_ge(s_dt, 2 * (i - 1))
                    mm(ps[i % 2][:, 0:w], W("w_sd", D, D), xt[:, c:c + w], start=True, stop=True)
                    mm(ps[2 + i % 2][:, 0:w], W("w_sd", 0, D), xt[:, c:c + w], start=True, stop=True).then_inc(s_dtp, 1)
            with pe.Else():
                for u in range(NHEAD):
                    mm(ps[u][:, 0:D], C("spread_t", u * P, P), sd[:, 0, 0:D], start=True, stop=True).then_inc(s_su, 1)
                for i, (t, u, k, n) in enumerate(BAT):
                    first = u is None
                    if first and t >= 2:
                        pe.wait_ge(s_agg, t - 1)
                    pe.wait_ge(s_gel, i + 1)
                    pe.wait_ge(s_dia, i + 1)
                    for j in range(n):
                        last = mm(ps[4 + t % 2][:, 0:P], gel(i)[:, j * D:(j + 1) * D], dia(i)[:, j * P:(j + 1) * P],
                                  start=first, stop=(i == LASTB[t] and j == n - 1))
                    last.then_inc(s_bat, 1)
            pe.wait_ge(s_agg, T)
            for t in range(T):
                s = slice(t * P, (t + 1) * P)
                if t >= 8:
                    pe.wait_ge(s_ug, t - 7)
                mm(ps[t % 8][:, 0:D], xt[:, s], W("upd_x"), start=True, stop=False)
                mm(ps[t % 8][:, 0:D], pt1[:, s], W("upd_a"), start=False, stop=False)
                mm(ps[t % 8][:, 0:D], C("ones")[0:1, :], rowv[0:1, 1, :], start=False, stop=True).then_inc(s_up, 1)
            transposes(3, xb)

            mm(ps[0][:, 0:2], W("w3"), W("att_src", 0, 2), start=True, stop=True).then_inc(s_att, 1)
            pe.wait_ge(s_attc, 2)
            for t in range(T):
                pe.wait_ge(s_xt[3], t + 1)
                if t >= 6:
                    pe.wait_ge(s_attc, 2 + 2 * (t - 5))
                s = slice(t * P, (t + 1) * P)
                mm(ps[t % 6][:, 0:D], xt[:, s], W("w3_t"), start=True, stop=True)
                mm(ps[t % 6][:, D:D + 1], xt[:, s], att[:, 0:1], start=True, stop=True).then_inc(s_att, 1)
            pe.wait_ge(s_attc, 2 + 2 * T)
            for i, (h, c, w) in enumerate(CH):
                mm(ps[i % 6][:, 0:w], att[:, 2:2 + P], xt[:, c:c + w], start=True, stop=True).then_inc(s_att, 1)
            pe.wait_ge(s_attc, 2 + 2 * T + len(CH))
            for n in range(STEPS):
                h, t = half(n)
                if n == T:
                    pe.wait_ge(s_z, 3 * NB)
                pe.wait_ge(s_t2, n + 1)
                for b, (c, w) in enumerate(chunks(h)):
                    last = mm(ps[b][:, 0:w], hn[:, t, :], cols[:, 4 + n % 2, c:c + w],
                              start=(t == 0), stop=(t == T - 1))
                if t % 2:
                    pe.wait_ge(s_tsum, n // 2 + 1)
                    at = n // 2 % 2 * HWID[0]
                    for b, (c, w) in enumerate(chunks(h)):
                        last = mm(ps[NB + b][:, 0:w], C("ones"), pt2[:, at + c:at + c + w],
                                  start=(t == 1), stop=(t == T - 1))
                last.then_inc(s_pe3, 1)
            pe.wait_ge(s_z, 3 * len(CH))
            for t in range(T):
                if t >= 2:
                    pe.wait_ge(s_zs, t - 1)
                nc.tensor.transpose(ps[6 + t % 2][:, 0:P], pt1[:, t * P:(t + 1) * P], ident).then_inc(s_zp, 1)


_INS = ("x", "adj_rows", "adj_cols", "head", "weights", "rows4", "consts")


def kernel(**inputs):
    import concourse.bacc as bacc
    from concourse.bass_utils import run_bass_kernel_spmd as run

    a = {k: np.ascontiguousarray(v) for k, v in inputs.items()}
    adj = a["adj"]
    lay = {}
    xp = np.zeros((NP, D), adj.dtype)
    xp[:N] = a["x"]
    lay["x"] = np.ascontiguousarray(xp.reshape(T, P, D).transpose(1, 0, 2))
    for name, m in (("adj_rows", adj), ("adj_cols", adj.T)):
        lay[name] = np.zeros((NP, N), adj.dtype)
        lay[name][:N] = m
    head = np.zeros((P, HEAD_AT[NHEAD]), adj.dtype)
    for u, (row, nrows, parts) in enumerate(HEAD):
        for part in range(parts):
            m = adj[row:row + nrows, part::parts]
            head[part::parts, HEAD_AT[u]:HEAD_AT[u] + m.shape[1]] = m
    lay["head"] = head
    diag = np.zeros(NP, adj.dtype)
    diag[:N] = adj[np.arange(N), np.arange(N)]
    mw, uw = a["L2_gnn_msg_w"], a["L2_gnn_upd_w"]
    w = {
        "w_in": a["L0_gnn_W_in"], "w_out": a["L0_gnn_W_out"],
        "w_msg_t": a["L1_gnn_W_msg"].T, "w_ih_t": a["L1_gnn_W_ih"].T, "w_hh_t": a["L1_gnn_W_hh"].T,
        "w_sd": np.concatenate([mw[:, :D].T, mw[:, D:].T], axis=1), "upd_x": uw[:, :D].T, "upd_a": uw[:, D:].T,
        "w3_t": a["L3_gnn_weight"].T, "w3": a["L3_gnn_weight"],
        "b_msg": a["L1_gnn_b_msg"].reshape(D, 1),
        "b_ih": a["L1_gnn_b_ih"].reshape(3, D).T, "b_hh": a["L1_gnn_b_hh"].reshape(3, D).T,
        "msg_b": a["L2_gnn_msg_b"].reshape(D, 1),
        "att_src": a["L3_gnn_att_src"].reshape(D, 1), "att_dst": a["L3_gnn_att_dst"].reshape(D, 1),
        "diag": diag.reshape(T, P).T,
    }
    lay["weights"] = np.concatenate([w[k] for k in WEIGHT], axis=1)
    lay["rows4"] = np.stack([a["L2_gnn_msg_b"], a["L2_gnn_upd_b"], a["L2_gnn_ln_w"], a["L2_gnn_ln_b"]])[None]
    lay["consts"] = constants()

    nc = bacc.Bacc("TRN2", target_bir_lowering=False, num_devices=1)
    arrays = {f"in_{k}_dram": np.ascontiguousarray(lay[k]) for k in _INS}
    args = [nc.dram_tensor(k, v.shape, mybir.dt.from_np(v.dtype), kind="ExternalInput").ap() for k, v in arrays.items()]
    out = nc.dram_tensor("out_0_dram", (N, D), mybir.dt.float32, kind="ExternalOutput").ap()
    build(nc, *args, out)
    r = run(nc, [arrays], core_ids=[0])
    return r.results[0]["out_0_dram"]
```

```python
import math
from contextlib import ExitStack

import numpy as np

import concourse.bass as bass
from concourse import mybir
from concourse.alu_op_type import AluOpType as ALU

P = 128
N = 2708
T = -(-N // P)
NP = T * P
D = 128
HT = T // 2
HOFF = (0, HT * P)
HWID = (HT * P, N - HT * P)
BANK = 512
RING = 5
EPS = 1e-5

HEAD = ((0, 16, 8), (16, 16, 8), (32, 32, 4), (64, 64, 2))
HEAD_SLOTS = (40, 14, 20, 24)
HEAD_W = tuple(-(-N // parts) for _, _, parts in HEAD)
HEAD_AT = tuple(sum(HEAD_W[:u]) for u in range(len(HEAD) + 1))
TILE_SLOTS = (33, 23, 21, 24, 18, 18, 17, 17, 16, 14, 14, 14, 15, 12, 15, 11, 13, 12, 12, 11, 12)
SLOTS = HEAD_SLOTS + TILE_SLOTS
UNITS = len(SLOTS)
NHEAD = len(HEAD)
ROUNDS = tuple(-(-k // 8) for k in SLOTS)
SLOT_AT = tuple(8 * sum(ROUNDS[:u]) for u in range(UNITS + 1))
SLOT_N = SLOT_AT[UNITS]
CHUNKS = (12, 6, 8, 12) + (16, 13, 11, 10, 9, 8, 8, 7, 7, 7, 6, 6, 6, 6, 5, 5, 5, 5, 5, 5, 1)
CHUNK_AT = tuple(sum(CHUNKS[:u]) for u in range(UNITS + 1))
CHUNK_N = CHUNK_AT[UNITS]
R_MAX = max(k * 3 * c for k, c in zip(SLOTS, CHUNKS))
SEG_KINDS = ((11, 5), (9, 3), (6, 2))


def seg_kind(t):
    return 0 if t <= 2 else 1 if t <= 6 else 2


def seg_bounds(kind):
    n0, n1 = SEG_KINDS[kind]
    h = HOFF[1]
    first = [0]
    for k in range(1, n0):
        first.append(max(first[-1] + 8, round(h * (k / n0) ** 2)))
    a = math.sqrt(h / N)
    second = [round(N * (a + (1 - a) * k / n1) ** 2) for k in range(n1)]
    return [*first, h], [*second, N]


def cand_width(t):
    return 8 * sum(SEG_KINDS[seg_kind(t)])


CAND_AT = {t: sum(cand_width(s) for s in range(1, t)) for t in range(1, T + 1)}
BASE_AT = (0, 8 * sum(SEG_KINDS[0]), 8 * (sum(SEG_KINDS[0]) + sum(SEG_KINDS[1])))
BASE_N = BASE_AT[2] + 8 * sum(SEG_KINDS[2])
WIDEST = 8 * sum(SEG_KINDS[0])

BATCH = 4
IOTA = BATCH * P
CONST = {
    "ident": P,
    "spread_t": NHEAD * P,
    "before": P,
    "twice": 2 * P,
    "seg_base": BASE_N,
    "iota": IOTA,
    "batch_at": 4,
    "row": T,
    "head_row": NHEAD,
    "head_part": NHEAD,
    "ones": P,
}
CONST_AT = {}
for _name in CONST:
    CONST_AT[_name] = sum(CONST[k] for k in list(CONST)[: list(CONST).index(_name)])
CONST_N = sum(CONST.values())

WEIGHT = {
    "w_in": D, "w_out": D,
    "w_msg_t": D, "w_ih_t": 3 * D, "w_hh_t": 3 * D,
    "w_sd": 2 * D, "upd_x": D, "upd_a": D,
    "w3_t": D, "w3": D,
    "b_msg": 1, "b_ih": 3, "b_hh": 3, "msg_b": 1, "att_src": 1, "att_dst": 1,
    "diag": T,
}
WEIGHT_AT = {}
for _name in WEIGHT:
    WEIGHT_AT[_name] = sum(WEIGHT[k] for k in list(WEIGHT)[: list(WEIGHT).index(_name)])
WEIGHT_N = sum(WEIGHT.values())
ROWS4 = 4


def constants():
    c = {k: np.zeros((P, w), np.float32) for k, w in CONST.items()}
    c["ident"][:] = np.eye(P)
    c["ones"][:] = 1
    c["before"][:] = np.triu(np.ones((P, P)), 1)
    c["twice"][:] = np.arange(2 * P) % P
    c["iota"][:] = np.arange(IOTA)
    c["batch_at"][:] = -float(BATCH * P) * np.arange(4)
    c["row"][:] = np.arange(P)[:, None] + P * np.arange(T)
    for u, (row, _, parts) in enumerate(HEAD):
        p = np.arange(P)
        r = row + p // parts
        c["spread_t"][r, u * P + p] = 1
        c["head_row"][:, u] = r
        c["head_part"][:, u] = p % parts
    for kind in range(3):
        first, second = seg_bounds(kind)
        starts = first[:-1] + second[:-1]
        c["seg_base"][:, BASE_AT[kind]:BASE_AT[kind] + 8 * len(starts)] = np.repeat(starts, 8)
    return np.concatenate([c[k] for k in CONST], axis=1)




def batches():
    out = []
    for t in range(T):
        out.append((t, None, 0, 1))
        for u in (range(NHEAD) if t == 0 else [NHEAD + t - 1]):
            for k in range(0, CHUNKS[u], BATCH):
                out.append((t, u, k, min(BATCH, CHUNKS[u] - k)))
    return out


def chunks(h):
    return [(c, min(BANK, HWID[h] - c)) for c in range(0, HWID[h], BANK)]


CH = [(h, HOFF[h] + c, w) for h in range(2) for c, w in chunks(h)]
NB = len(chunks(0))
GROUP = [(HT * h + 4 * b, min(HT * h + 4 * b + 4, HT * (h + 1))) for h in range(2) for b in range(NB)]
assert len(chunks(1)) == NB


BATCH_AT = tuple(sum(-(-c // BATCH) for c in CHUNKS[:u]) for u in range(UNITS + 1))
BATCH_N = BATCH_AT[UNITS]
NG, NZ = 4, 3
EARLY = 5
FILL_AFTER = {3: 1, 7: 2, 11: 3, **{T + 4 * q: NHEAD + q - 1 for q in range(1, EARLY + 1)}}
ASSIGN_AT = (5, 9, 13, T + 5, T + 9, T + 13, T + 17)
ASSIGN_AFTER = {n: u for u, n in enumerate(ASSIGN_AT)}
TURN_AFTER = {3: 0, **{n + 2: u + 1 for u, n in enumerate(ASSIGN_AT)}}
L1_TURN_AFTER = {1 + 5 * k // 2: u + 1 for k, u in enumerate(range(len(ASSIGN_AT), UNITS))}
assert max(L1_TURN_AFTER) < 2 * T
MESSAGE_AFTER = {T + 6: 0, T + 11: 1, T + 16: 2}
GATES_AFTER = {T + 7: 0, T + 12: 1, T + 17: 2}
SD_PAIR = [(t, min(t + 2, b)) for a, b in GROUP for t in range(a, b, 2)]
SD_AT = [sum(p[0] < a for p in SD_PAIR) for a, _ in GROUP] + [len(SD_PAIR)]
LAG_AGG, LAG_UP, LAG_SUM, LAG_NORM, LAG_ATT, TAIL = 1, 2, 4, 5, 7, 8
NORM4_AT = (4, 7, 10)


def build(nc, x, adj_rows, adj_cols, head, weights, rows4, consts, out):
    f32, u32, i32, bf16 = mybir.dt.float32, mybir.dt.uint32, mybir.dt.int32, mybir.dt.bfloat16
    ACT = mybir.ActivationFunctionType
    AX = mybir.AxisListType.X
    d_table = nc.dram_tensor("d_table", (NP, D), f32).ap()

    ctx = ExitStack()
    with ctx:
        def sb(name, shape, dt=f32):
            return ctx.enter_context(nc.sbuf_tensor(name, shape, dt))

        def sem(name):
            return ctx.enter_context(nc.semaphore(name))

        xa = sb("xa", [P, T, D])
        xb = sb("xb", [P, T, D])
        xt = sb("xt", [P, NP])
        pt1 = sb("pt1", [P, NP])
        pt2 = sb("pt2", [P, NP])
        hn = sb("hn", [P, T, D])
        sd = sb("sd", [P, T, 2 * D])
        rows = sb("rows", [P, RING, HWID[0]])
        cols = sb("cols", [P, RING, HWID[0]])
        cand = sb("cand", [P, CAND_AT[T]])
        cand_i = sb("cand_i", [P, CAND_AT[T]], u32)
        cand_c = sb("cand_c", [P, 2, WIDEST])
        cand_v = sb("cand_v", [P, 2, WIDEST])
        pos = sb("pos", [P, SLOT_N], u32)
        pos_f = sb("pos_f", [P, SLOT_N])
        vals = sb("vals", [P, SLOT_N])
        col_f = sb("col_f", [P, SLOT_N])
        count = sb("count", [P, UNITS])
        base = sb("base", [P, UNITS])
        end = sb("end", [P, UNITS])
        edge_i = sb("edge_i", [P, 2, 48], i32)
        edge_c = sb("edge_c", [P, 2, 48], i32)
        edge_x = sb("edge_x", [P, 2, 48])
        shift_i = sb("shift_i", [P, 2], i32)
        shift = sb("shift", [P, 2])
        rest = sb("rest", [P, 3, 48])
        onehot = sb("onehot", [P, 2, 2 * P], bf16)
        rec = sb("rec", [P, 2, R_MAX])
        e_val = sb("e_val", [P, CHUNK_N])
        e_col = sb("e_col", [P, CHUNK_N], u32)
        e_row = sb("e_row", [P, CHUNK_N])
        lo = sb("lo", [P, BATCH_N])
        hi = sb("hi", [P, BATCH_N])
        cst = sb("cst", [P, CONST_N])
        wts = sb("wts", [P, WEIGHT_N])
        rowv = sb("rowv", [P, ROWS4, D])
        sums = sb("sums", [P, 3, 2, T])
        head_sg = sb("head_sg", [P, NHEAD])
        recip = sb("recip", [P, 2, T])
        degs = sb("degs", [P, 3, 2, T])
        found = sb("found", [P, UNITS])
        left = sb("left", [P, 4, UNITS])
        bad = sb("bad", [P, 5, UNITS])
        badc = sb("badc", [P, 1])
        flag = sb("flag", [1, 1], i32)
        stats = sb("stats", [P, T, 6])
        mv = sb("mv", [P, T, 2])
        rstd = sb("rstd", [P, 2, T])
        nwi = sb("nwi", [P, T], i32)
        nwg = sb("nwg", [P, T], i32)
        nwt = sb("nwt", [P, 3, T])
        b_rz = sb("b_rz", [P, 2])
        eps = sb("eps", [P, 1])
        att = sb("att", [P, 2 + P])
        src = sb("src", [P, T])
        src2 = sb("src2", [P, T])

        flat = lambda a: a[:, :, :].rearrange("p t d -> p (t d)")
        head_a = flat(hn)[:, 0:HEAD_AT[NHEAD]]
        unread = flat(sd)
        spare = lambda a, b: flat(sd)[:, 3 * HWID[0] + a:3 * HWID[0] + b]
        look = spare(0, 2 * WIDEST).rearrange("p (b w) -> p b w", b=2)
        part = spare(2 * WIDEST, 2 * WIDEST + 288).bitcast(bf16).rearrange("p (b k f) -> p b k f", b=2, f=6)
        assign = spare(2 * WIDEST + 288, 2 * WIDEST + 288 + R_MAX // 3).bitcast(bf16).rearrange(
            "p (b k) -> p b k", b=2)
        counting = spare(2 * WIDEST + 288 + R_MAX // 3, 2 * WIDEST + 336 + R_MAX // 3)
        assert 2 * WIDEST + 336 + R_MAX // 3 <= HWID[0] and HEAD_AT[NHEAD] <= 3 * HWID[0]
        gate = lambda n, w: flat(hn)[:, n * BANK:n * BANK + w]
        ring2 = cols[:, :, :].rearrange("p r w -> p (r w)")
        QW = BATCH * D
        got = lambda b: ring2[:, (b % NG) * QW:(b % NG + 1) * QW]
        zed = lambda b: ring2[:, (NG + b % NZ) * QW:(NG + b % NZ + 1) * QW]
        gel = lambda b: ring2[:, (NG + NZ + b % NZ) * QW:(NG + NZ + b % NZ + 1) * QW]
        dia = lambda b: ring2[:, (NG + 2 * NZ + b % NZ) * QW:(NG + 2 * NZ + b % NZ + 1) * QW]
        assert (NG + 3 * NZ) * QW <= RING * HWID[0] and 2 * NP <= RING * HWID[0]
        hot = lambda b, n: rec[:, b % 2, n * QW:(n + 1) * QW]
        assert R_MAX >= 2 * QW and R_MAX >= HWID[0]
        record = lambda u: rec[:, u % 2, 0:3 * SLOTS[u] * CHUNKS[u]].bitcast(bf16)

        ps = [ctx.enter_context(nc.psum_tensor(f"ps{b}", [P, BANK], f32)) for b in range(8)]

        def C(name, a=0, w=None):
            at = CONST_AT[name] + a
            return cst[:, at:at + (CONST[name] if w is None else w)]

        def W(name, a=0, w=None):
            at = WEIGHT_AT[name] + a
            return wts[:, at:at + (WEIGHT[name] if w is None else w)]

        ident = C("ident")

        s_xin = [sem("s_xin0"), sem("s_xin1")]
        s_const = sem("s_const")
        s_wts = sem("s_wts")
        s_head = sem("s_head")
        s_rows = [sem(f"s_rows{r}") for r in range(RING)]
        s_cols = [sem(f"s_cols{r}") for r in range(RING)]
        s_pe0 = sem("s_pe0")
        s_act0 = sem("s_act0")
        s_max = sem("s_max")
        s_cand = sem("s_cand")
        s_hsg = sem("s_hsg")
        s_ev0 = sem("s_ev0")
        s_deg = sem("s_deg")
        s_p0 = sem("s_p0")
        s_h0 = sem("s_h0")
        s_ex = sem("s_ex")
        s_cnt = sem("s_cnt")
        s_turn = sem("s_turn")
        s_base = sem("s_base")
        s_slots = sem("s_slots")
        s_asg = sem("s_asg")
        s_pool = sem("s_pool")
        s_rec = sem("s_rec")
        s_bad = sem("s_bad")
        s_list = sem("s_list")
        s_mv = [sem(f"s_mv{l}") for l in range(5)]
        s_std = [sem(f"s_std{l}") for l in range(5)]
        s_rs = [sem(f"s_rs{l}") for l in range(5)]
        s_x = [sem(f"s_x{l}") for l in range(5)]
        s_tp = [sem(f"s_tp{l}") for l in range(5)]
        s_xt = [sem(f"s_xt{l}") for l in range(5)]
        s_pe1 = sem("s_pe1")
        s_ev1 = sem("s_ev1")
        s_msgp = sem("s_msgp")
        s_msg = sem("s_msg")
        s_gp = sem("s_gp")
        s_rz = sem("s_rz")
        s_nin = sem("s_nin")
        s_n = sem("s_n")
        s_hc = sem("s_hc")
        s_hp = sem("s_hp")
        s_badp = sem("s_badp")
        s_flag = sem("s_flag")
        s_sdp = sem("s_sdp")
        s_sd = sem("s_sd")
        s_tab = sem("s_tab")
        s_got = [sem(f"s_got{r}") for r in range(NG)]
        s_hotp = sem("s_hotp")
        s_sep = sem("s_sep")
        s_zed = sem("s_zed")
        s_dia = sem("s_dia")
        s_gel = sem("s_gel")
        s_su = sem("s_su")
        s_suc = sem("s_suc")
        s_bat = sem("s_bat")
        s_agg = sem("s_agg")
        s_dtp = sem("s_dtp")
        s_dt = sem("s_dt")
        s_row = [sem(f"s_row{r}") for r in range(2)]
        s_gd = sem("s_gd")
        s_dense = sem("s_dense")
        s_up = sem("s_up")
        s_ug = sem("s_ug")
        s_h2 = sem("s_h2")
        s_att = sem("s_att")
        s_attc = sem("s_attc")
        s_src2 = sem("s_src2")
        s_rel = sem("s_rel")
        s_g = sem("s_g")
        s_t1 = sem("s_t1")
        s_t2 = sem("s_t2")
        s_tsum = sem("s_tsum")
        s_pe3 = sem("s_pe3")
        s_z = sem("s_z")
        s_zp = sem("s_zp")
        s_out = sem("s_out")

        block = ctx.enter_context(nc.Block())
        STEPS = 2 * T
        BAT = batches()
        LASTB = {t: max(i for i, b in enumerate(BAT) if b[0] == t) for t in range(T)}
        gather_no = {}
        for i, (t, u, k, n) in enumerate(BAT):
            if u is not None:
                gather_no[i] = len(gather_no)
        batch_of = {g: i for i, g in gather_no.items()}
        place_sum = [sum(BAT[batch_of[j]][3] for j in range(g % NG, g + 1, NG)) for g in range(len(gather_no))]
        tile_group = {t: i for i, (a, b) in enumerate(GROUP) for t in range(a, b)}

        def half(n):
            return n // T % 2, n % T

        def bank_0(t):
            return t % 7 if t < 14 else NB + (t - 14) % 4

        def sums_read(t):
            a, b = GROUP[tile_group[t]]
            return a + t + (b - a) + 1

        @block.sync
        def _(sp):
            def load(ring, sems, dram, n):
                h, t = half(n)
                sp.dma_start(ring[:, n % RING, 0:HWID[h]],
                             dram[t * P:(t + 1) * P, HOFF[h]:HOFF[h] + HWID[h]]).then_inc(sems[n % RING], 16)

            for n in range(STEPS):
                if n >= RING:
                    m = n - RING
                    sp.wait_ge(s_pe0, m + 1)
                    sp.wait_ge(s_act0, 3 * (m + 1))
                    taken = (m // T) * (T - 1) + m % T
                    if taken:
                        sp.wait_ge(s_cand, taken)
                if n == 0:
                    sp.dma_start(xa[:, 0:2, :], x[:, 0:2, :]).then_inc(s_xin[0], 16)
                load(cols, s_cols, adj_cols, n)
                load(rows, s_rows, adj_rows, n)
                if n == 0:
                    sp.dma_start(head_a, head).then_inc(s_head, 16)
                if n == 1:
                    sp.dma_start(xa[:, 2:T, :], x[:, 2:T, :]).then_inc(s_xin[1], 16)
                    sp.dma_start(cst[:], consts).then_inc(s_const, 16)
                if n == RING:
                    sp.dma_start(wts[:], weights).then_inc(s_wts, 16)
                    sp.dma_start(rowv[:, :, :], rows4.broadcast_to([P, ROWS4, D])).then_inc(s_wts, 16)
            for n in range(STEPS, 2 * STEPS):
                m = n - RING
                if m < STEPS:
                    sp.wait_ge(s_pe0, m + 1)
                    sp.wait_ge(s_act0, 3 * (m + 1))
                else:
                    sp.wait_ge(s_pe1, m + 1 - STEPS)
                load(cols, s_cols, adj_cols, n)
            for n in range(STEPS, STEPS + RING):
                m = n - RING
                sp.wait_ge(s_cand, (m // T) * (T - 1) + m % T)
                sp.wait_ge(s_pe0, m + 1)
                sp.wait_ge(s_act0, 3 * (m + 1))
                load(rows, s_rows, adj_rows, n)
            for i, (a, b) in enumerate(GROUP):
                sp.wait_ge(s_sd, SD_AT[i + 1])
                sp.dma_start(d_table[a * P:b * P, :].rearrange("(t p) d -> p t d", p=P),
                             sd[:, a:b, D:2 * D]).then_inc(s_tab, 16)
            sp.wait_ge(s_flag, 1)
            over = sp.value_load(flag[0:1, 0:1], min_val=0, max_val=1)
            with sp.If(over > 0):
                with sp.Fori(0, N // 2) as g:
                    for r in range(2):
                        sp.wait_ge(s_dense, 2 * g + r + 1)
                        sp.dma_start(ring2[:, r * NP:r * NP + N],
                                     adj_rows[bass.ds(2 * g + r, 1), :].broadcast_to([P, N])).then_inc(s_row[r], 16)
            with sp.Else():
                sp.nop()
            for n in range(STEPS + RING, 2 * STEPS):
                sp.wait_ge(s_t2, n - RING + 1 - STEPS)
                load(rows, s_rows, adj_rows, n)
            full = N // P
            for i, (a, b) in enumerate(GROUP):
                sp.wait_ge(s_x[4], b)
                c = min(b, full)
                sp.dma_start(out[a * P:c * P, :].rearrange("(t p) d -> p t d", p=P), xa[:, a:c, :]).then_inc(s_out, 16)
            sp.dma_start(out[full * P:N, :], xa[0:N - full * P, full, :]).then_inc(s_out, 16)
            sp.wait_ge(s_out, 16 * (len(GROUP) + 1))

        @block.gpsimd
        def _(pool):
            G = nc.gpsimd
            steps = [0]

            def px(ins, wait=True):
                steps[0] += 1
                ins.then_inc(s_pool, 1)
                if wait:
                    pool.wait_ge(s_pool, steps[0])

            def split(u):
                b, n = u % 2, SLOTS[u]
                s = slice(SLOT_AT[u], SLOT_AT[u] + n)
                v1, c1, row, v2, c2, v3 = (part[:, b, 0:n, f] for f in range(6))
                r1, r2, rc = (rest[:, f, 0:n] for f in range(3))
                px(G.tensor_copy(v1, vals[:, s]), False)
                px(G.tensor_copy(c1, col_f[:, s]), False)
                px(G.tensor_scalar(row, C("iota", 0, n), 0.0, C("head_row", u, 1) if u < NHEAD else C("row", 0, 1),
                                   ALU.mult, ALU.add))
                px(G.tensor_tensor(r1, vals[:, s], v1, ALU.subtract), False)
                px(G.tensor_tensor(rc, col_f[:, s], c1, ALU.subtract))
                px(G.tensor_copy(v2, r1), False)
                px(G.tensor_copy(c2, rc))
                px(G.tensor_tensor(r2, r1, v2, ALU.subtract))
                px(G.tensor_copy(v3, r2))

            def records(u):
                b, n, c = u % 2, SLOTS[u], CHUNKS[u]
                pool.wait_ge(s_asg, u + 1)
                G.tensor_tensor(record(u).rearrange("p (k f c) -> p k f c", f=6, c=c),
                                assign[:, b, 0:n * c].rearrange("p (k c) -> p k c", c=c).unsqueeze(2).broadcast_to([P, n, 6, c]),
                                part[:, b, 0:n, :].unsqueeze(3).broadcast_to([P, n, 6, c]), ALU.mult).then_inc(s_rec, 1)

            pool.wait_ge(s_const, 16)
            for u in range(UNITS):
                if u >= 2:
                    pool.wait_ge(s_rec, u - 1)
                pool.wait_ge(s_slots, u + 1)
                split(u)
                if u:
                    records(u - 1)
            records(UNITS - 1)

            pool.wait_ge(s_flag, 1)
            over = pool.value_load(flag[0:1, 0:1], min_val=0, max_val=1)
            with pool.If(over > 0):
                pool.nop()
            with pool.Else():
                pool.wait_ge(s_list, 5 * UNITS)
                pool.wait_ge(s_tab, 16 * len(GROUP))
                for i, (t, u, k, n) in enumerate(BAT):
                    if u is None:
                        continue
                    g = gather_no[i]
                    if g >= NG:
                        pool.wait_ge(s_zed, batch_of[g - NG] + 1)
                    for j in range(n):
                        at = CHUNK_AT[u] + k + j
                        nc.gpsimd.indirect_dma_start(
                            got(g)[:, j * D:(j + 1) * D], None, d_table,
                            bass.IndirectOffsetOnAxis(ap=e_col[:, at:at + 1], axis=0),
                        ).then_inc(s_got[g % NG], 16)

        @block.scalar
        def _(act):
            A = nc.scalar

            def copy_turn(u):
                act.wait_ge(s_turn, u + 1)
                if u:
                    c = CHUNKS[u - 1]
                    s = slice(CHUNK_AT[u - 1], CHUNK_AT[u])
                    A.copy(e_val[:, s], ps[7][:, 0:c]).then_inc(s_list, 1)
                    A.copy(e_col[:, s], ps[7][:, c:2 * c]).then_inc(s_list, 1)
                    A.copy(e_row[:, s], ps[7][:, 2 * c:3 * c]).then_inc(s_list, 1)
                if u < UNITS:
                    q = slice(BATCH_AT[u], BATCH_AT[u + 1])
                    nb = BATCH_AT[u + 1] - BATCH_AT[u]
                    A.copy(base[:, u:u + 1], ps[7][:, 64:65]).then_inc(s_base, 1)
                    A.activation(end[:, u:u + 1], ps[7][:, 64:65], ACT.Identity, bias=count[:, u:u + 1]).then_inc(s_base, 1)
                    act.wait_ge(s_base, 2 * u + 2)
                    A.activation(lo[:, q], C("batch_at", 0, nb), ACT.Identity, bias=base[:, u:u + 1]).then_inc(s_list, 1)
                    A.activation(hi[:, q], C("batch_at", 0, nb), ACT.Identity, bias=end[:, u:u + 1]).then_inc(s_list, 1)

            act.wait_ge(s_head, 16)
            for u in range(NHEAD):
                A.activation(unread[:, HEAD_AT[u]:HEAD_AT[u + 1]], head_a[:, HEAD_AT[u]:HEAD_AT[u + 1]], ACT.Sign,
                             accum_out=head_sg[:, u:u + 1]).then_inc(s_hsg, 1)
            act.wait_ge(s_hsg, NHEAD)
            for n in range(STEPS):
                h, t = half(n)
                for q, (ring, sems, func) in enumerate(((rows, s_rows, ACT.Copy), (rows, s_rows, ACT.Sign),
                                                        (cols, s_cols, ACT.Copy))):
                    if q != 1:
                        act.wait_ge(sems[n % RING], 16 * (n // RING + 1))
                    m = 3 * n + q
                    if m >= 3:
                        act.wait_ge(s_act0, m - 2)
                    A.activation(unread[:, q * HWID[0]:q * HWID[0] + HWID[h]],
                                 ring[:, n % RING, 0:HWID[h]], func,
                                 accum_out=sums[:, q, h, t:t + 1]).then_inc(s_act0, 1)
                if n in TURN_AFTER:
                    copy_turn(TURN_AFTER[n])
                if t == T - 1:
                    act.wait_ge(s_pe0, n + 1)
                    for b, (c, w) in enumerate(chunks(h)):
                        A.copy(pt1[:, HOFF[h] + c:HOFF[h] + c + w], ps[b][:, 0:w]).then_inc(s_ev0, 1)
                        A.copy(pt2[:, HOFF[h] + c:HOFF[h] + c + w], ps[NB + b][:, 0:w]).then_inc(s_ev0, 1)
            act.wait_ge(s_deg, 4)
            for i, (a, b) in enumerate(GROUP):
                act.wait_ge(s_mv[0], 2 * b)
                A.activation(rstd[:, 0, a:b], mv[:, a:b, 1], ACT.Sqrt, bias=eps[:, 0:1]).then_inc(s_std[0], 1)

            def into_xt(l, i, bank):
                a, b = GROUP[i]
                act.wait_ge(s_tp[l], i + 1)
                A.copy(xt[:, a * P:b * P], ps[bank][:, 0:(b - a) * P]).then_inc(s_xt[l], 1)

            def out_of_1(h):
                act.wait_ge(s_pe1, (h + 1) * T)
                for b, (c, w) in enumerate(chunks(h)):
                    A.copy(pt1[:, HOFF[h] + c:HOFF[h] + c + w], ps[NB * h + b][:, 0:w]).then_inc(s_ev1, 1)

            def gru(i):
                h, c, w = CH[i]
                act.wait_ge(s_msgp, i + 1)
                A.activation(pt2[:, c:c + w], ps[2][:, 0:w], ACT.Relu, bias=W("b_msg")).then_inc(s_msg, 1)
                if i:
                    act.wait_ge(s_hc, 4 * i)
                for g in range(2):
                    act.wait_ge(s_gp, 4 * i + (1, 3)[g])
                    A.activation(gate(g, w), ps[g][:, 0:w], ACT.Sigmoid, bias=b_rz[:, g:g + 1]).then_inc(s_rz, 1)
                act.wait_ge(s_nin, 2 * (i + 1))
                A.activation(gate(3, w), gate(2, w), ACT.Tanh, bias=W("b_ih", 2, 1)).then_inc(s_n, 1)

            def s_and_d(i):
                for j in range(SD_AT[i], SD_AT[i + 1]):
                    a, b = SD_PAIR[j]
                    act.wait_ge(s_sdp, j + 1)
                    A.copy(flat(sd)[:, 2 * D * a:2 * D * b], ps[(7, 5)[j % 2]][:, 0:2 * D * (b - a)]).then_inc(s_sd, 1)

            for n in range(STEPS):
                if n == T - 1:
                    out_of_1(0)
                if 0 <= n - T < len(GROUP):
                    into_xt(0, n - T, 6)
                if n in L1_TURN_AFTER:
                    copy_turn(L1_TURN_AFTER[n])
                if n in GATES_AFTER:
                    gru(GATES_AFTER[n])
            out_of_1(1)
            for i in range(NB, 2 * NB):
                gru(i)
                if i > NB:
                    into_xt(1, i - NB - 1, 5)
                    s_and_d(i - NB - 1)
            for i in range(NB - 1, 2 * NB):
                into_xt(1, i, 5)
                s_and_d(i)

            def aggregated(t):
                act.wait_ge(s_bat, LASTB[t] + 1)
                A.copy(pt1[:, t * P:(t + 1) * P], ps[4 + t % 2][:, 0:P]).then_inc(s_agg, 1)

            def update(t):
                act.wait_ge(s_up, t + 1)
                A.activation(hn[:, t, :], ps[6 + t % 2][:, 0:D], ACT.Gelu).then_inc(s_ug, 1)

            def attention(i):
                a, b = GROUP[i]
                h, c, w = CH[i]
                into_xt(3, i, 2)
                act.wait_ge(s_att, 2 + 2 * i)
                A.copy(flat(hn)[:, a * D:b * D], ps[3][:, 0:(b - a) * D]).then_inc(s_attc, 1)
                A.copy(src[:, a:b], ps[2][:, 0:b - a]).then_inc(s_attc, 1)
                act.wait_ge(s_att, 3 + 2 * i)
                A.copy(pt1[:, c:c + w], ps[2][:, 0:w]).then_inc(s_attc, 1)

            act.wait_ge(s_flag, 1)
            over = act.value_load(flag[0:1, 0:1], min_val=0, max_val=1)
            act.wait_ge(s_att, 1)
            A.copy(att[:, 0:2], ps[3][:, 0:2]).then_inc(s_attc, 1)
            act.wait_ge(s_attc, 1)
            A.activation(att[:, 2:2 + P], C("ones"), ACT.Identity, scale=att[:, 1:2]).then_inc(s_attc, 1)
            with act.If(over > 0):
                for i, (h, c, w) in enumerate(CH):
                    act.wait_ge(s_dtp, i + 1)
                    A.activation(pt1[:, c:c + w], ps[i % 2][:, 0:w], ACT.Identity).then_inc(s_dt, 1)
                    A.activation(pt2[:, c:c + w], ps[2 + i % 2][:, 0:w], ACT.Identity,
                                 bias=W("msg_b")).then_inc(s_dt, 1)
                act.wait_ge(s_dt, 2 * len(CH))
                with act.Fori(0, N // 2) as g:
                    for r in range(2):
                        act.wait_ge(s_dense, 2 * g + r + 1)
                        A.activation(flat(hn)[:, 0:N], pt1[:, 0:N], ACT.Gelu,
                                     bias=pt2[:, bass.ds(2 * g + r, 1)]).then_inc(s_gd, 1)
                for i, (a, b) in enumerate(GROUP):
                    for t in range(a, b):
                        update(t)
                    attention(i)
            with act.Else():
                for u in range(NHEAD):
                    act.wait_ge(s_su, u + 1)
                    A.copy(pt2[:, u * D:(u + 1) * D], ps[u][:, 0:D]).then_inc(s_suc, 1)
                for i in range(len(BAT) + TAIL):
                    if i < len(BAT):
                        n = BAT[i][3]
                        act.wait_ge(s_zed, i + 1)
                        if i >= NZ:
                            act.wait_ge(s_bat, i - NZ + 1)
                        A.activation(gel(i)[:, 0:n * D], zed(i)[:, 0:n * D], ACT.Gelu).then_inc(s_gel, 1)
                    for t in range(T):
                        if LASTB[t] + LAG_AGG == i:
                            aggregated(t)
                    for t in range(T):
                        if LASTB[t] + LAG_UP == i:
                            update(t)
                    for g, (a, b) in enumerate(GROUP):
                        if LASTB[b - 1] + LAG_ATT == i:
                            attention(g)
            A.mul(src2[:, :], src[:, :], 0.2).then_inc(s_src2, 1)
            act.wait_ge(s_src2, 1)
            for n in range(STEPS):
                h, t = half(n)
                g = rec[:, n % 2, 0:HWID[h]]
                if n >= 2:
                    act.wait_ge(s_t1, n - 1)
                A.activation(g, pt1[:, HOFF[h]:HOFF[h] + HWID[h]], ACT.Relu, bias=src[:, t:t + 1]).then_inc(s_rel, 1)
                act.wait_ge(s_rel, n + 1)
                A.activation(g, g, ACT.Exp, bias=src2[:, t:t + 1], scale=0.8).then_inc(s_g, 1)

        @block.vector
        def _(dve):
            V = nc.vector
            V.memset(pt1[:, N:NP], 0.0).then_inc(s_deg, 1)
            V.memset(pt2[:, N:NP], 0.0).then_inc(s_deg, 1)
            V.memset(left[:, :, :], 0.0).then_inc(s_deg, 1)
            V.memset(eps[:, :], EPS).then_inc(s_deg, 1)
            dve.wait_ge(s_deg, 4)
            dve.wait_ge(s_head, 16)
            dve.wait_ge(s_hsg, NHEAD)
            ex = [0]

            def sx(ins, wait=True):
                ex[0] += 1
                ins.then_inc(s_ex, 1)
                if wait:
                    dve.wait_ge(s_ex, ex[0])

            def counted(u):
                s = slice(SLOT_AT[u], SLOT_AT[u] + SLOTS[u])
                V.tensor_scalar(counting[:, 0:SLOTS[u]], vals[:, s], 0.0, 0.0, ALU.is_gt, ALU.add,
                                accum_out=count[:, u:u + 1]).then_inc(s_cnt, 1)

            def fill_head(u):
                a = head_a[:, HEAD_AT[u]:HEAD_AT[u + 1]]
                for r in range(ROUNDS[u]):
                    at = SLOT_AT[u] + 8 * r
                    sx(V.max(vals[:, at:at + 8], a))
                    sx(V.max_index(pos[:, at:at + 8], vals[:, at:at + 8], a))
                    sx(V.match_replace(a, vals[:, at:at + 8], a, 0.0))
                s = slice(SLOT_AT[u], SLOT_AT[u + 1])
                sx(V.reduce_max(left[:, 0, u:u + 1], a, AX), False)
                dve.wait_ge(s_const, 16)
                sx(V.tensor_scalar(col_f[:, s], pos[:, s], float(HEAD[u][2]), C("head_part", u, 1), ALU.mult, ALU.add), False)
                if SLOTS[u] % 8:
                    sx(V.reduce_max(left[:, 2, u:u + 1], vals[:, SLOT_AT[u] + SLOTS[u]:SLOT_AT[u + 1]], AX), False)
                sx(V.tensor_scalar(counting[:, 0:8 * ROUNDS[u]], vals[:, s], 0.0, 0.0, ALU.is_gt, ALU.add,
                                   accum_out=found[:, u:u + 1]))
                counted(u)
                dve.wait_ge(s_cnt, u + 1)
                sx(V.scalar_tensor_tensor(vals[:, s], col_f[:, s], C("head_row", u, 1), vals[:, s], ALU.not_equal, ALU.mult))
                V.tensor_scalar(col_f[:, s], col_f[:, s], float(N - 1), None, ALU.min).then_inc(s_slots, 1)

            def fill_tile(u):
                t = u - NHEAD + 1
                kind, w, b = seg_kind(t), cand_width(t), t % 2
                v = cand[:, CAND_AT[t]:CAND_AT[t] + w]
                cc, cv = cand_c[:, b, 0:w], cand_v[:, b, 0:w]
                sx(V.tensor_tensor(cc, cand_i[:, CAND_AT[t]:CAND_AT[t] + w], C("seg_base", BASE_AT[kind], w), ALU.add), False)
                sx(V.tensor_scalar(cv, v, 0.0, 0.0, ALU.is_gt, ALU.add, accum_out=found[:, u:u + 1]), False)
                sx(V.reduce_max(left[:, 1, u:u + 1], v.rearrange("p (s e) -> p s e", e=8)[:, :, 7], AX))
                sx(V.scalar_tensor_tensor(cv, cc, C("row", t, 1), v, ALU.not_equal, ALU.mult))
                s0 = SLOT_AT[u]
                for r in range(ROUNDS[u]):
                    at = s0 + 8 * r
                    sx(V.max(vals[:, at:at + 8], cv))
                    sx(V.max_index(pos[:, at:at + 8], vals[:, at:at + 8], cv), False)
                    sx(V.match_replace(cv, vals[:, at:at + 8], cv, 0.0))
                sx(V.tensor_copy(pos_f[:, s0:SLOT_AT[u + 1]], pos[:, s0:SLOT_AT[u + 1]]), False)
                sx(V.reduce_max(left[:, 0, u:u + 1], cv, AX), False)
                if SLOTS[u] % 8:
                    sx(V.reduce_max(left[:, 2, u:u + 1], vals[:, s0 + SLOTS[u]:SLOT_AT[u + 1]], AX), False)
                counted(u)
                dve.wait_ge(s_cnt, u + 1)
                for k in range(SLOTS[u]):
                    if k >= 2:
                        dve.wait_ge(s_ex, ex[0] - 1)
                    ins = V.scalar_tensor_tensor(look[:, k % 2, 0:w], C("iota", 0, w), pos_f[:, s0 + k:s0 + k + 1], cc,
                                                 ALU.is_equal, ALU.mult, accum_out=col_f[:, s0 + k:s0 + k + 1])
                    if k < SLOTS[u] - 1:
                        sx(ins, False)
                ins.then_inc(s_slots, 1)

            def assigned(u):
                b, n, c = u % 2, SLOTS[u], CHUNKS[u]
                s = slice(SLOT_AT[u], SLOT_AT[u] + n)
                ei, ec, ex_ = edge_i[:, b, 0:n], edge_c[:, b, 0:n], edge_x[:, b, 0:n]
                dve.wait_ge(s_base, 2 * u + 2)
                sx(V.tensor_scalar(ei, C("iota", 0, n), base[:, u:u + 1], None, ALU.add), False)
                dve.wait_ge(s_slots, u + 1)
                sx(V.tensor_scalar(ex_, vals[:, s], 0.0, 4096.0, ALU.is_le, ALU.mult))
                sx(V.tensor_scalar(left[:, 3, u:u + 1], end[:, u:u + 1], float(-P * c), 0.0, ALU.add, ALU.max), False)
                sx(V.tensor_scalar(shift_i[:, b:b + 1], ei[:, 0:1], P - 1, None, ALU.bitwise_and), False)
                sx(V.tensor_scalar(ec, ei, 7, None, ALU.arith_shift_right))
                sx(V.tensor_copy(shift[:, b:b + 1], shift_i[:, b:b + 1]), False)
                sx(V.tensor_tensor(ex_, ex_, ec, ALU.add))
                sx(V.tensor_scalar(onehot[:, b, :], C("twice"), shift[:, b:b + 1], None, ALU.is_equal), False)
                V.tensor_tensor(assign[:, b, 0:n * c].rearrange("p (k c) -> p k c", c=c),
                                C("iota", 0, c).unsqueeze(1).broadcast_to([P, n, c]),
                                ex_.unsqueeze(2).broadcast_to([P, n, c]), ALU.is_equal).then_inc(s_asg, 1)

            fill_head(0)

            nm = 0
            for n in range(STEPS):
                h, t = half(n)
                if t:
                    dve.wait_ge(s_rows[n % RING], 16 * (n // RING + 1))
                    kind = seg_kind(t)
                    bounds = seg_bounds(kind)[h]
                    at = CAND_AT[t] + 8 * (SEG_KINDS[kind][0] if h else 0)
                    parts = [(at + 8 * k, rows[:, n % RING, bounds[k] - HOFF[h]:bounds[k + 1] - HOFF[h]])
                             for k in range(len(bounds) - 1)]
                    for c, a in parts:
                        V.max(cand[:, c:c + 8], a).then_inc(s_max, 1)
                    nm += len(parts)
                    dve.wait_ge(s_max, nm)
                    for c, a in parts:
                        ins = V.max_index(cand_i[:, c:c + 8], cand[:, c:c + 8], a)
                    ins.then_inc(s_cand, 1)
                if n in FILL_AFTER:
                    u = FILL_AFTER[n]
                    if u < NHEAD:
                        fill_head(u)
                    else:
                        dve.wait_ge(s_cand, T - 1 + t)
                        fill_tile(u)
                if n in ASSIGN_AFTER:
                    assigned(ASSIGN_AFTER[n])

            dg = [4]

            def dx(ins):
                dg[0] += 1
                ins.then_inc(s_deg, 1)
                dve.wait_ge(s_deg, dg[0])

            dve.wait_ge(s_act0, 3 * STEPS)
            dve.wait_ge(s_wts, 32)
            dx(V.tensor_tensor(degs[:, 0, :, :], sums[:, 0::2, 0, :], sums[:, 0::2, 1, :], ALU.add))
            dx(V.tensor_scalar(degs[:, 1, :, :], degs[:, 0, :, :], 0.0, None, ALU.is_gt))
            dx(V.tensor_tensor(degs[:, 0, :, :], degs[:, 0, :, :], degs[:, 1, :, :], ALU.mult))
            dx(V.tensor_scalar(degs[:, 2, :, :], degs[:, 1, :, :], -1.0, 1.0, ALU.mult, ALU.add))
            dx(V.tensor_tensor(b_rz[:, :], W("b_ih", 0, 2), W("b_hh", 0, 2), ALU.add))
            dx(V.tensor_tensor(degs[:, 0, :, :], degs[:, 0, :, :], degs[:, 2, :, :], ALU.add))
            dx(V.reciprocal(recip[:, :, :], degs[:, 0, :, :]))

            def moments(l, i, h_tile):
                a, b = GROUP[i]
                for t in range(a, b):
                    V.bn_stats(stats[:, t, :], h_tile(t)).then_inc(s_mv[l], 1)
                dve.wait_ge(s_mv[l], a + b)
                for t in range(a, b):
                    V.bn_aggr(mv[:, t, :], stats[:, t, :]).then_inc(s_mv[l], 1)
                dve.wait_ge(s_mv[l], 2 * b)

            rsn = [0] * 5

            def rx(l, ins):
                rsn[l] += 1
                ins.then_inc(s_rs[l], 1)
                dve.wait_ge(s_rs[l], rsn[l])

            def inverse(l, i):
                s = slice(*GROUP[i])
                v, y, q = nwt[:, 0, s], rstd[:, 1, s], nwt[:, 1, s]
                rx(l, V.tensor_scalar(v, mv[:, s, 1], EPS, None, ALU.add))
                rx(l, V.tensor_scalar(nwi[:, s], v.bitcast(i32), 1, None, ALU.arith_shift_right))
                rx(l, V.tensor_scalar(y.bitcast(i32), nwi[:, s], -1.0, float(0x5F3759DF), ALU.mult, ALU.add))
                for _ in range(3):
                    rx(l, V.tensor_tensor(q, y, y, ALU.mult))
                    rx(l, V.scalar_tensor_tensor(q, q, -0.5, v, ALU.mult, ALU.mult))
                    rx(l, V.scalar_tensor_tensor(y, q, 1.5, y, ALU.add, ALU.mult))

            def normalised(l, i, h_tile, to):
                for t in range(*GROUP[i]):
                    V.tensor_scalar(to(t), h_tile(t), mv[:, t, 0:1], rstd[:, 1, t:t + 1],
                                    ALU.subtract, ALU.mult).then_inc(s_x[l], 1)

            tile = lambda a: (lambda t: a[:, t, :])

            def close0(i):
                dve.wait_ge(s_std[0], i + 1)
                s = slice(*GROUP[i])
                rx(0, V.reciprocal(rstd[:, 1, s], rstd[:, 0, s]))
                normalised(0, i, tile(hn), tile(xb))

            for i, (a, b) in enumerate(GROUP):
                for t in range(a, b):
                    dve.wait_ge(s_p0, t + 1)
                    V.scalar_tensor_tensor(hn[:, t, :], ps[bank_0(t)][:, 0:D], recip[:, 0, t:t + 1], xa[:, t, :],
                                           ALU.mult, ALU.add).then_inc(s_h0, 1)
                dve.wait_ge(s_h0, a + b)
                for t in range(a, b):
                    V.scalar_tensor_tensor(hn[:, t, :], ps[bank_0(t)][:, D:2 * D], recip[:, 1, t:t + 1], hn[:, t, :],
                                           ALU.mult, ALU.add).then_inc(s_h0, 1)
                dve.wait_ge(s_h0, 2 * b)
                moments(0, i, tile(hn))
                if i:
                    close0(i - 1)
            close0(len(GROUP) - 1)

            def gru(i):
                h, c, w = CH[i]
                r, z, a, m, o = (gate(k, w) for k in range(5))
                dve.wait_ge(s_rz, 2 * i + 1)
                dve.wait_ge(s_gp, 4 * i + 2)
                V.scalar_tensor_tensor(a, ps[6][:, 0:w], W("b_hh", 2, 1), r, ALU.add, ALU.mult).then_inc(s_nin, 1)
                dve.wait_ge(s_nin, 2 * i + 1)
                dve.wait_ge(s_gp, 4 * i + 4)
                V.tensor_tensor(a, a, ps[2][:, 0:w], ALU.add).then_inc(s_nin, 1)
                dve.wait_ge(s_rz, 2 * i + 2)
                dve.wait_ge(s_n, i + 1)
                V.tensor_tensor(o, xt[:, c:c + w], m, ALU.subtract).then_inc(s_hc, 1)
                dve.wait_ge(s_hc, 4 * i + 1)
                V.tensor_tensor(o, z, o, ALU.mult).then_inc(s_hc, 1)
                dve.wait_ge(s_hc, 4 * i + 2)
                V.tensor_tensor(o, m, o, ALU.add).then_inc(s_hc, 1)
                dve.wait_ge(s_hc, 4 * i + 3)
                V.tensor_tensor(pt1[:, c:c + w], xt[:, c:c + w], o, ALU.add).then_inc(s_hc, 1)

            def norm1(i):
                a, b = GROUP[i]
                in_bank = lambda t: ps[3 + i % 2][:, (t - a) * D:(t - a + 1) * D]
                dve.wait_ge(s_hp, i + 1)
                moments(1, i, in_bank)
                inverse(1, i)
                normalised(1, i, in_bank, tile(xa))

            dve.wait_ge(s_cand, 2 * (T - 1))
            for n in range(STEPS):
                if n in L1_TURN_AFTER:
                    u = L1_TURN_AFTER[n]
                    if NHEAD + EARLY <= u < UNITS:
                        fill_tile(u)
                    assigned(u - 1)
                if n in GATES_AFTER:
                    gru(GATES_AFTER[n])

            dve.wait_ge(s_asg, UNITS)
            sx(V.tensor_tensor(degs[:, 0, 0, :], sums[:, 1, 0, :], sums[:, 1, 1, :], ALU.add))
            sx(V.tensor_tensor(bad[:, 0, 0:NHEAD], found[:, 0:NHEAD], head_sg[:, :], ALU.not_equal), False)
            sx(V.tensor_tensor(bad[:, 0, NHEAD:UNITS], found[:, NHEAD:UNITS], degs[:, 0, 0, 1:T], ALU.not_equal), False)
            sx(V.tensor_scalar(bad[:, 1:5, :], left[:, :, :], 0.0, None, ALU.not_equal))
            V.tensor_reduce(badc[:, :], bad[:, :, :], mybir.AxisListType.XY, ALU.add).then_inc(s_bad, 1)
            for i in range(NB, 2 * NB):
                gru(i)
                if i == NB:
                    dve.wait_ge(s_badp, 1)
                    V.tensor_scalar(flag[0:1, 0:1], ps[7][0:1, 255:256], 0.0, None, ALU.not_equal).then_inc(s_flag, 1)
                norm1(i - NB)
            for i in range(NB, 2 * NB):
                norm1(i)

            h2 = [0]

            def hx(ins, wait=True):
                h2[0] += 1
                ins.then_inc(s_h2, 1)
                if wait:
                    dve.wait_ge(s_h2, h2[0])

            def update(t):
                dve.wait_ge(s_ug, t + 1)
                hx(V.tensor_tensor(hn[:, t, :], hn[:, t, :], xa[:, t, :], ALU.add), False)

            def norm23(i):
                a, b = GROUP[i]
                g = hn[:, a:b, :]
                on_tiles = lambda r: rowv[:, r:r + 1, :].broadcast_to([P, b - a, D])
                dve.wait_ge(s_h2, h2[0])
                moments(2, i, tile(hn))
                inverse(2, i)
                normalised(2, i, tile(hn), tile(hn))
                dve.wait_ge(s_x[2], b)
                hx(V.tensor_tensor(g, g, on_tiles(2), ALU.mult))
                hx(V.tensor_tensor(g, g, on_tiles(3), ALU.add))
                hx(V.tensor_tensor(g, g, xa[:, a:b, :], ALU.add))
                moments(3, i, tile(hn))
                inverse(3, i)
                normalised(3, i, tile(hn), tile(xb))

            dve.wait_ge(s_flag, 1)
            over = dve.value_load(flag[0:1, 0:1], min_val=0, max_val=1)
            dve.wait_ge(s_sd, len(SD_PAIR))
            with dve.If(over > 0):
                V.memset(badc[:, :], 0.0).then_inc(s_dense, 1)
                with dve.Fori(0, N // 2) as g:
                    for r in range(2):
                        dve.wait_ge(s_row[r], 16 * g + 16)
                        dve.wait_ge(s_gd, 2 * g + r + 1)
                        V.scalar_tensor_tensor(flat(hn)[:, 0:N], flat(hn)[:, 0:N], 1.0, ring2[:, r * NP:r * NP + N],
                                               ALU.mult, ALU.mult,
                                               accum_out=flat(xb)[:, bass.ds(2 * g + r, 1)]).then_inc(s_dense, 1)
                dve.wait_ge(s_dense, N + 1)
                V.tensor_copy(pt1[:, 0:N], flat(xb)[:, 0:N]).then_inc(s_agg, T)
                dve.wait_ge(s_agg, T)
                for i, (a, b) in enumerate(GROUP):
                    for t in range(a, b):
                        update(t)
                    norm23(i)
            with dve.Else():
                h2[0] = 0
                rsn[2] = rsn[3] = 0

                def one_hot(i):
                    t, u, k, n = BAT[i]
                    g, w = gather_no[i], n * P
                    q = BATCH_AT[u] + k // BATCH
                    if g >= 2:
                        dve.wait_ge(s_sep, g - 1)
                    V.tensor_scalar(hot(g, 1)[:, 0:w], C("iota", 0, w), lo[:, q:q + 1], None, ALU.is_ge).then_inc(s_hotp, 1)
                    dve.wait_ge(s_hotp, 2 * g + 1)
                    V.scalar_tensor_tensor(hot(g, 0)[:, 0:w], C("iota", 0, w), hi[:, q:q + 1], hot(g, 1)[:, 0:w],
                                           ALU.is_lt, ALU.mult).then_inc(s_hotp, 1)

                one_hot(batch_of[0])
                for i in range(len(BAT) + TAIL):
                    if i < len(BAT):
                        t, u, k, n = BAT[i]
                        if u is not None and gather_no[i] + 1 < len(gather_no):
                            one_hot(batch_of[gather_no[i] + 1])
                        if i >= NZ:
                            dve.wait_ge(s_bat, i - NZ + 1)
                        for j in range(n):
                            if u is None:
                                ins = V.tensor_scalar(dia(i)[:, 0:P], ident, W("diag", t, 1), None, ALU.mult)
                            else:
                                at = CHUNK_AT[u] + k + j
                                ins = V.tensor_scalar(dia(i)[:, j * P:(j + 1) * P], C("iota", 0, P), e_row[:, at:at + 1],
                                                      e_val[:, at:at + 1], ALU.is_equal, ALU.mult)
                        ins.then_inc(s_dia, 1)
                        if i >= NZ:
                            dve.wait_ge(s_gel, i - NZ + 1)
                        if u is None:
                            V.tensor_tensor(zed(i)[:, 0:D], sd[:, t, 0:D], sd[:, t, D:2 * D], ALU.add).then_inc(s_zed, 1)
                        else:
                            g = gather_no[i]
                            dve.wait_ge(s_got[g % NG], 16 * place_sum[g])
                            dve.wait_ge(s_sep, g + 1)
                            V.tensor_tensor(zed(i)[:, 0:n * D], got(g)[:, 0:n * D], ps[g % 2][:, 0:n * D],
                                            ALU.add).then_inc(s_zed, 1)
                    for t in range(T):
                        if LASTB[t] + LAG_SUM == i:
                            update(t)
                    for g, (a, b) in enumerate(GROUP):
                        if LASTB[b - 1] + LAG_NORM == i:
                            norm23(g)

            def quotient(i):
                h, c, w = CH[i]
                b = i % NB
                V.reciprocal(pt1[:, c:c + w], ps[NB + b][:, 0:w]).then_inc(s_z, 1)
                dve.wait_ge(s_z, 3 * i + 1)
                V.tensor_tensor(pt1[:, c:c + w], ps[b][:, 0:w], pt1[:, c:c + w], ALU.mult).then_inc(s_z, 1)
                dve.wait_ge(s_z, 3 * i + 2)
                V.tensor_tensor(pt1[:, c:c + w], pt1[:, c:c + w], xt[:, c:c + w], ALU.add).then_inc(s_z, 1)

            def norm4(i):
                a, b = GROUP[i]
                in_bank = lambda t: ps[6 + i % 2][:, (t - a) * D:(t - a + 1) * D]
                dve.wait_ge(s_zp, i + 1)
                moments(4, i, in_bank)
                inverse(4, i)
                normalised(4, i, in_bank, tile(xa))

            dve.wait_ge(s_attc, 2 + 3 * len(GROUP))
            for n in range(STEPS):
                h, t = half(n)
                w = HWID[h]
                g, t1, t2 = rec[:, n % 2, 0:w], cols[:, n % 2, 0:w], cols[:, 2 + n % 2, 0:w]
                pair = pt2[:, n // 2 % 2 * HWID[0]:n // 2 % 2 * HWID[0] + w]
                a = rows[:, (n + STEPS) % RING, 0:w]
                dve.wait_ge(s_rows[(n + STEPS) % RING], 16 * ((n + STEPS) // RING + 1))
                dve.wait_ge(s_g, n + 1)
                if n >= 2:
                    dve.wait_ge(s_pe3, n - 1)
                    dve.wait_ge(s_tsum, n // 2)
                V.tensor_tensor(t1, a, g, ALU.mult).then_inc(s_t1, 1)
                dve.wait_ge(s_t1, n + 1)
                V.tensor_tensor(t2, a, t1, ALU.mult).then_inc(s_t2, 1)
                if t % 2:
                    if n >= 4:
                        dve.wait_ge(s_pe3, n - 3)
                    V.tensor_tensor(pair, cols[:, 0, 0:w], t1, ALU.add).then_inc(s_tsum, 1)
                if t == T - 1:
                    dve.wait_ge(s_pe3, T * (h + 1))
                    for i in range(NB * h, NB * (h + 1)):
                        quotient(i)
                for i in range(NB):
                    if n == T + NORM4_AT[i]:
                        norm4(i)
            for i in range(NB, 2 * NB):
                norm4(i)

        @block.tensor
        def _(pe):
            mm = nc.tensor.matmul

            def back(l, i, of, bank, done):
                a, b = GROUP[i]
                for t in range(a, b):
                    last = nc.tensor.transpose(ps[bank][:, (t - a) * P:(t - a + 1) * P], of(t), ident)
                last.then_inc(done, 1)

            def turn(u):
                if u:
                    pe.wait_ge(s_base, 2 * u)
                    pe.wait_ge(s_rec, u)
                    n, c = SLOTS[u - 1], CHUNKS[u - 1]
                    for k in range(n):
                        r = record(u - 1)[:, 6 * c * k:6 * c * (k + 1)]
                        move = onehot[:, (u - 1) % 2, P - k:2 * P - k]
                        mm(ps[7][:, 0:3 * c], move, r[:, 0:3 * c], start=(k == 0), stop=False)
                        mm(ps[7][:, 0:2 * c], move, r[:, 3 * c:5 * c], start=False, stop=False)
                        last = mm(ps[7][:, 0:c], move, r[:, 5 * c:6 * c], start=False, stop=(k == n - 1))
                if u < UNITS:
                    pe.wait_ge(s_cnt, u + 1)
                    last = mm(ps[7][:, 64:65], C("before"), count[:, u:u + 1], start=True, stop=True)
                last.then_inc(s_turn, 1)

            for n in range(STEPS):
                h, t = half(n)
                pe.wait_ge(s_xin[n > 1], 16)
                pe.wait_ge(s_cols[n % RING], 16 * (n // RING + 1))
                if n == T:
                    pe.wait_ge(s_ev0, 2 * NB)
                for ring, sems, b0 in ((cols, s_cols, 0), (rows, s_rows, NB)):
                    pe.wait_ge(sems[n % RING], 16 * (n // RING + 1))
                    for b, (c, w) in enumerate(chunks(h)):
                        last = mm(ps[b0 + b][:, 0:w], xa[:, t, :], ring[:, n % RING, c:c + w],
                                  start=(t == 0), stop=(t == T - 1))
                last.then_inc(s_pe0, 1)
                if n == min(TURN_AFTER):
                    pe.wait_ge(s_const, 16)
                if n in TURN_AFTER:
                    turn(TURN_AFTER[n])
            pe.wait_ge(s_ev0, 4 * NB)
            pe.wait_ge(s_deg, 2)
            pe.wait_ge(s_wts, 32)
            for t in range(T):
                before = [q for q in range(t) if bank_0(q) == bank_0(t)]
                if before:
                    pe.wait_ge(s_h0, sums_read(before[-1]))
                s = slice(t * P, (t + 1) * P)
                mm(ps[bank_0(t)][:, 0:D], pt1[:, s], W("w_in"), start=True, stop=True)
                mm(ps[bank_0(t)][:, D:2 * D], pt2[:, s], W("w_out"), start=True, stop=True).then_inc(s_p0, 1)

            def message(i):
                h, c, w = CH[i]
                pe.wait_ge(s_ev1, (h + 1) * NB)
                if i:
                    pe.wait_ge(s_nin, 2 * i)
                mm(ps[2][:, 0:w], W("w_msg_t"), pt1[:, c:c + w], start=True, stop=True).then_inc(s_msgp, 1)

            def gates(i):
                h, c, w = CH[i]
                pe.wait_ge(s_xt[0], len(GROUP))
                pe.wait_ge(s_msg, i + 1)
                if i:
                    pe.wait_ge(s_rz, 2 * i)
                ih = lambda g: (W("w_ih_t", g * D, D), pt2[:, c:c + w])
                hh = lambda g: (W("w_hh_t", g * D, D), xt[:, c:c + w])
                mm(ps[0][:, 0:w], *ih(0), start=True, stop=False)
                mm(ps[0][:, 0:w], *hh(0), start=False, stop=True).then_inc(s_gp, 1)
                mm(ps[6][:, 0:w], *hh(2), start=True, stop=True).then_inc(s_gp, 1)
                mm(ps[1][:, 0:w], *ih(1), start=True, stop=False)
                mm(ps[1][:, 0:w], *hh(1), start=False, stop=True).then_inc(s_gp, 1)
                mm(ps[2][:, 0:w], *ih(2), start=True, stop=True).then_inc(s_gp, 1)

            for n in range(STEPS):
                h, t = half(n)
                m = n + STEPS
                pe.wait_ge(s_cols[m % RING], 16 * (m // RING + 1))
                pe.wait_ge(s_x[0], t + 1)
                if n in (0, T):
                    pe.wait_ge(s_h0, max(sums_read(q) for q in range(T) if n or bank_0(q) < NB))
                for b, (c, w) in enumerate(chunks(h)):
                    last = mm(ps[NB * h + b][:, 0:w], xb[:, t, :], cols[:, m % RING, c:c + w],
                              start=(t == 0), stop=(t == T - 1))
                last.then_inc(s_pe1, 1)
                if h == 1 and t < len(GROUP):
                    if t:
                        pe.wait_ge(s_xt[0], t)
                    back(0, t, lambda q: xb[:, q, :], 6, s_tp[0])
                if n in L1_TURN_AFTER:
                    turn(L1_TURN_AFTER[n])
                if n in MESSAGE_AFTER:
                    message(MESSAGE_AFTER[n])
                if n in GATES_AFTER:
                    gates(GATES_AFTER[n])
            pe.wait_ge(s_list, 5 * UNITS)
            pe.wait_ge(s_bad, 1)
            mm(ps[7][0:1, 255:256], badc[:, 0:1], C("ones", 0, 1), start=True, stop=True).then_inc(s_badp, 1)

            def new_state(i):
                pe.wait_ge(s_hc, 4 * (i + 1))
                if i >= 2:
                    pe.wait_ge(s_x[1], GROUP[i - 2][1])
                else:
                    pe.wait_ge(s_ev1, 2 * NB)
                back(1, i, lambda t: pt1[:, t * P:(t + 1) * P], 3 + i % 2, s_hp)

            def s_and_d(i):
                pe.wait_ge(s_x[1], GROUP[i][1])
                if i:
                    pe.wait_ge(s_sd, SD_AT[i])
                back(1, i, lambda t: xa[:, t, :], 5, s_tp[1])
                pe.wait_ge(s_xt[1], i + 1)
                for j in range(SD_AT[i], SD_AT[i + 1]):
                    a, b = SD_PAIR[j]
                    bank = ps[(7, 5)[j % 2]]
                    if j >= 2:
                        pe.wait_ge(s_sd, j - 1)
                    for t in range(a, b):
                        o = 2 * D * (t - a)
                        mm(bank[:, o:o + 2 * D], xt[:, t * P:(t + 1) * P], W("w_sd"), start=True, stop=False)
                        last = mm(bank[:, o:o + D], C("ones")[0:1, :], rowv[0:1, 0, :], start=False, stop=True)
                    last.then_inc(s_sdp, 1)

            for i in range(NB, 2 * NB):
                message(i)
                new_state(i - NB)
                gates(i)
                if i > NB:
                    s_and_d(i - NB - 1)
                else:
                    pe.wait_ge(s_flag, 1)
            for i in range(NB, 2 * NB):
                new_state(i)
                s_and_d(i - 1)
            s_and_d(2 * NB - 1)

            def update(t):
                s = slice(t * P, (t + 1) * P)
                pe.wait_ge(s_agg, t + 1)
                if t >= 2:
                    pe.wait_ge(s_ug, t - 1)
                bank = ps[6 + t % 2]
                mm(bank[:, 0:D], xt[:, s], W("upd_x"), start=True, stop=False)
                mm(bank[:, 0:D], pt1[:, s], W("upd_a"), start=False, stop=False)
                mm(bank[:, 0:D], C("ones")[0:1, :], rowv[0:1, 1, :], start=False, stop=True).then_inc(s_up, 1)

            def attention(i):
                a, b = GROUP[i]
                h, c, w = CH[i]
                pe.wait_ge(s_x[3], b)
                pe.wait_ge(s_attc, 2 + 3 * i)
                back(3, i, lambda t: xb[:, t, :], 2, s_tp[3])
                pe.wait_ge(s_xt[3], i + 1)
                for t in range(a, b):
                    o = (t - a) * D
                    mm(ps[3][:, o:o + D], xt[:, t * P:(t + 1) * P], W("w3_t"), start=True, stop=True)
                    last = mm(ps[2][:, t - a:t - a + 1], xt[:, t * P:(t + 1) * P], att[:, 0:1], start=True, stop=True)
                last.then_inc(s_att, 1)
                pe.wait_ge(s_attc, 4 + 3 * i)
                mm(ps[2][:, 0:w], att[:, 2:2 + P], xt[:, c:c + w], start=True, stop=True).then_inc(s_att, 1)

            pe.wait_ge(s_flag, 1)
            over = pe.value_load(flag[0:1, 0:1], min_val=0, max_val=1)
            pe.wait_ge(s_sd, len(SD_PAIR))
            pe.wait_ge(s_x[1], T)
            mm(ps[3][:, 0:2], W("w3"), W("att_src", 0, 2), start=True, stop=True).then_inc(s_att, 1)
            pe.wait_ge(s_attc, 2)
            with pe.If(over > 0):
                for i, (h, c, w) in enumerate(CH):
                    if i >= 2:
                        pe.wait_ge(s_dt, 2 * (i - 1))
                    mm(ps[i % 2][:, 0:w], W("w_sd", D, D), xt[:, c:c + w], start=True, stop=True)
                    mm(ps[2 + i % 2][:, 0:w], W("w_sd", 0, D), xt[:, c:c + w], start=True, stop=True).then_inc(s_dtp, 1)
                for i, (a, b) in enumerate(GROUP):
                    for t in range(a, b):
                        update(t)
                    attention(i)
            with pe.Else():
                for u in range(NHEAD):
                    mm(ps[u][:, 0:D], C("spread_t", u * P, P), sd[:, 0, 0:D], start=True, stop=True).then_inc(s_su, 1)
                pe.wait_ge(s_suc, NHEAD)

                def rows_of_edges(i):
                    t, u, k, n = BAT[i]
                    g = gather_no[i]
                    s_of = pt2[:, u * D:(u + 1) * D] if u < NHEAD else sd[:, t, 0:D]
                    pe.wait_ge(s_hotp, 2 * g + 2)
                    if g >= 2:
                        pe.wait_ge(s_zed, batch_of[g - 2] + 1)
                    for j in range(n):
                        last = mm(ps[g % 2][:, j * D:(j + 1) * D], hot(g, 0)[:, j * P:(j + 1) * P], s_of,
                                  start=True, stop=True)
                    last.then_inc(s_sep, 1)

                rows_of_edges(batch_of[0])
                for i in range(len(BAT) + TAIL):
                    if i < len(BAT):
                        t, u, k, n = BAT[i]
                        if u is not None and gather_no[i] + 1 < len(gather_no):
                            rows_of_edges(batch_of[gather_no[i] + 1])
                        if u is None and t >= 2:
                            pe.wait_ge(s_agg, t - 1)
                        pe.wait_ge(s_gel, i + 1)
                        pe.wait_ge(s_dia, i + 1)
                        for j in range(n):
                            last = mm(ps[4 + t % 2][:, 0:P], gel(i)[:, j * D:(j + 1) * D], dia(i)[:, j * P:(j + 1) * P],
                                      start=(u is None), stop=(i == LASTB[t] and j == n - 1))
                        last.then_inc(s_bat, 1)
                    for t in range(T):
                        if LASTB[t] + LAG_AGG == i:
                            update(t)
                    for g, (a, b) in enumerate(GROUP):
                        if LASTB[b - 1] + LAG_ATT == i:
                            attention(g)

            pe.wait_ge(s_attc, 2 + 3 * len(GROUP))
            pe.wait_ge(s_ug, T)
            for n in range(STEPS):
                h, t = half(n)
                if n == T:
                    pe.wait_ge(s_z, 3 * NB)
                pe.wait_ge(s_t2, n + 1)
                for b, (c, w) in enumerate(chunks(h)):
                    last = mm(ps[b][:, 0:w], hn[:, t, :], cols[:, 2 + n % 2, c:c + w],
                              start=(t == 0), stop=(t == T - 1))
                if t % 2:
                    pe.wait_ge(s_tsum, n // 2 + 1)
                    at = n // 2 % 2 * HWID[0]
                    for b, (c, w) in enumerate(chunks(h)):
                        last = mm(ps[NB + b][:, 0:w], C("ones"), pt2[:, at + c:at + c + w],
                                  start=(t == 1), stop=(t == T - 1))
                last.then_inc(s_pe3, 1)
                for i in range(NB):
                    if n == T + NORM4_AT[i] - 1:
                        if i == 2:
                            pe.wait_ge(s_x[4], GROUP[0][1])
                        back(4, i, lambda q: pt1[:, q * P:(q + 1) * P], 6 + i % 2, s_zp)
            for i in range(NB, 2 * NB):
                pe.wait_ge(s_z, 3 * (i + 1))
                pe.wait_ge(s_x[4], GROUP[i - 2][1])
                back(4, i, lambda q: pt1[:, q * P:(q + 1) * P], 6 + i % 2, s_zp)


_INS = ("x", "adj_rows", "adj_cols", "head", "weights", "rows4", "consts")


def kernel(**inputs):
    import concourse.bacc as bacc
    from concourse.bass_utils import run_bass_kernel_spmd as run

    a = {k: np.ascontiguousarray(v) for k, v in inputs.items()}
    adj = a["adj"]
    lay = {}
    xp = np.zeros((NP, D), adj.dtype)
    xp[:N] = a["x"]
    lay["x"] = np.ascontiguousarray(xp.reshape(T, P, D).transpose(1, 0, 2))
    for name, m in (("adj_rows", adj), ("adj_cols", adj.T)):
        lay[name] = np.zeros((NP, N), adj.dtype)
        lay[name][:N] = m
    head = np.zeros((P, HEAD_AT[NHEAD]), adj.dtype)
    for u, (row, nrows, parts) in enumerate(HEAD):
        for part in range(parts):
            m = adj[row:row + nrows, part::parts]
            head[part::parts, HEAD_AT[u]:HEAD_AT[u] + m.shape[1]] = m
    lay["head"] = head
    diag = np.zeros(NP, adj.dtype)
    diag[:N] = adj[np.arange(N), np.arange(N)]
    mw, uw = a["L2_gnn_msg_w"], a["L2_gnn_upd_w"]
    w = {
        "w_in": a["L0_gnn_W_in"], "w_out": a["L0_gnn_W_out"],
        "w_msg_t": a["L1_gnn_W_msg"].T, "w_ih_t": a["L1_gnn_W_ih"].T, "w_hh_t": a["L1_gnn_W_hh"].T,
        "w_sd": np.concatenate([mw[:, :D].T, mw[:, D:].T], axis=1), "upd_x": uw[:, :D].T, "upd_a": uw[:, D:].T,
        "w3_t": a["L3_gnn_weight"].T, "w3": a["L3_gnn_weight"],
        "b_msg": a["L1_gnn_b_msg"].reshape(D, 1),
        "b_ih": a["L1_gnn_b_ih"].reshape(3, D).T, "b_hh": a["L1_gnn_b_hh"].reshape(3, D).T,
        "msg_b": a["L2_gnn_msg_b"].reshape(D, 1),
        "att_src": a["L3_gnn_att_src"].reshape(D, 1), "att_dst": a["L3_gnn_att_dst"].reshape(D, 1),
        "diag": diag.reshape(T, P).T,
    }
    lay["weights"] = np.concatenate([w[k] for k in WEIGHT], axis=1)
    lay["rows4"] = np.stack([a["L2_gnn_msg_b"], a["L2_gnn_upd_b"], a["L2_gnn_ln_w"], a["L2_gnn_ln_b"]])[None]
    lay["consts"] = constants()

    nc = bacc.Bacc("TRN2", target_bir_lowering=False, num_devices=1)
    arrays = {f"in_{k}_dram": np.ascontiguousarray(lay[k]) for k in _INS}
    args = [nc.dram_tensor(k, v.shape, mybir.dt.from_np(v.dtype), kind="ExternalInput").ap() for k, v in arrays.items()]
    out = nc.dram_tensor("out_0_dram", (N, D), mybir.dt.float32, kind="ExternalOutput").ap()
    build(nc, *args, out)
    r = run(nc, [arrays], core_ids=[0])
    return r.results[0]["out_0_dram"]
```

```python
import math
from contextlib import ExitStack

import numpy as np

import concourse.bass as bass
from concourse import mybir
from concourse.alu_op_type import AluOpType as ALU

P = 128
N = 2708
T = -(-N // P)
NP = T * P
D = 128
HT = T // 2
HOFF = (0, HT * P)
HWID = (HT * P, N - HT * P)
BANK = 512
RING = 5
EPS = 1e-5

HEAD = ((0, 16, 8), (16, 16, 8), (32, 32, 4), (64, 64, 2))
HEAD_SLOTS = (40, 14, 20, 24)
HEAD_W = tuple(-(-N // parts) for _, _, parts in HEAD)
HEAD_AT = tuple(sum(HEAD_W[:u]) for u in range(len(HEAD) + 1))
TILE_SLOTS = (33, 23, 21, 24, 18, 18, 17, 17, 16, 14, 14, 14, 15, 12, 15, 11, 13, 12, 12, 11, 12)
SLOTS = HEAD_SLOTS + TILE_SLOTS
UNITS = len(SLOTS)
NHEAD = len(HEAD)
ROUNDS = tuple(-(-k // 8) for k in SLOTS)
SLOT_AT = tuple(8 * sum(ROUNDS[:u]) for u in range(UNITS + 1))
SLOT_N = SLOT_AT[UNITS]
CHUNKS = (12, 6, 8, 12) + (16, 13, 11, 10, 9, 8, 8, 7, 7, 7, 6, 6, 6, 6, 5, 5, 5, 5, 5, 5, 1)
CHUNK_AT = tuple(sum(CHUNKS[:u]) for u in range(UNITS + 1))
CHUNK_N = CHUNK_AT[UNITS]
R_MAX = max(k * 3 * c for k, c in zip(SLOTS, CHUNKS))
SEG_KINDS = ((11, 5), (9, 3), (6, 2))


def seg_kind(t):
    return 0 if t <= 2 else 1 if t <= 6 else 2


def seg_bounds(kind):
    n0, n1 = SEG_KINDS[kind]
    h = HOFF[1]
    first = [0]
    for k in range(1, n0):
        first.append(max(first[-1] + 8, round(h * (k / n0) ** 2)))
    a = math.sqrt(h / N)
    second = [round(N * (a + (1 - a) * k / n1) ** 2) for k in range(n1)]
    return [*first, h], [*second, N]


def cand_width(t):
    return 8 * sum(SEG_KINDS[seg_kind(t)])


CAND_AT = {t: sum(cand_width(s) for s in range(1, t)) for t in range(1, T + 1)}
BASE_AT = (0, 8 * sum(SEG_KINDS[0]), 8 * (sum(SEG_KINDS[0]) + sum(SEG_KINDS[1])))
BASE_N = BASE_AT[2] + 8 * sum(SEG_KINDS[2])
WIDEST = 8 * sum(SEG_KINDS[0])

BATCH = 4
IOTA = BATCH * P
CONST = {
    "ident": P,
    "spread_t": NHEAD * P,
    "before": P,
    "twice": 2 * P,
    "seg_base": BASE_N,
    "iota": IOTA,
    "batch_at": 10,
    "row": T,
    "head_row": NHEAD,
    "head_part": NHEAD,
    "ones": P,
}
CONST_AT = {}
for _name in CONST:
    CONST_AT[_name] = sum(CONST[k] for k in list(CONST)[: list(CONST).index(_name)])
CONST_N = sum(CONST.values())

WEIGHT = {
    "w_in": D, "w_out": D,
    "w_msg_t": D, "w_ih_t": 3 * D, "w_hh_t": 3 * D,
    "w_sd": 2 * D, "upd_x": D, "upd_a": D,
    "w3_t": D, "w3": D,
    "b_msg": 1, "b_ih": 3, "b_hh": 3, "msg_b": 1, "att_src": 1, "att_dst": 1,
    "diag": T,
}
WEIGHT_AT = {}
for _name in WEIGHT:
    WEIGHT_AT[_name] = sum(WEIGHT[k] for k in list(WEIGHT)[: list(WEIGHT).index(_name)])
WEIGHT_N = sum(WEIGHT.values())
ROWS4 = 4


def constants():
    c = {k: np.zeros((P, w), np.float32) for k, w in CONST.items()}
    c["ident"][:] = np.eye(P)
    c["ones"][:] = 1
    c["before"][:] = np.triu(np.ones((P, P)), 1)
    c["twice"][:] = np.arange(2 * P) % P
    c["iota"][:] = np.arange(IOTA)
    for diag in range(2):
        first = np.maximum(BATCH * P * np.arange(5) - diag * P, 0)
        c["batch_at"][:, 5 * diag:5 * diag + 5] = first + 0.5
    c["row"][:] = np.arange(P)[:, None] + P * np.arange(T)
    for u, (row, _, parts) in enumerate(HEAD):
        p = np.arange(P)
        r = row + p // parts
        c["spread_t"][r, u * P + p] = 1
        c["head_row"][:, u] = r
        c["head_part"][:, u] = p % parts
    for kind in range(3):
        first, second = seg_bounds(kind)
        starts = first[:-1] + second[:-1]
        c["seg_base"][:, BASE_AT[kind]:BASE_AT[kind] + 8 * len(starts)] = np.repeat(starts, 8)
    return np.concatenate([c[k] for k in CONST], axis=1)




def with_diagonal(u):
    return int(u == 0 or u >= NHEAD)


def batches():
    out = []
    for t in range(T):
        for u in (range(NHEAD) if t == 0 else [NHEAD + t - 1]):
            k = 0
            while k < CHUNKS[u]:
                diag = int(k == 0 and with_diagonal(u))
                n = min(BATCH - diag, CHUNKS[u] - k)
                out.append((t, u, k, n, diag))
                k += n
    return out


def chunks(h):
    return [(c, min(BANK, HWID[h] - c)) for c in range(0, HWID[h], BANK)]


CH = [(h, HOFF[h] + c, w) for h in range(2) for c, w in chunks(h)]
NB = len(chunks(0))
GROUP = [(HT * h + 4 * b, min(HT * h + 4 * b + 4, HT * (h + 1))) for h in range(2) for b in range(NB)]
assert len(chunks(1)) == NB


BATCH_AT = tuple(sum(-(-(CHUNKS[q] + with_diagonal(q)) // BATCH) for q in range(u)) for u in range(UNITS + 1))
BATCH_N = BATCH_AT[UNITS]
NG, NZ = 6, 5
EARLY = 4
FILL_AFTER = {3: 1, 8: 2, 13: 3, **{T + 4 * q: NHEAD + q - 1 for q in range(1, EARLY + 1)}}
ASSIGN_AT = (6, 11, 16, T + 5, T + 9, T + 13)
ASSIGN_AFTER = {n: u for u, n in enumerate(ASSIGN_AT)}
TURN_AFTER = {3: 0, **{n + 2: u + 1 for u, n in enumerate(ASSIGN_AT)}}
L1_LEFT = UNITS - len(ASSIGN_AT)
L1_TURN_AFTER = {1 + k * (2 * T - 2) // (L1_LEFT - 1): len(ASSIGN_AT) + k + 1 for k in range(L1_LEFT)}
assert max(L1_TURN_AFTER) < 2 * T
MESSAGE_AFTER = {T + 5: 0, T + 11: 1, T + 18: 2}
GATES_AFTER = {T + 6: 0, T + 12: 1, T + 19: 2}
GRU_AFTER = {T + 8: 0, T + 14: 1, T + 21: 2}
STATE_AFTER = {T + 10: 0, T + 16: 1}
NORM_AFTER = {T + 12: 0, T + 18: 1}
SD_PAIR = [(t, min(t + 2, b)) for a, b in GROUP for t in range(a, b, 2)]
SD_AT = [sum(p[0] < a for p in SD_PAIR) for a, _ in GROUP] + [len(SD_PAIR)]
LAG_AGG, LAG_UP, LAG_GELU, LAG_SUM, LAG_NORM, LAG_ATT, TAIL = 1, 1, 2, 3, 3, 8, 14
LASTG = len(GROUP) - 1
LATE = LASTG - 1
NORM_LAGS, NORMALISE_LAGS = (0, 2, 3), (1, 4)
NORM_STEP = {0: (LATE, 0), 2: (LATE, 1), 3: (LATE, 2), 5: (LASTG, 0), 7: (LASTG, 1), 8: (LASTG, 2)}
NORMALISE_STEP = {2: (LATE, 0), 5: (LATE, 1), 7: (LASTG, 0), 10: (LASTG, 1)}
ATT_PE = {6 + 6 * (i - LATE) + 2 * q: (i, q) for i in range(LATE, LASTG + 1) for q in range(3)}
ATT_ACT = {n + 2: work for n, work in ATT_PE.items()}
QUADS = (T - 1) // 4
SINGLE = 4 * QUADS
CLOSE_PE, CLOSE_DVE = (4, 8, 12), (7, 11, 15)
COPY_Z = T + 3


def build(nc, x, adj_rows, adj_cols, head, weights, rows4, consts, out):
    f32, u32, i32, bf16 = mybir.dt.float32, mybir.dt.uint32, mybir.dt.int32, mybir.dt.bfloat16
    ACT = mybir.ActivationFunctionType
    AX = mybir.AxisListType.X
    d_table = nc.dram_tensor("d_table", (NP, D), f32).ap()

    ctx = ExitStack()
    with ctx:
        def sb(name, shape, dt=f32):
            return ctx.enter_context(nc.sbuf_tensor(name, shape, dt))

        def sem(name):
            return ctx.enter_context(nc.semaphore(name))

        xa = sb("xa", [P, T, D])
        xb = sb("xb", [P, T, D])
        xt = sb("xt", [P, NP])
        pt1 = sb("pt1", [P, NP])
        pt2 = sb("pt2", [P, NP])
        hn = sb("hn", [P, T, D])
        sd = sb("sd", [P, T, 2 * D])
        rows = sb("rows", [P, RING, HWID[0]])
        cols = sb("cols", [P, RING, HWID[0]])
        cand = sb("cand", [P, CAND_AT[T]])
        cand_i = sb("cand_i", [P, CAND_AT[T]], u32)
        cand_c = sb("cand_c", [P, 2, WIDEST])
        cand_v = sb("cand_v", [P, 2, WIDEST])
        pos = sb("pos", [P, SLOT_N], u32)
        pos_f = sb("pos_f", [P, SLOT_N])
        vals = sb("vals", [P, SLOT_N])
        col_f = sb("col_f", [P, SLOT_N])
        count = sb("count", [P, UNITS])
        base = sb("base", [P, UNITS])
        end = sb("end", [P, UNITS])
        minus = sb("minus", [P, 2, UNITS])
        edge_i = sb("edge_i", [P, 2, 48], i32)
        edge_c = sb("edge_c", [P, 2, 48], i32)
        edge_x = sb("edge_x", [P, 2, 48])
        shift_i = sb("shift_i", [P, 2], i32)
        shift = sb("shift", [P, 2])
        rest = sb("rest", [P, 3, 48])
        onehot = sb("onehot", [P, 2, 2 * P], bf16)
        rec = sb("rec", [P, 2, R_MAX])
        e_val = sb("e_val", [P, CHUNK_N])
        e_col = sb("e_col", [P, CHUNK_N], u32)
        e_row = sb("e_row", [P, CHUNK_N])
        middle = sb("middle", [P, BATCH_N])
        reach = sb("reach", [P, UNITS])
        cst = sb("cst", [P, CONST_N])
        wts = sb("wts", [P, WEIGHT_N])
        rowv = sb("rowv", [P, ROWS4, D])
        sums = sb("sums", [P, 3, 2, T])
        head_sg = sb("head_sg", [P, NHEAD])
        recip = sb("recip", [P, 2, T])
        degs = sb("degs", [P, 3, 2, T])
        found = sb("found", [P, UNITS])
        left = sb("left", [P, 4, UNITS])
        bad = sb("bad", [P, 5, UNITS])
        badc = sb("badc", [P, 1])
        flag = sb("flag", [1, 1], i32)
        stats = sb("stats", [P, T, 6])
        mv = sb("mv", [P, T, 2])
        rstd = sb("rstd", [P, 2, T])
        nwi = sb("nwi", [P, T], i32)
        nwg = sb("nwg", [P, T], i32)
        nwt = sb("nwt", [P, 3, T])
        b_rz = sb("b_rz", [P, 2])
        eps = sb("eps", [P, 1])
        att = sb("att", [P, 2 + P])
        src = sb("src", [P, T])
        src2 = sb("src2", [P, T])
        inv = sb("inv", [P, T])

        flat = lambda a: a[:, :, :].rearrange("p t d -> p (t d)")
        head_a = flat(hn)[:, 0:HEAD_AT[NHEAD]]
        unread = flat(sd)
        spare = lambda a, b: flat(sd)[:, 3 * HWID[0] + a:3 * HWID[0] + b]
        look = spare(0, 2 * WIDEST).rearrange("p (b w) -> p b w", b=2)
        part = spare(2 * WIDEST, 2 * WIDEST + 288).bitcast(bf16).rearrange("p (b k f) -> p b k f", b=2, f=6)
        assign = spare(2 * WIDEST + 288, 2 * WIDEST + 288 + R_MAX // 3).bitcast(bf16).rearrange(
            "p (b k) -> p b k", b=2)
        counting = spare(2 * WIDEST + 288 + R_MAX // 3, 2 * WIDEST + 336 + R_MAX // 3)
        assert 2 * WIDEST + 336 + R_MAX // 3 <= HWID[0] and HEAD_AT[NHEAD] <= 3 * HWID[0]
        gate = lambda n, w: flat(hn)[:, n * BANK:n * BANK + w]
        ring2 = cols[:, :, :].rearrange("p r w -> p (r w)")
        QW = BATCH * D
        IN_COLS = RING * HWID[0] // QW
        AHEAD = 2

        def place(k):
            at = (k - IN_COLS) * QW
            return ring2[:, k * QW:(k + 1) * QW] if k < IN_COLS else rows[:, 1:4, :].rearrange("p r w -> p (r w)")[:, at:at + QW]

        got = lambda b: place(b % NG)
        zed = lambda b: place(NG + b % NZ)
        gel = lambda b: place(NG + NZ + b % NZ)
        dia = lambda b: place(NG + 2 * NZ + b % NZ)
        assert (NG + 3 * NZ - IN_COLS) * QW <= 3 * HWID[0] and 2 * NP <= RING * HWID[0]
        assert all((2 * T + n) % RING in (0, 4) for n in range(AHEAD))
        hot = lambda b, n: rec[:, b % 2, n * QW:(n + 1) * QW]
        assert R_MAX >= 2 * QW and R_MAX >= HWID[0]
        record = lambda u: rec[:, u % 2, 0:3 * SLOTS[u] * CHUNKS[u]].bitcast(bf16)

        ps = [ctx.enter_context(nc.psum_tensor(f"ps{b}", [P, BANK], f32)) for b in range(8)]

        def C(name, a=0, w=None):
            at = CONST_AT[name] + a
            return cst[:, at:at + (CONST[name] if w is None else w)]

        def W(name, a=0, w=None):
            at = WEIGHT_AT[name] + a
            return wts[:, at:at + (WEIGHT[name] if w is None else w)]

        ident = C("ident")

        s_xin = [sem("s_xin0"), sem("s_xin1")]
        s_const = sem("s_const")
        s_wts = sem("s_wts")
        s_head = sem("s_head")
        s_rows = [sem(f"s_rows{r}") for r in range(RING)]
        s_cols = [sem(f"s_cols{r}") for r in range(RING)]
        s_pe0 = sem("s_pe0")
        s_act0 = sem("s_act0")
        s_max = sem("s_max")
        s_cand = sem("s_cand")
        s_hsg = sem("s_hsg")
        s_ev0 = sem("s_ev0")
        s_deg = sem("s_deg")
        s_p0 = sem("s_p0")
        s_h0 = sem("s_h0")
        s_ex = sem("s_ex")
        s_cnt = sem("s_cnt")
        s_turn = sem("s_turn")
        s_base = sem("s_base")
        s_mid = sem("s_mid")
        s_dist = sem("s_dist")
        s_slots = sem("s_slots")
        s_asg = sem("s_asg")
        s_pool = sem("s_pool")
        s_rec = sem("s_rec")
        s_bad = sem("s_bad")
        s_list = sem("s_list")
        s_mv = [sem(f"s_mv{l}") for l in range(5)]
        s_std = [sem(f"s_std{l}") for l in range(5)]
        s_rs = [sem(f"s_rs{l}") for l in range(5)]
        s_x = [sem(f"s_x{l}") for l in range(5)]
        s_tp = [sem(f"s_tp{l}") for l in range(5)]
        s_xt = [sem(f"s_xt{l}") for l in range(5)]
        s_pe1 = sem("s_pe1")
        s_ev1 = sem("s_ev1")
        s_msgp = sem("s_msgp")
        s_msg = sem("s_msg")
        s_gp = sem("s_gp")
        s_rz = sem("s_rz")
        s_nin = sem("s_nin")
        s_n = sem("s_n")
        s_hc = sem("s_hc")
        s_hp = sem("s_hp")
        s_badp = sem("s_badp")
        s_flag = sem("s_flag")
        s_sdp = sem("s_sdp")
        s_sd = sem("s_sd")
        s_bias = sem("s_bias")
        s_tab = sem("s_tab")
        s_got = [sem(f"s_got{r}") for r in range(NG)]
        s_hotp = sem("s_hotp")
        s_sep = sem("s_sep")
        s_zed = sem("s_zed")
        s_dia = sem("s_dia")
        s_gel = sem("s_gel")
        s_su = sem("s_su")
        s_suc = sem("s_suc")
        s_bat = sem("s_bat")
        s_agg = sem("s_agg")
        s_dtp = sem("s_dtp")
        s_dt = sem("s_dt")
        s_row = [sem(f"s_row{r}") for r in range(2)]
        s_gd = sem("s_gd")
        s_dense = sem("s_dense")
        s_up = sem("s_up")
        s_ug = sem("s_ug")
        s_h2 = sem("s_h2")
        s_att = sem("s_att")
        s_attc = sem("s_attc")
        s_src2 = sem("s_src2")
        s_rel = sem("s_rel")
        s_g = sem("s_g")
        s_t1 = sem("s_t1")
        s_t2 = sem("s_t2")
        s_tsum = sem("s_tsum")
        s_pe3 = sem("s_pe3")
        s_qsum = sem("s_qsum")
        s_zc = sem("s_zc")
        s_sr = sem("s_sr")
        s_zp = sem("s_zp")
        s_rq = sem("s_rq")
        s_q = sem("s_q")
        s_out = sem("s_out")

        block = ctx.enter_context(nc.Block())
        STEPS = 2 * T
        BAT = batches()
        LASTB = {t: max(i for i, b in enumerate(BAT) if b[0] == t) for t in range(T)}
        place_sum = [sum(BAT[j][3] for j in range(i % NG, i + 1, NG)) for i in range(len(BAT))]
        tile_group = {t: i for i, (a, b) in enumerate(GROUP) for t in range(a, b)}

        def half(n):
            return n // T % 2, n % T

        place_1 = lambda n: (0, 1, 4)[n % 3]

        def place_g(n, w):
            at = (n % 4) * HWID[0]
            return rec[:, n % 4, 0:w] if n % 4 < 2 else flat(sd)[:, at:at + w]

        def place_2(n, w):
            at = (n % 4) * HWID[0]
            return flat(sd)[:, at:at + w] if n % 4 < 2 else cols[:, n % 4, 0:w]

        bank_3 = lambda i: (2, 3) if i < LATE else (7, 6)

        def attc_of(t):
            return 2 + 3 * (tile_group[t] + 1)

        def quad(q, w):
            return pt2[:, q % 2 * HWID[0]:q % 2 * HWID[0] + w]

        def pool_steps(n):
            h, t = half(n)
            return 3 * QUADS * h + sum(1 for q in range(min(t, SINGLE - 1) + 1) if q % 4)

        def bank_0(t):
            return t % 7 if t < 14 else NB + (t - 14) % 4

        def bank_1(i):
            return 6 if i < 2 else 3 + i % 2

        def sums_read(t):
            a, b = GROUP[tile_group[t]]
            return a + t + (b - a) + 1

        @block.sync
        def _(sp):
            def load(ring, sems, dram, n):
                h, t = half(n)
                sp.dma_start(ring[:, n % RING, 0:HWID[h]],
                             dram[t * P:(t + 1) * P, HOFF[h]:HOFF[h] + HWID[h]]).then_inc(sems[n % RING], 16)

            for n in range(STEPS):
                if n >= RING:
                    m = n - RING
                    sp.wait_ge(s_pe0, m + 1)
                    sp.wait_ge(s_act0, 3 * (m + 1))
                    taken = (m // T) * (T - 1) + m % T
                    if taken:
                        sp.wait_ge(s_cand, taken)
                if n == 0:
                    sp.dma_start(xa[:, 0:2, :], x[:, 0:2, :]).then_inc(s_xin[0], 16)
                load(cols, s_cols, adj_cols, n)
                load(rows, s_rows, adj_rows, n)
                if n == 0:
                    sp.dma_start(head_a, head).then_inc(s_head, 16)
                if n == 1:
                    sp.dma_start(xa[:, 2:T, :], x[:, 2:T, :]).then_inc(s_xin[1], 16)
                    sp.dma_start(cst[:], consts).then_inc(s_const, 16)
                if n == RING:
                    sp.dma_start(wts[:], weights).then_inc(s_wts, 16)
                    sp.dma_start(rowv[:, :, :], rows4.broadcast_to([P, ROWS4, D])).then_inc(s_wts, 16)
            for n in range(STEPS, 2 * STEPS):
                m = n - RING
                if m < STEPS:
                    sp.wait_ge(s_pe0, m + 1)
                    sp.wait_ge(s_act0, 3 * (m + 1))
                else:
                    sp.wait_ge(s_pe1, m + 1 - STEPS)
                load(cols, s_cols, adj_cols, n)
            for n in range(STEPS, STEPS + AHEAD):
                m = n - RING
                sp.wait_ge(s_cand, (m // T) * (T - 1) + m % T)
                sp.wait_ge(s_pe0, m + 1)
                sp.wait_ge(s_act0, 3 * (m + 1))
                load(rows, s_rows, adj_rows, n)
            for i, (a, b) in enumerate(GROUP):
                sp.wait_ge(s_sd, SD_AT[i + 1])
                sp.dma_start(d_table[a * P:b * P, :].rearrange("(t p) d -> p t d", p=P),
                             sd[:, a:b, D:2 * D]).then_inc(s_tab, 16)
            sp.wait_ge(s_flag, 1)
            over = sp.value_load(flag[0:1, 0:1], min_val=0, max_val=1)
            with sp.If(over > 0):
                with sp.Fori(0, N // 2) as g:
                    for r in range(2):
                        sp.wait_ge(s_dense, 2 * g + r + 1)
                        sp.dma_start(ring2[:, r * NP:r * NP + N],
                                     adj_rows[bass.ds(2 * g + r, 1), :].broadcast_to([P, N])).then_inc(s_row[r], 16)
            with sp.Else():
                sp.wait_ge(s_bat, len(BAT))
            for n in range(STEPS + AHEAD, 2 * STEPS):
                if n >= STEPS + RING:
                    sp.wait_ge(s_t2, n - RING + 1 - STEPS)
                load(rows, s_rows, adj_rows, n)
            full = N // P
            for i, (a, b) in enumerate(GROUP):
                sp.wait_ge(s_x[4], b)
                c = min(b, full)
                sp.dma_start(out[a * P:c * P, :].rearrange("(t p) d -> p t d", p=P), xa[:, a:c, :]).then_inc(s_out, 16)
            sp.dma_start(out[full * P:N, :], xa[0:N - full * P, full, :]).then_inc(s_out, 16)
            sp.wait_ge(s_out, 16 * (len(GROUP) + 1))

        @block.gpsimd
        def _(pool):
            G = nc.gpsimd
            steps = [0]

            def px(ins, wait=True):
                steps[0] += 1
                ins.then_inc(s_pool, 1)
                if wait:
                    pool.wait_ge(s_pool, steps[0])

            def split(u):
                b, n = u % 2, SLOTS[u]
                s = slice(SLOT_AT[u], SLOT_AT[u] + n)
                v1, c1, row, v2, c2, v3 = (part[:, b, 0:n, f] for f in range(6))
                r1, r2, rc = (rest[:, f, 0:n] for f in range(3))
                px(G.tensor_copy(v1, vals[:, s]), False)
                px(G.tensor_copy(c1, col_f[:, s]), False)
                px(G.tensor_scalar(row, C("iota", 0, n), 0.0, C("head_row", u, 1) if u < NHEAD else C("row", 0, 1),
                                   ALU.mult, ALU.add))
                px(G.tensor_tensor(r1, vals[:, s], v1, ALU.subtract), False)
                px(G.tensor_tensor(rc, col_f[:, s], c1, ALU.subtract))
                px(G.tensor_copy(v2, r1), False)
                px(G.tensor_copy(c2, rc))
                px(G.tensor_tensor(r2, r1, v2, ALU.subtract))
                px(G.tensor_copy(v3, r2))

            def records(u):
                b, n, c = u % 2, SLOTS[u], CHUNKS[u]
                pool.wait_ge(s_asg, u + 1)
                G.tensor_tensor(record(u).rearrange("p (k f c) -> p k f c", f=6, c=c),
                                assign[:, b, 0:n * c].rearrange("p (k c) -> p k c", c=c).unsqueeze(2).broadcast_to([P, n, 6, c]),
                                part[:, b, 0:n, :].unsqueeze(3).broadcast_to([P, n, 6, c]), ALU.mult).then_inc(s_rec, 1)

            pool.wait_ge(s_const, 16)
            for u in range(UNITS):
                if u >= 2:
                    pool.wait_ge(s_rec, u - 1)
                pool.wait_ge(s_slots, u + 1)
                split(u)
                if u:
                    records(u - 1)
            records(UNITS - 1)

            pool.wait_ge(s_wts, 32)
            for i, (a, b) in enumerate(GROUP):
                pool.wait_ge(s_sd, SD_AT[i + 1])
                G.tensor_tensor(sd[:, a:b, 0:D], sd[:, a:b, 0:D], rowv[:, 0:1, :].broadcast_to([P, b - a, D]),
                                ALU.add).then_inc(s_bias, 1)
            pool.wait_ge(s_flag, 1)
            over = pool.value_load(flag[0:1, 0:1], min_val=0, max_val=1)
            with pool.If(over > 0):
                pool.nop()
            with pool.Else():
                pool.wait_ge(s_list, 5 * UNITS)
                pool.wait_ge(s_tab, 16 * len(GROUP))
                for i, (t, u, k, n, diag) in enumerate(BAT):
                    if i >= NG:
                        pool.wait_ge(s_zed, i - NG + 1)
                    for j in range(n):
                        at = CHUNK_AT[u] + k + j
                        nc.gpsimd.indirect_dma_start(
                            got(i)[:, j * D:(j + 1) * D], None, d_table,
                            bass.IndirectOffsetOnAxis(ap=e_col[:, at:at + 1], axis=0),
                        ).then_inc(s_got[i % NG], 16)

            for n in range(STEPS):
                h, t = half(n)
                w = HWID[h]
                if t >= SINGLE or t % 4 == 0:
                    continue
                q = QUADS * h + t // 4
                pool.wait_ge(s_t1, n + 1)
                if t % 4 == 1:
                    if q >= 2:
                        pool.wait_ge(s_qsum, q - 1)
                    a = cols[:, place_1(n - 1), 0:w]
                else:
                    pool.wait_ge(s_tsum, pool_steps(n) - 1)
                    a = quad(q, w)
                G.tensor_tensor(quad(q, w), a, cols[:, place_1(n), 0:w], ALU.add).then_inc(s_tsum, 1)

        @block.scalar
        def _(act):
            A = nc.scalar

            def copy_turn(u):
                act.wait_ge(s_turn, u + 1)
                if u:
                    c = CHUNKS[u - 1]
                    s = slice(CHUNK_AT[u - 1], CHUNK_AT[u])
                    A.copy(e_val[:, s], ps[7][:, 0:c]).then_inc(s_list, 1)
                    A.copy(e_col[:, s], ps[7][:, c:2 * c]).then_inc(s_list, 1)
                    A.copy(e_row[:, s], ps[7][:, 2 * c:3 * c]).then_inc(s_list, 1)
                if u < UNITS:
                    q = slice(BATCH_AT[u], BATCH_AT[u + 1])
                    nb = BATCH_AT[u + 1] - BATCH_AT[u]
                    A.copy(base[:, u:u + 1], ps[7][:, 64:65]).then_inc(s_base, 1)
                    A.activation(end[:, u:u + 1], ps[7][:, 64:65], ACT.Identity, bias=count[:, u:u + 1]).then_inc(s_base, 1)
                    act.wait_ge(s_base, 2 * u + 2)
                    A.activation(reach[:, u:u + 1], count[:, u:u + 1], ACT.Square, scale=0.5).then_inc(s_list, 1)
                    A.activation(minus[:, 0, u:u + 1], base[:, u:u + 1], ACT.Identity, scale=-1.0).then_inc(s_mid, 1)
                    act.wait_ge(s_mid, 2 * u + 1)
                    A.activation(minus[:, 1, u:u + 1], count[:, u:u + 1], ACT.Identity, scale=-0.5,
                                 bias=minus[:, 0, u:u + 1]).then_inc(s_mid, 1)
                    act.wait_ge(s_mid, 2 * u + 2)
                    A.activation(middle[:, q], C("batch_at", 5 * with_diagonal(u), nb), ACT.Identity,
                                 bias=minus[:, 1, u:u + 1]).then_inc(s_list, 1)

            act.wait_ge(s_head, 16)
            for u in range(NHEAD):
                A.activation(unread[:, HEAD_AT[u]:HEAD_AT[u + 1]], head_a[:, HEAD_AT[u]:HEAD_AT[u + 1]], ACT.Sign,
                             accum_out=head_sg[:, u:u + 1]).then_inc(s_hsg, 1)
            act.wait_ge(s_hsg, NHEAD)
            for n in range(STEPS):
                h, t = half(n)
                for q, (ring, sems, func) in enumerate(((rows, s_rows, ACT.Copy), (rows, s_rows, ACT.Sign),
                                                        (cols, s_cols, ACT.Copy))):
                    if q != 1:
                        act.wait_ge(sems[n % RING], 16 * (n // RING + 1))
                    m = 3 * n + q
                    if m >= 3:
                        act.wait_ge(s_act0, m - 2)
                    A.activation(unread[:, q * HWID[0]:q * HWID[0] + HWID[h]],
                                 ring[:, n % RING, 0:HWID[h]], func,
                                 accum_out=sums[:, q, h, t:t + 1]).then_inc(s_act0, 1)
                if n in TURN_AFTER:
                    copy_turn(TURN_AFTER[n])
                if t == T - 1:
                    act.wait_ge(s_pe0, n + 1)
                    for b, (c, w) in enumerate(chunks(h)):
                        A.copy(pt1[:, HOFF[h] + c:HOFF[h] + c + w], ps[b][:, 0:w]).then_inc(s_ev0, 1)
                        A.copy(pt2[:, HOFF[h] + c:HOFF[h] + c + w], ps[NB + b][:, 0:w]).then_inc(s_ev0, 1)
            act.wait_ge(s_deg, 4)

            def normalise(i):
                act.wait_ge(s_rs[0], 2 * (i + 1))
                for t in range(*GROUP[i]):
                    A.activation(xb[:, t, :], hn[:, t, :], ACT.Identity, bias=rstd[:, 0, t:t + 1],
                                 scale=rstd[:, 1, t:t + 1]).then_inc(s_x[0], 1)

            for i, (a, b) in enumerate(GROUP):
                act.wait_ge(s_mv[0], 2 * b)
                A.activation(rstd[:, 0, a:b], mv[:, a:b, 1], ACT.Sqrt, bias=eps[:, 0:1]).then_inc(s_std[0], 1)
                if i:
                    normalise(i - 1)
            normalise(len(GROUP) - 1)

            def into_xt(l, i, bank):
                a, b = GROUP[i]
                act.wait_ge(s_tp[l], i + 1)
                A.copy(xt[:, a * P:b * P], ps[bank][:, 0:(b - a) * P]).then_inc(s_xt[l], 1)

            def out_of_1(h):
                act.wait_ge(s_pe1, (h + 1) * T)
                for b, (c, w) in enumerate(chunks(h)):
                    A.copy(pt1[:, HOFF[h] + c:HOFF[h] + c + w], ps[NB * h + b][:, 0:w]).then_inc(s_ev1, 1)

            def gru(i):
                h, c, w = CH[i]
                act.wait_ge(s_msgp, i + 1)
                A.activation(pt2[:, c:c + w], ps[2][:, 0:w], ACT.Relu, bias=W("b_msg")).then_inc(s_msg, 1)
                if i:
                    act.wait_ge(s_hc, 4 * i)
                for g in range(2):
                    act.wait_ge(s_gp, 4 * i + (1, 3)[g])
                    A.activation(gate(g, w), ps[g][:, 0:w], ACT.Sigmoid, bias=b_rz[:, g:g + 1]).then_inc(s_rz, 1)
                act.wait_ge(s_nin, 2 * (i + 1))
                A.activation(gate(3, w), gate(2, w), ACT.Tanh, bias=W("b_ih", 2, 1)).then_inc(s_n, 1)

            def s_and_d(i):
                for j in range(SD_AT[i], SD_AT[i + 1]):
                    a, b = SD_PAIR[j]
                    act.wait_ge(s_sdp, j + 1)
                    A.copy(flat(sd)[:, 2 * D * a:2 * D * b], ps[(7, 5)[j % 2]][:, 0:2 * D * (b - a)]).then_inc(s_sd, 1)

            for n in range(STEPS):
                if n == T - 1:
                    out_of_1(0)
                if 0 <= n - T < len(GROUP):
                    into_xt(0, n - T, 6)
                if n in L1_TURN_AFTER:
                    copy_turn(L1_TURN_AFTER[n])
                if n in GATES_AFTER:
                    gru(GATES_AFTER[n])
            out_of_1(1)
            for i in range(NB, 2 * NB):
                gru(i)
                for g in ((0, 1) if i == NB else (i - 2,)):
                    into_xt(1, g, 5)
                    s_and_d(g)
            for i in range(2 * NB - 2, 2 * NB):
                into_xt(1, i, 5)
                s_and_d(i)

            def aggregated(t):
                act.wait_ge(s_bat, LASTB[t] + 1)
                A.copy(pt1[:, t * P:(t + 1) * P], ps[4 + t % 2][:, 0:P]).then_inc(s_agg, 1)

            def update(t):
                act.wait_ge(s_up, t + 1)
                A.activation(hn[:, t, :], ps[6 + t % 2][:, 0:D], ACT.Gelu).then_inc(s_ug, 1)

            def normalise(l, i, to):
                act.wait_ge(s_rs[l], 13 * (i + 1))
                for t in range(*GROUP[i]):
                    A.activation(to[:, t, :], hn[:, t, :], ACT.Identity, bias=rstd[:, 0, t:t + 1],
                                 scale=rstd[:, 1, t:t + 1]).then_inc(s_x[l], 1)

            def attention(i, stage):
                a, b = GROUP[i]
                h, c, w = CH[i]
                if stage == 0:
                    into_xt(3, i, bank_3(i)[0])
                elif stage == 1:
                    act.wait_ge(s_att, 2 + 2 * i)
                    A.copy(flat(hn)[:, a * D:b * D], ps[bank_3(i)[1]][:, 0:(b - a) * D]).then_inc(s_attc, 1)
                    A.copy(src[:, a:b], ps[bank_3(i)[0]][:, 0:b - a]).then_inc(s_attc, 1)
                    act.wait_ge(s_attc, 4 + 3 * i)
                    A.mul(src2[:, a:b], src[:, a:b], 0.2).then_inc(s_src2, 1)
                else:
                    act.wait_ge(s_att, 3 + 2 * i)
                    A.copy(pt1[:, c:c + w], ps[bank_3(i)[0]][:, 0:w]).then_inc(s_attc, 1)

            act.wait_ge(s_flag, 1)
            over = act.value_load(flag[0:1, 0:1], min_val=0, max_val=1)
            act.wait_ge(s_att, 1)
            A.copy(att[:, 0:2], ps[3][:, 0:2]).then_inc(s_attc, 1)
            act.wait_ge(s_attc, 1)
            A.activation(att[:, 2:2 + P], C("ones"), ACT.Identity, scale=att[:, 1:2]).then_inc(s_attc, 1)
            with act.If(over > 0):
                for i, (h, c, w) in enumerate(CH):
                    act.wait_ge(s_dtp, i + 1)
                    A.activation(pt1[:, c:c + w], ps[i % 2][:, 0:w], ACT.Identity).then_inc(s_dt, 1)
                    A.activation(pt2[:, c:c + w], ps[2 + i % 2][:, 0:w], ACT.Identity,
                                 bias=W("msg_b")).then_inc(s_dt, 1)
                act.wait_ge(s_dt, 2 * len(CH))
                with act.Fori(0, N // 2) as g:
                    for r in range(2):
                        act.wait_ge(s_dense, 2 * g + r + 1)
                        A.activation(flat(hn)[:, 0:N], pt1[:, 0:N], ACT.Gelu,
                                     bias=pt2[:, bass.ds(2 * g + r, 1)]).then_inc(s_gd, 1)
                for i, (a, b) in enumerate(GROUP[:LASTG]):
                    for t in range(a, b):
                        update(t)
                    if i < LATE:
                        normalise(2, i, hn)
                        normalise(3, i, xb)
                        for stage in range(3):
                            attention(i, stage)
            with act.Else():
                for u in range(NHEAD):
                    act.wait_ge(s_su, u + 1)
                    A.copy(pt2[:, u * D:(u + 1) * D], ps[u][:, 0:D]).then_inc(s_suc, 1)

                def distances(i):
                    t, u, k, n, diag = BAT[i]
                    q = BATCH_AT[u] + -(-k // BATCH)
                    if i >= 2:
                        act.wait_ge(s_hotp, i - 1)
                    A.activation(hot(i, 1)[:, 0:n * P], C("iota", 0, n * P), ACT.Square,
                                 bias=middle[:, q:q + 1]).then_inc(s_dist, 1)

                act.wait_ge(s_list, 5 * UNITS)
                distances(0)
                distances(1)
                for i in range(len(BAT) + TAIL):
                    if i + 2 < len(BAT):
                        distances(i + 2)
                    if i < len(BAT):
                        n = BAT[i][3] + BAT[i][4]
                        act.wait_ge(s_zed, i + 1)
                        if i >= NZ:
                            act.wait_ge(s_bat, i - NZ + 1)
                        A.activation(gel(i)[:, 0:n * D], zed(i)[:, 0:n * D], ACT.Gelu).then_inc(s_gel, 1)
                    for t in range(T):
                        if LASTB[t] + LAG_AGG == i:
                            aggregated(t)
                        if LASTB[t] + LAG_GELU == i and t < GROUP[LASTG][0]:
                            update(t)
                    for g, (a, b) in enumerate(GROUP[:LATE]):
                        if i - LASTB[b - 1] - LAG_NORM in NORMALISE_LAGS:
                            q = NORMALISE_LAGS.index(i - LASTB[b - 1] - LAG_NORM)
                            normalise(2 + q, g, (hn, xb)[q])
                    for g, (a, b) in enumerate(GROUP[:LATE]):
                        if i - LASTB[b - 1] - LAG_ATT in (1, 3, 5):
                            attention(g, (i - LASTB[b - 1] - LAG_ATT) // 2)
            def z_out(i):
                h, c, w = CH[i]
                A.copy(pt1[:, c:c + w], ps[i % NB][:, 0:w]).then_inc(s_zc, 1)

            def sums_out(i):
                h, c, w = CH[i]
                A.copy(xt[0:1, c:c + w], ps[NB + i % NB][0:1, 0:w]).then_inc(s_sr, 1)

            for n in range(STEPS):
                h, t = half(n)
                g = place_g(n, HWID[h])
                if n < T:
                    act.wait_ge(s_attc, max(attc_of(t), 2 + 3 * NB))
                    act.wait_ge(s_src2, tile_group[t] + 1)
                elif n == T:
                    act.wait_ge(s_attc, attc_of(T - 1))
                if n >= 4:
                    act.wait_ge(s_t1, n - 3)
                A.activation(g, pt1[:, HOFF[h]:HOFF[h] + HWID[h]], ACT.Relu, bias=src[:, t:t + 1]).then_inc(s_rel, 1)
                act.wait_ge(s_rel, n + 1)
                A.activation(g, g, ACT.Exp, bias=src2[:, t:t + 1], scale=0.8).then_inc(s_g, 1)
                if n == 0:
                    for q in range(*GROUP[LASTG]):
                        update(q)
                if n in NORMALISE_STEP:
                    i, q = NORMALISE_STEP[n]
                    normalise(2 + q, i, (hn, xb)[q])
                if n in ATT_ACT:
                    attention(*ATT_ACT[n])
                if n == COPY_Z:
                    act.wait_ge(s_pe3, T)
                    for i in range(NB):
                        z_out(i)
                    for i in range(NB):
                        sums_out(i)
            act.wait_ge(s_pe3, 2 * T)
            for i in range(NB, 2 * NB):
                z_out(i)
                sums_out(i)
            for i in range(NB, 2 * NB):
                act.wait_ge(s_rs[4], 12 * NB + 13 * (i + 1 - NB))
                for t in range(*GROUP[i]):
                    A.activation(xa[:, t, :], xa[:, t, :], ACT.Identity, bias=rstd[:, 0, t:t + 1],
                                 scale=rstd[:, 1, t:t + 1]).then_inc(s_x[4], 1)

        @block.vector
        def _(dve):
            V = nc.vector
            V.memset(pt1[:, N:NP], 0.0).then_inc(s_deg, 1)
            V.memset(pt2[:, N:NP], 0.0).then_inc(s_deg, 1)
            V.memset(left[:, :, :], 0.0).then_inc(s_deg, 1)
            V.memset(eps[:, :], EPS).then_inc(s_deg, 1)
            dve.wait_ge(s_deg, 4)
            dve.wait_ge(s_head, 16)
            dve.wait_ge(s_hsg, NHEAD)
            ex = [0]

            def sx(ins, wait=True):
                ex[0] += 1
                ins.then_inc(s_ex, 1)
                if wait:
                    dve.wait_ge(s_ex, ex[0])

            def counted(u):
                s = slice(SLOT_AT[u], SLOT_AT[u] + SLOTS[u])
                V.tensor_scalar(counting[:, 0:SLOTS[u]], vals[:, s], 0.0, 0.0, ALU.is_gt, ALU.add,
                                accum_out=count[:, u:u + 1]).then_inc(s_cnt, 1)

            def fill_head(u):
                a = head_a[:, HEAD_AT[u]:HEAD_AT[u + 1]]
                for r in range(ROUNDS[u]):
                    at = SLOT_AT[u] + 8 * r
                    sx(V.max(vals[:, at:at + 8], a))
                    sx(V.max_index(pos[:, at:at + 8], vals[:, at:at + 8], a))
                    sx(V.match_replace(a, vals[:, at:at + 8], a, 0.0))
                s = slice(SLOT_AT[u], SLOT_AT[u + 1])
                sx(V.reduce_max(left[:, 0, u:u + 1], a, AX), False)
                dve.wait_ge(s_const, 16)
                sx(V.tensor_scalar(col_f[:, s], pos[:, s], float(HEAD[u][2]), C("head_part", u, 1), ALU.mult, ALU.add), False)
                if SLOTS[u] % 8:
                    sx(V.reduce_max(left[:, 2, u:u + 1], vals[:, SLOT_AT[u] + SLOTS[u]:SLOT_AT[u + 1]], AX), False)
                sx(V.tensor_scalar(counting[:, 0:8 * ROUNDS[u]], vals[:, s], 0.0, 0.0, ALU.is_gt, ALU.add,
                                   accum_out=found[:, u:u + 1]))
                counted(u)
                dve.wait_ge(s_cnt, u + 1)
                sx(V.scalar_tensor_tensor(vals[:, s], col_f[:, s], C("head_row", u, 1), vals[:, s], ALU.not_equal, ALU.mult))
                V.tensor_scalar(col_f[:, s], col_f[:, s], float(N - 1), None, ALU.min).then_inc(s_slots, 1)

            def fill_tile(u):
                t = u - NHEAD + 1
                kind, w, b = seg_kind(t), cand_width(t), t % 2
                v = cand[:, CAND_AT[t]:CAND_AT[t] + w]
                cc, cv = cand_c[:, b, 0:w], cand_v[:, b, 0:w]
                sx(V.tensor_tensor(cc, cand_i[:, CAND_AT[t]:CAND_AT[t] + w], C("seg_base", BASE_AT[kind], w), ALU.add), False)
                sx(V.tensor_scalar(cv, v, 0.0, 0.0, ALU.is_gt, ALU.add, accum_out=found[:, u:u + 1]), False)
                sx(V.reduce_max(left[:, 1, u:u + 1], v.rearrange("p (s e) -> p s e", e=8)[:, :, 7], AX))
                sx(V.scalar_tensor_tensor(cv, cc, C("row", t, 1), v, ALU.not_equal, ALU.mult))
                s0 = SLOT_AT[u]
                for r in range(ROUNDS[u]):
                    at = s0 + 8 * r
                    sx(V.max(vals[:, at:at + 8], cv))
                    sx(V.max_index(pos[:, at:at + 8], vals[:, at:at + 8], cv), False)
                    sx(V.match_replace(cv, vals[:, at:at + 8], cv, 0.0))
                sx(V.tensor_copy(pos_f[:, s0:SLOT_AT[u + 1]], pos[:, s0:SLOT_AT[u + 1]]), False)
                sx(V.reduce_max(left[:, 0, u:u + 1], cv, AX), False)
                if SLOTS[u] % 8:
                    sx(V.reduce_max(left[:, 2, u:u + 1], vals[:, s0 + SLOTS[u]:SLOT_AT[u + 1]], AX), False)
                counted(u)
                dve.wait_ge(s_cnt, u + 1)
                for k in range(SLOTS[u]):
                    if k >= 2:
                        dve.wait_ge(s_ex, ex[0] - 1)
                    ins = V.scalar_tensor_tensor(look[:, k % 2, 0:w], C("iota", 0, w), pos_f[:, s0 + k:s0 + k + 1], cc,
                                                 ALU.is_equal, ALU.mult, accum_out=col_f[:, s0 + k:s0 + k + 1])
                    if k < SLOTS[u] - 1:
                        sx(ins, False)
                ins.then_inc(s_slots, 1)

            def assigned(u):
                b, n, c = u % 2, SLOTS[u], CHUNKS[u]
                s = slice(SLOT_AT[u], SLOT_AT[u] + n)
                ei, ec, ex_ = edge_i[:, b, 0:n], edge_c[:, b, 0:n], edge_x[:, b, 0:n]
                dve.wait_ge(s_base, 2 * u + 2)
                sx(V.tensor_scalar(ei, C("iota", 0, n), base[:, u:u + 1], None, ALU.add), False)
                dve.wait_ge(s_slots, u + 1)
                sx(V.tensor_scalar(ex_, vals[:, s], 0.0, 4096.0, ALU.is_le, ALU.mult))
                sx(V.tensor_scalar(left[:, 3, u:u + 1], end[:, u:u + 1], float(-P * c), 0.0, ALU.add, ALU.max), False)
                sx(V.tensor_scalar(shift_i[:, b:b + 1], ei[:, 0:1], P - 1, None, ALU.bitwise_and), False)
                sx(V.tensor_scalar(ec, ei, 7, None, ALU.arith_shift_right))
                sx(V.tensor_copy(shift[:, b:b + 1], shift_i[:, b:b + 1]), False)
                sx(V.tensor_tensor(ex_, ex_, ec, ALU.add))
                sx(V.tensor_scalar(onehot[:, b, :], C("twice"), shift[:, b:b + 1], None, ALU.is_equal), False)
                V.tensor_tensor(assign[:, b, 0:n * c].rearrange("p (k c) -> p k c", c=c),
                                C("iota", 0, c).unsqueeze(1).broadcast_to([P, n, c]),
                                ex_.unsqueeze(2).broadcast_to([P, n, c]), ALU.is_equal).then_inc(s_asg, 1)

            fill_head(0)

            nm = 0
            for n in range(STEPS):
                h, t = half(n)
                if t:
                    dve.wait_ge(s_rows[n % RING], 16 * (n // RING + 1))
                    kind = seg_kind(t)
                    bounds = seg_bounds(kind)[h]
                    at = CAND_AT[t] + 8 * (SEG_KINDS[kind][0] if h else 0)
                    parts = [(at + 8 * k, rows[:, n % RING, bounds[k] - HOFF[h]:bounds[k + 1] - HOFF[h]])
                             for k in range(len(bounds) - 1)]
                    for c, a in parts:
                        V.max(cand[:, c:c + 8], a).then_inc(s_max, 1)
                    nm += len(parts)
                    dve.wait_ge(s_max, nm)
                    for c, a in parts:
                        ins = V.max_index(cand_i[:, c:c + 8], cand[:, c:c + 8], a)
                    ins.then_inc(s_cand, 1)
                if n in FILL_AFTER:
                    u = FILL_AFTER[n]
                    if u < NHEAD:
                        fill_head(u)
                    else:
                        dve.wait_ge(s_cand, T - 1 + t)
                        fill_tile(u)
                if n in ASSIGN_AFTER:
                    assigned(ASSIGN_AFTER[n])

            dg = [4]

            def dx(ins):
                dg[0] += 1
                ins.then_inc(s_deg, 1)
                dve.wait_ge(s_deg, dg[0])

            dve.wait_ge(s_act0, 3 * STEPS)
            dve.wait_ge(s_wts, 32)
            dx(V.tensor_tensor(degs[:, 0, :, :], sums[:, 0::2, 0, :], sums[:, 0::2, 1, :], ALU.add))
            dx(V.tensor_scalar(degs[:, 1, :, :], degs[:, 0, :, :], 0.0, None, ALU.is_gt))
            dx(V.tensor_tensor(degs[:, 0, :, :], degs[:, 0, :, :], degs[:, 1, :, :], ALU.mult))
            dx(V.tensor_scalar(degs[:, 2, :, :], degs[:, 1, :, :], -1.0, 1.0, ALU.mult, ALU.add))
            dx(V.tensor_tensor(b_rz[:, :], W("b_ih", 0, 2), W("b_hh", 0, 2), ALU.add))
            dx(V.tensor_tensor(degs[:, 0, :, :], degs[:, 0, :, :], degs[:, 2, :, :], ALU.add))
            dx(V.reciprocal(recip[:, :, :], degs[:, 0, :, :]))

            def moments(l, i, h_tile):
                a, b = GROUP[i]
                for t in range(a, b):
                    V.bn_stats(stats[:, t, :], h_tile(t)).then_inc(s_mv[l], 1)
                dve.wait_ge(s_mv[l], a + b)
                for t in range(a, b):
                    V.bn_aggr(mv[:, t, :], stats[:, t, :]).then_inc(s_mv[l], 1)
                dve.wait_ge(s_mv[l], 2 * b)

            rsn = [0] * 5

            def rx(l, ins):
                rsn[l] += 1
                ins.then_inc(s_rs[l], 1)
                dve.wait_ge(s_rs[l], rsn[l])

            def inverse(l, i):
                s = slice(*GROUP[i])
                v, y, q = nwt[:, 0, s], rstd[:, 1, s], nwt[:, 1, s]
                rx(l, V.tensor_scalar(v, mv[:, s, 1], EPS, None, ALU.add))
                rx(l, V.tensor_scalar(nwi[:, s], v.bitcast(i32), 1, None, ALU.arith_shift_right))
                rx(l, V.tensor_scalar(y.bitcast(i32), nwi[:, s], -1.0, float(0x5F3759DF), ALU.mult, ALU.add))
                for _ in range(3):
                    rx(l, V.tensor_tensor(q, y, y, ALU.mult))
                    rx(l, V.scalar_tensor_tensor(q, q, -0.5, v, ALU.mult, ALU.mult))
                    rx(l, V.scalar_tensor_tensor(y, q, 1.5, y, ALU.add, ALU.mult))

            def shift_of(l, i):
                s = slice(*GROUP[i])
                rx(l, V.scalar_tensor_tensor(rstd[:, 0, s], mv[:, s, 0], -1.0, rstd[:, 1, s], ALU.mult, ALU.mult))

            def normalised(l, i, h_tile, to):
                for t in range(*GROUP[i]):
                    V.tensor_scalar(to(t), h_tile(t), mv[:, t, 0:1], rstd[:, 1, t:t + 1],
                                    ALU.subtract, ALU.mult).then_inc(s_x[l], 1)

            tile = lambda a: (lambda t: a[:, t, :])

            def close0(i):
                dve.wait_ge(s_std[0], i + 1)
                s = slice(*GROUP[i])
                rx(0, V.reciprocal(rstd[:, 1, s], rstd[:, 0, s]))
                rx(0, V.scalar_tensor_tensor(rstd[:, 0, s], mv[:, s, 0], -1.0, rstd[:, 1, s], ALU.mult, ALU.mult))

            for i, (a, b) in enumerate(GROUP):
                for t in range(a, b):
                    dve.wait_ge(s_p0, t + 1)
                    V.scalar_tensor_tensor(hn[:, t, :], ps[bank_0(t)][:, 0:D], recip[:, 0, t:t + 1], xa[:, t, :],
                                           ALU.mult, ALU.add).then_inc(s_h0, 1)
                dve.wait_ge(s_h0, a + b)
                for t in range(a, b):
                    V.scalar_tensor_tensor(hn[:, t, :], ps[bank_0(t)][:, D:2 * D], recip[:, 1, t:t + 1], hn[:, t, :],
                                           ALU.mult, ALU.add).then_inc(s_h0, 1)
                dve.wait_ge(s_h0, 2 * b)
                moments(0, i, tile(hn))
                if i:
                    close0(i - 1)
            close0(len(GROUP) - 1)

            dve.wait_ge(s_x[0], T)

            def gru(i):
                h, c, w = CH[i]
                r, z, a, m, o = (gate(k, w) for k in range(5))
                dve.wait_ge(s_rz, 2 * i + 1)
                dve.wait_ge(s_gp, 4 * i + 2)
                V.scalar_tensor_tensor(a, ps[6][:, 0:w], W("b_hh", 2, 1), r, ALU.add, ALU.mult).then_inc(s_nin, 1)
                dve.wait_ge(s_nin, 2 * i + 1)
                dve.wait_ge(s_gp, 4 * i + 4)
                V.tensor_tensor(a, a, ps[2][:, 0:w], ALU.add).then_inc(s_nin, 1)
                dve.wait_ge(s_rz, 2 * i + 2)
                dve.wait_ge(s_n, i + 1)
                V.tensor_tensor(o, xt[:, c:c + w], m, ALU.subtract).then_inc(s_hc, 1)
                dve.wait_ge(s_hc, 4 * i + 1)
                V.tensor_tensor(o, z, o, ALU.mult).then_inc(s_hc, 1)
                dve.wait_ge(s_hc, 4 * i + 2)
                V.tensor_tensor(o, m, o, ALU.add).then_inc(s_hc, 1)
                dve.wait_ge(s_hc, 4 * i + 3)
                V.tensor_tensor(pt1[:, c:c + w], xt[:, c:c + w], o, ALU.add).then_inc(s_hc, 1)

            def norm1(i):
                a, b = GROUP[i]
                in_bank = lambda t: ps[bank_1(i)][:, (t - a) * D:(t - a + 1) * D]
                dve.wait_ge(s_hp, i + 1)
                moments(1, i, in_bank)
                inverse(1, i)
                normalised(1, i, in_bank, tile(xa))

            dve.wait_ge(s_cand, 2 * (T - 1))
            for n in range(STEPS):
                if n in L1_TURN_AFTER:
                    u = L1_TURN_AFTER[n]
                    if NHEAD + EARLY <= u < UNITS:
                        fill_tile(u)
                    assigned(u - 1)
                if n in GRU_AFTER:
                    gru(GRU_AFTER[n])
                if n in NORM_AFTER:
                    norm1(NORM_AFTER[n])

            dve.wait_ge(s_asg, UNITS)
            sx(V.tensor_tensor(degs[:, 0, 0, :], sums[:, 1, 0, :], sums[:, 1, 1, :], ALU.add))
            sx(V.tensor_tensor(bad[:, 0, 0:NHEAD], found[:, 0:NHEAD], head_sg[:, :], ALU.not_equal), False)
            sx(V.tensor_tensor(bad[:, 0, NHEAD:UNITS], found[:, NHEAD:UNITS], degs[:, 0, 0, 1:T], ALU.not_equal), False)
            sx(V.tensor_scalar(bad[:, 1:5, :], left[:, :, :], 0.0, None, ALU.not_equal))
            V.tensor_reduce(badc[:, :], bad[:, :, :], mybir.AxisListType.XY, ALU.add).then_inc(s_bad, 1)
            norm1(NB - 1)
            dve.wait_ge(s_badp, 1)
            V.tensor_scalar(flag[0:1, 0:1], ps[7][0:1, 255:256], 0.0, None, ALU.not_equal).then_inc(s_flag, 1)
            gru(NB)
            for i in range(NB, 2 * NB):
                if i + 1 < 2 * NB:
                    gru(i + 1)
                norm1(i)

            h2 = [0]

            def hx(ins, wait=True):
                h2[0] += 1
                ins.then_inc(s_h2, 1)
                if wait:
                    dve.wait_ge(s_h2, h2[0])

            def update(t):
                dve.wait_ge(s_ug, t + 1)
                hx(V.tensor_tensor(hn[:, t, :], hn[:, t, :], xa[:, t, :], ALU.add), False)

            def norm23(i, stage):
                a, b = GROUP[i]
                g = hn[:, a:b, :]
                on_tiles = lambda r: rowv[:, r:r + 1, :].broadcast_to([P, b - a, D])
                if stage == 0:
                    dve.wait_ge(s_h2, h2[0])
                    moments(2, i, tile(hn))
                    inverse(2, i)
                    shift_of(2, i)
                elif stage == 1:
                    dve.wait_ge(s_x[2], b)
                    hx(V.tensor_tensor(g, g, on_tiles(2), ALU.mult))
                    hx(V.tensor_tensor(g, g, on_tiles(3), ALU.add))
                    hx(V.tensor_tensor(g, g, xa[:, a:b, :], ALU.add))
                else:
                    moments(3, i, tile(hn))
                    inverse(3, i)
                    shift_of(3, i)

            dve.wait_ge(s_flag, 1)
            over = dve.value_load(flag[0:1, 0:1], min_val=0, max_val=1)
            dve.wait_ge(s_bias, len(GROUP))
            with dve.If(over > 0):
                V.memset(badc[:, :], 0.0).then_inc(s_dense, 1)
                with dve.Fori(0, N // 2) as g:
                    for r in range(2):
                        dve.wait_ge(s_row[r], 16 * g + 16)
                        dve.wait_ge(s_gd, 2 * g + r + 1)
                        V.scalar_tensor_tensor(flat(hn)[:, 0:N], flat(hn)[:, 0:N], 1.0, ring2[:, r * NP:r * NP + N],
                                               ALU.mult, ALU.mult,
                                               accum_out=flat(xb)[:, bass.ds(2 * g + r, 1)]).then_inc(s_dense, 1)
                dve.wait_ge(s_dense, N + 1)
                V.tensor_copy(pt1[:, 0:N], flat(xb)[:, 0:N]).then_inc(s_agg, T)
                dve.wait_ge(s_agg, T)
                for i, (a, b) in enumerate(GROUP[:LASTG]):
                    for t in range(a, b):
                        update(t)
                    for stage in range(3 if i < LATE else 0):
                        norm23(i, stage)
            with dve.Else():
                h2[0] = 0
                rsn[2] = rsn[3] = 0

                def one_hot(i):
                    t, u, k, n, diag = BAT[i]
                    w = n * P
                    if i >= 2:
                        dve.wait_ge(s_sep, i - 1)
                    dve.wait_ge(s_dist, i + 1)
                    V.tensor_scalar(hot(i, 0)[:, 0:w], hot(i, 1)[:, 0:w], reach[:, u:u + 1], None,
                                    ALU.is_le).then_inc(s_hotp, 1)

                one_hot(0)
                for i in range(len(BAT) + TAIL):
                    if i < len(BAT):
                        t, u, k, n, diag = BAT[i]
                        if i + 1 < len(BAT):
                            one_hot(i + 1)
                        if i >= NZ:
                            dve.wait_ge(s_bat, i - NZ + 1)
                        for j in range(n):
                            at = CHUNK_AT[u] + k + j
                            ins = V.tensor_scalar(dia(i)[:, j * P:(j + 1) * P], C("iota", 0, P), e_row[:, at:at + 1],
                                                  e_val[:, at:at + 1], ALU.is_equal, ALU.mult)
                        if diag:
                            ins = V.tensor_scalar(dia(i)[:, n * P:(n + 1) * P], ident, W("diag", t, 1), None, ALU.mult)
                        ins.then_inc(s_dia, 1)
                        if i >= NZ:
                            dve.wait_ge(s_gel, i - NZ + 1)
                        if diag:
                            V.tensor_tensor(zed(i)[:, n * D:(n + 1) * D], sd[:, t, 0:D], sd[:, t, D:2 * D], ALU.add)
                        dve.wait_ge(s_got[i % NG], 16 * place_sum[i])
                        dve.wait_ge(s_sep, i + 1)
                        V.tensor_tensor(zed(i)[:, 0:n * D], got(i)[:, 0:n * D], ps[i % 2][:, 0:n * D],
                                        ALU.add).then_inc(s_zed, 1)
                    for t in range(T):
                        if LASTB[t] + LAG_SUM == i and t < GROUP[LASTG][0]:
                            update(t)
                    for g, (a, b) in enumerate(GROUP[:LATE]):
                        if i - LASTB[b - 1] - LAG_NORM in NORM_LAGS:
                            norm23(g, NORM_LAGS.index(i - LASTB[b - 1] - LAG_NORM))
                dve.wait_ge(s_bat, len(BAT))

            def quotients(i):
                for j in range(SD_AT[i], SD_AT[i + 1]):
                    a, b = SD_PAIR[j]
                    bank = ps[6 + j % 2]
                    dve.wait_ge(s_zp, j + 1)
                    V.reciprocal(inv[:, a:b], bank[:, 2 * P:2 * P + b - a]).then_inc(s_rq, 1)
                    dve.wait_ge(s_rq, j + 1)
                    for t in range(a, b):
                        ins = V.scalar_tensor_tensor(xa[:, t, :], bank[:, (t - a) * D:(t - a + 1) * D],
                                                     inv[:, t:t + 1], xb[:, t, :], ALU.mult, ALU.add)
                    ins.then_inc(s_q, 1)

            def norm4(i, stage):
                if stage == 0:
                    dve.wait_ge(s_q, SD_AT[i + 1])
                    moments(4, i, tile(xa))
                    inverse(4, i)
                else:
                    normalised(4, i, tile(xa), tile(xa))

            for n in range(STEPS):
                h, t = half(n)
                w = HWID[h]
                g, t1, t2 = place_g(n, w), cols[:, place_1(n), 0:w], place_2(n, w)
                a = rows[:, (n + STEPS) % RING, 0:w]
                dve.wait_ge(s_rows[(n + STEPS) % RING], 16 * ((n + STEPS) // RING + 1))
                dve.wait_ge(s_g, n + 1)
                if n >= 4:
                    dve.wait_ge(s_pe3, n - 3)
                m = n - 3
                if m >= 0:
                    if half(m)[1] < SINGLE:
                        dve.wait_ge(s_tsum, pool_steps(m if half(m)[1] % 4 else m + 1))
                    else:
                        dve.wait_ge(s_pe3, m + 1)
                V.tensor_tensor(t1, a, g, ALU.mult).then_inc(s_t1, 1)
                dve.wait_ge(s_t1, n + 1)
                V.tensor_tensor(t2, a, t1, ALU.mult).then_inc(s_t2, 1)
                if n == 1:
                    for q in range(*GROUP[LASTG]):
                        update(q)
                if n in NORM_STEP:
                    norm23(*NORM_STEP[n])
                if h and t in CLOSE_DVE:
                    quotients(CLOSE_DVE.index(t))
                for stage in range(2):
                    if h and t - 1 - stage in CLOSE_DVE:
                        norm4(CLOSE_DVE.index(t - 1 - stage), stage)
            quotients(NB)
            for i in range(NB, 2 * NB):
                if i + 1 < 2 * NB:
                    quotients(i + 1)
                norm4(i, 0)
                shift_of(4, i)

        @block.tensor
        def _(pe):
            mm = nc.tensor.matmul

            def back(l, i, of, bank, done):
                a, b = GROUP[i]
                for t in range(a, b):
                    last = nc.tensor.transpose(ps[bank][:, (t - a) * P:(t - a + 1) * P], of(t), ident)
                last.then_inc(done, 1)

            def turn(u):
                if u:
                    pe.wait_ge(s_base, 2 * u)
                    pe.wait_ge(s_rec, u)
                    n, c = SLOTS[u - 1], CHUNKS[u - 1]
                    for k in range(n):
                        r = record(u - 1)[:, 6 * c * k:6 * c * (k + 1)]
                        move = onehot[:, (u - 1) % 2, P - k:2 * P - k]
                        mm(ps[7][:, 0:3 * c], move, r[:, 0:3 * c], start=(k == 0), stop=False)
                        mm(ps[7][:, 0:2 * c], move, r[:, 3 * c:5 * c], start=False, stop=False)
                        last = mm(ps[7][:, 0:c], move, r[:, 5 * c:6 * c], start=False, stop=(k == n - 1))
                if u < UNITS:
                    pe.wait_ge(s_cnt, u + 1)
                    last = mm(ps[7][:, 64:65], C("before"), count[:, u:u + 1], start=True, stop=True)
                last.then_inc(s_turn, 1)

            for n in range(STEPS):
                h, t = half(n)
                pe.wait_ge(s_xin[n > 1], 16)
                pe.wait_ge(s_cols[n % RING], 16 * (n // RING + 1))
                if n == T:
                    pe.wait_ge(s_ev0, 2 * NB)
                for ring, sems, b0 in ((cols, s_cols, 0), (rows, s_rows, NB)):
                    pe.wait_ge(sems[n % RING], 16 * (n // RING + 1))
                    for b, (c, w) in enumerate(chunks(h)):
                        last = mm(ps[b0 + b][:, 0:w], xa[:, t, :], ring[:, n % RING, c:c + w],
                                  start=(t == 0), stop=(t == T - 1))
                last.then_inc(s_pe0, 1)
                if n == min(TURN_AFTER):
                    pe.wait_ge(s_const, 16)
                if n in TURN_AFTER:
                    turn(TURN_AFTER[n])
            pe.wait_ge(s_ev0, 4 * NB)
            pe.wait_ge(s_deg, 2)
            pe.wait_ge(s_wts, 32)
            for t in range(T):
                before = [q for q in range(t) if bank_0(q) == bank_0(t)]
                if before:
                    pe.wait_ge(s_h0, sums_read(before[-1]))
                s = slice(t * P, (t + 1) * P)
                mm(ps[bank_0(t)][:, 0:D], pt1[:, s], W("w_in"), start=True, stop=True)
                mm(ps[bank_0(t)][:, D:2 * D], pt2[:, s], W("w_out"), start=True, stop=True).then_inc(s_p0, 1)

            def message(i):
                h, c, w = CH[i]
                pe.wait_ge(s_ev1, (h + 1) * NB)
                if i:
                    pe.wait_ge(s_nin, 2 * i)
                mm(ps[2][:, 0:w], W("w_msg_t"), pt1[:, c:c + w], start=True, stop=True).then_inc(s_msgp, 1)

            def gates(i):
                h, c, w = CH[i]
                pe.wait_ge(s_xt[0], len(GROUP))
                pe.wait_ge(s_msg, i + 1)
                if i:
                    pe.wait_ge(s_rz, 2 * i)
                if 0 < i < 3:
                    pe.wait_ge(s_x[1], GROUP[i - 1][1])
                ih = lambda g: (W("w_ih_t", g * D, D), pt2[:, c:c + w])
                hh = lambda g: (W("w_hh_t", g * D, D), xt[:, c:c + w])
                mm(ps[0][:, 0:w], *ih(0), start=True, stop=False)
                mm(ps[0][:, 0:w], *hh(0), start=False, stop=True).then_inc(s_gp, 1)
                mm(ps[6][:, 0:w], *hh(2), start=True, stop=True).then_inc(s_gp, 1)
                mm(ps[1][:, 0:w], *ih(1), start=True, stop=False)
                mm(ps[1][:, 0:w], *hh(1), start=False, stop=True).then_inc(s_gp, 1)
                mm(ps[2][:, 0:w], *ih(2), start=True, stop=True).then_inc(s_gp, 1)

            def new_state(i):
                pe.wait_ge(s_hc, 4 * (i + 1))
                if i > NB:
                    pe.wait_ge(s_x[1], GROUP[i - 2][1])
                back(1, i, lambda t: pt1[:, t * P:(t + 1) * P], bank_1(i), s_hp)

            for n in range(STEPS):
                h, t = half(n)
                m = n + STEPS
                pe.wait_ge(s_cols[m % RING], 16 * (m // RING + 1))
                pe.wait_ge(s_x[0], t + 1)
                if n in (0, T):
                    pe.wait_ge(s_h0, max(sums_read(q) for q in range(T) if n or bank_0(q) < NB))
                for b, (c, w) in enumerate(chunks(h)):
                    last = mm(ps[NB * h + b][:, 0:w], xb[:, t, :], cols[:, m % RING, c:c + w],
                              start=(t == 0), stop=(t == T - 1))
                last.then_inc(s_pe1, 1)
                if h == 1 and t < len(GROUP):
                    if t:
                        pe.wait_ge(s_xt[0], t)
                    back(0, t, lambda q: xb[:, q, :], 6, s_tp[0])
                if n in L1_TURN_AFTER:
                    turn(L1_TURN_AFTER[n])
                if n in MESSAGE_AFTER:
                    message(MESSAGE_AFTER[n])
                if n in GATES_AFTER:
                    gates(GATES_AFTER[n])
                if n in STATE_AFTER:
                    new_state(STATE_AFTER[n])
            def s_and_d(i):
                pe.wait_ge(s_x[1], GROUP[i][1])
                if i:
                    pe.wait_ge(s_sd, SD_AT[i])
                back(1, i, lambda t: xa[:, t, :], 5, s_tp[1])
                pe.wait_ge(s_xt[1], i + 1)
                for j in range(SD_AT[i], SD_AT[i + 1]):
                    a, b = SD_PAIR[j]
                    bank = ps[(7, 5)[j % 2]]
                    if j >= 2:
                        pe.wait_ge(s_sd, j - 1)
                    for t in range(a, b):
                        o = 2 * D * (t - a)
                        last = mm(bank[:, o:o + 2 * D], xt[:, t * P:(t + 1) * P], W("w_sd"), start=True, stop=True)
                    last.then_inc(s_sdp, 1)

            for i in range(NB, 2 * NB):
                message(i)
                if i == NB:
                    new_state(i - 1)
                gates(i)
                if i == NB:
                    pe.wait_ge(s_list, 5 * UNITS)
                    pe.wait_ge(s_bad, 1)
                    mm(ps[7][0:1, 255:256], badc[:, 0:1], C("ones", 0, 1), start=True, stop=True).then_inc(s_badp, 1)
                    pe.wait_ge(s_flag, 1)
                    s_and_d(0)
                else:
                    new_state(i - 1)
                s_and_d(i - 2)
            new_state(2 * NB - 1)
            for i in range(2 * NB - 2, 2 * NB):
                s_and_d(i)

            def update(t):
                s = slice(t * P, (t + 1) * P)
                pe.wait_ge(s_agg, t + 1)
                if t >= 2:
                    pe.wait_ge(s_ug, t - 1)
                bank = ps[6 + t % 2]
                mm(bank[:, 0:D], xt[:, s], W("upd_x"), start=True, stop=False)
                mm(bank[:, 0:D], pt1[:, s], W("upd_a"), start=False, stop=False)
                mm(bank[:, 0:D], C("ones")[0:1, :], rowv[0:1, 1, :], start=False, stop=True).then_inc(s_up, 1)

            def attention(i, stage):
                a, b = GROUP[i]
                h, c, w = CH[i]
                if stage == 0:
                    pe.wait_ge(s_x[3], b)
                    pe.wait_ge(s_attc, 2 + 3 * i)
                    back(3, i, lambda t: xb[:, t, :], bank_3(i)[0], s_tp[3])
                elif stage == 1:
                    pe.wait_ge(s_xt[3], i + 1)
                    for t in range(a, b):
                        o = (t - a) * D
                        mm(ps[bank_3(i)[1]][:, o:o + D], xt[:, t * P:(t + 1) * P], W("w3_t"), start=True, stop=True)
                        last = mm(ps[bank_3(i)[0]][:, t - a:t - a + 1], xt[:, t * P:(t + 1) * P], att[:, 0:1], start=True, stop=True)
                    last.then_inc(s_att, 1)
                else:
                    pe.wait_ge(s_attc, 4 + 3 * i)
                    mm(ps[bank_3(i)[0]][:, 0:w], att[:, 2:2 + P], xt[:, c:c + w], start=True, stop=True).then_inc(s_att, 1)

            pe.wait_ge(s_flag, 1)
            over = pe.value_load(flag[0:1, 0:1], min_val=0, max_val=1)
            pe.wait_ge(s_sd, len(SD_PAIR))
            pe.wait_ge(s_x[1], T)
            mm(ps[3][:, 0:2], W("w3"), W("att_src", 0, 2), start=True, stop=True).then_inc(s_att, 1)
            pe.wait_ge(s_attc, 2)
            with pe.If(over > 0):
                for i, (h, c, w) in enumerate(CH):
                    if i >= 2:
                        pe.wait_ge(s_dt, 2 * (i - 1))
                    mm(ps[i % 2][:, 0:w], W("w_sd", D, D), xt[:, c:c + w], start=True, stop=True)
                    mm(ps[2 + i % 2][:, 0:w], W("w_sd", 0, D), xt[:, c:c + w], start=True, stop=True).then_inc(s_dtp, 1)
                for i, (a, b) in enumerate(GROUP[:LASTG]):
                    for t in range(a, b):
                        update(t)
                    if i < LATE:
                        for stage in range(3):
                            attention(i, stage)
            with pe.Else():
                pe.wait_ge(s_bias, len(GROUP))
                for u in range(NHEAD):
                    mm(ps[u][:, 0:D], C("spread_t", u * P, P), sd[:, 0, 0:D], start=True, stop=True).then_inc(s_su, 1)
                pe.wait_ge(s_suc, NHEAD)

                def rows_of_edges(i):
                    t, u, k, n, diag = BAT[i]
                    s_of = pt2[:, u * D:(u + 1) * D] if u < NHEAD else sd[:, t, 0:D]
                    pe.wait_ge(s_hotp, i + 1)
                    if i >= 2:
                        pe.wait_ge(s_zed, i - 1)
                    for j in range(n):
                        last = mm(ps[i % 2][:, j * D:(j + 1) * D], hot(i, 0)[:, j * P:(j + 1) * P], s_of,
                                  start=True, stop=True)
                    last.then_inc(s_sep, 1)

                rows_of_edges(0)
                for i in range(len(BAT) + TAIL):
                    if i < len(BAT):
                        t, u, k, n, diag = BAT[i]
                        if i + 1 < len(BAT):
                            rows_of_edges(i + 1)
                        if diag and t >= 2:
                            pe.wait_ge(s_agg, t - 1)
                        pe.wait_ge(s_gel, i + 1)
                        pe.wait_ge(s_dia, i + 1)
                        for j in range(n + diag):
                            last = mm(ps[4 + t % 2][:, 0:P], gel(i)[:, j * D:(j + 1) * D], dia(i)[:, j * P:(j + 1) * P],
                                      start=bool(diag and j == 0), stop=(i == LASTB[t] and j == n + diag - 1))
                        last.then_inc(s_bat, 1)
                    for t in range(T):
                        if LASTB[t] + LAG_UP == i and t < GROUP[LASTG][0]:
                            update(t)
                    for g, (a, b) in enumerate(GROUP[:LATE]):
                        if i - LASTB[b - 1] - LAG_ATT in (0, 2, 4):
                            attention(g, (i - LASTB[b - 1] - LAG_ATT) // 2)

            def close(i):
                for j in range(SD_AT[i], SD_AT[i + 1]):
                    a, b = SD_PAIR[j]
                    bank = ps[6 + j % 2]
                    pe.wait_ge(s_zc, i + 1)
                    pe.wait_ge(s_sr, i + 1)
                    if j >= 2:
                        pe.wait_ge(s_q, j - 1)
                    for t in range(a, b):
                        s = slice(t * P, (t + 1) * P)
                        nc.tensor.transpose(bank[:, (t - a) * P:(t - a + 1) * P], pt1[:, s], ident)
                        last = mm(bank[:, 2 * P + t - a:2 * P + t - a + 1], xt[0:1, s], C("ones", 0, 1)[0:1, :],
                                  start=True, stop=True)
                    last.then_inc(s_zp, 1)

            for t in range(*GROUP[LASTG]):
                update(t)
            for n in range(STEPS):
                h, t = half(n)
                if t > 4 and t % 4 == 1:
                    q = QUADS * h + t // 4 - 1
                    pe.wait_ge(s_tsum, 3 * (q + 1))
                    if n == T + 5:
                        pe.wait_ge(s_sr, NB)
                    for b, (c, w) in enumerate(chunks(h)):
                        last = mm(ps[NB + b][:, 0:w], C("ones"), quad(q, HWID[h])[:, c:c + w], start=(t == 5), stop=False)
                    last.then_inc(s_qsum, 1)
                if n == T:
                    pe.wait_ge(s_zc, NB)
                pe.wait_ge(s_t2, n + 1)
                if n < T:
                    pe.wait_ge(s_attc, max(attc_of(t), 2 + 3 * LATE))
                for b, (c, w) in enumerate(chunks(h)):
                    last = mm(ps[b][:, 0:w], hn[:, t, :], place_2(n, HWID[h])[:, c:c + w],
                              start=(t == 0), stop=(t == T - 1))
                if t >= SINGLE:
                    for b, (c, w) in enumerate(chunks(h)):
                        last = mm(ps[NB + b][:, 0:w], C("ones"), cols[:, place_1(n), c:c + w], start=False, stop=(t == T - 1))
                last.then_inc(s_pe3, 1)
                if n in ATT_PE:
                    attention(*ATT_PE[n])
                if h and t in CLOSE_PE:
                    close(CLOSE_PE.index(t))
            for i in range(NB, 2 * NB):
                close(i)


_INS = ("x", "adj_rows", "adj_cols", "head", "weights", "rows4", "consts")


def kernel(**inputs):
    import concourse.bacc as bacc
    from concourse.bass_utils import run_bass_kernel_spmd as run

    a = {k: np.ascontiguousarray(v) for k, v in inputs.items()}
    adj = a["adj"]
    lay = {}
    xp = np.zeros((NP, D), adj.dtype)
    xp[:N] = a["x"]
    lay["x"] = np.ascontiguousarray(xp.reshape(T, P, D).transpose(1, 0, 2))
    for name, m in (("adj_rows", adj), ("adj_cols", adj.T)):
        lay[name] = np.zeros((NP, N), adj.dtype)
        lay[name][:N] = m
    head = np.zeros((P, HEAD_AT[NHEAD]), adj.dtype)
    for u, (row, nrows, parts) in enumerate(HEAD):
        for part in range(parts):
            m = adj[row:row + nrows, part::parts]
            head[part::parts, HEAD_AT[u]:HEAD_AT[u] + m.shape[1]] = m
    lay["head"] = head
    diag = np.zeros(NP, adj.dtype)
    diag[:N] = adj[np.arange(N), np.arange(N)]
    mw, uw = a["L2_gnn_msg_w"], a["L2_gnn_upd_w"]
    w = {
        "w_in": a["L0_gnn_W_in"], "w_out": a["L0_gnn_W_out"],
        "w_msg_t": a["L1_gnn_W_msg"].T, "w_ih_t": a["L1_gnn_W_ih"].T, "w_hh_t": a["L1_gnn_W_hh"].T,
        "w_sd": np.concatenate([mw[:, :D].T, mw[:, D:].T], axis=1), "upd_x": uw[:, :D].T, "upd_a": uw[:, D:].T,
        "w3_t": a["L3_gnn_weight"].T, "w3": a["L3_gnn_weight"],
        "b_msg": a["L1_gnn_b_msg"].reshape(D, 1),
        "b_ih": a["L1_gnn_b_ih"].reshape(3, D).T, "b_hh": a["L1_gnn_b_hh"].reshape(3, D).T,
        "msg_b": a["L2_gnn_msg_b"].reshape(D, 1),
        "att_src": a["L3_gnn_att_src"].reshape(D, 1), "att_dst": a["L3_gnn_att_dst"].reshape(D, 1),
        "diag": diag.reshape(T, P).T,
    }
    lay["weights"] = np.concatenate([w[k] for k in WEIGHT], axis=1)
    lay["rows4"] = np.stack([a["L2_gnn_msg_b"], a["L2_gnn_upd_b"], a["L2_gnn_ln_w"], a["L2_gnn_ln_b"]])[None]
    lay["consts"] = constants()

    nc = bacc.Bacc("TRN2", target_bir_lowering=False, num_devices=1)
    arrays = {f"in_{k}_dram": np.ascontiguousarray(lay[k]) for k in _INS}
    args = [nc.dram_tensor(k, v.shape, mybir.dt.from_np(v.dtype), kind="ExternalInput").ap() for k, v in arrays.items()]
    out = nc.dram_tensor("out_0_dram", (N, D), mybir.dt.float32, kind="ExternalOutput").ap()
    build(nc, *args, out)
    r = run(nc, [arrays], core_ids=[0])
    return r.results[0]["out_0_dram"]
```
